# Optimizing a Trainium2 kernel written in Bass

```python
import numpy as np
import jax
import jax.numpy as jnp

def _softmax(x, axis=-1):
    return jax.nn.softmax(x, axis=axis)
def _gelu(x):
    return jax.nn.gelu(x, approximate=True)
def _silu(x):
    return jax.nn.silu(x)
def _sigmoid(x):
    return jax.nn.sigmoid(x)
def _layernorm(x, axis=-1, eps=1e-5):
    m = jnp.mean(x, axis=axis, keepdims=True)
    v = jnp.var(x, axis=axis, keepdims=True)
    return (x - m) / jnp.sqrt(v + eps)
def _scatter_add(tgt, idx, src, axis=0):
    return tgt.at[idx].add(src)
def _segment_sum(src, seg, n):
    return jax.ops.segment_sum(src, seg, n)

kernel_name = 'mk_conv_seq_d2_conv_nchw512_2d7994'

def setup_inputs(seed: int = 0):
    np.random.seed(seed)
    _w = jnp.asarray
    def _rec_inputs():
        import jax
        import jax.numpy as jnp
        _gk = jax.random.key(seed)
        x = -0.0002928 + 1 * jax.random.normal(jax.random.fold_in(_gk, 1), (8, 512, 32, 32), jnp.float32)
        return x
    x = _rec_inputs()
    def _L0_conv_setup():
        import jax, jax.numpy as jnp
        import numpy as np
        N_HEAD = 8
        GROUPS = 32
        EPS = 1e-05

        def _group_norm(x, w, b):
            B, C, H, W = x.shape
            xg = x.reshape(B, GROUPS, C // GROUPS, H, W)
            mu = xg.mean(axis=(2, 3, 4), keepdims=True)
            var = xg.var(axis=(2, 3, 4), keepdims=True)
            xn = ((xg - mu) * jax.lax.rsqrt(var + EPS)).reshape(B, C, H, W)
            return xn * w[None, :, None, None] + b[None, :, None, None]
        key = jax.random.key(seed)
        k0, k1, k2, k3 = jax.random.split(key, 4)
        B, C, H, W = (8, 512, 32, 32)
        x = jax.random.normal(k0, (B, C, H, W), dtype=jnp.float32)
        gn_w = jnp.ones((C,), dtype=jnp.float32)
        gn_b = jnp.zeros((C,), dtype=jnp.float32)
        qkv_w = jax.random.normal(k1, (3 * C, C), dtype=jnp.float32) * 0.02
        out_w = jax.random.normal(k2, (C, C), dtype=jnp.float32) * 0.02
        out_b = jnp.zeros((C,), dtype=jnp.float32)
        return {'x': x, 'gn_w': gn_w, 'gn_b': gn_b, 'qkv_w': qkv_w, 'out_w': out_w, 'out_b': out_b}
    _L0_conv_all = _L0_conv_setup()
    _L0_conv_in = {k: v for k, v in _L0_conv_all.items() if k in ('gn_w', 'gn_b', 'qkv_w', 'out_w', 'out_b', )}
    del _L0_conv_all

    def _L1_conv_setup():
        import jax, jax.numpy as jnp
        import numpy as np
        C = 512
        G = 32
        EPS = 1e-06

        def _group_norm(x, scale, bias):
            b, c, h, w = x.shape
            xg = x.reshape(b, G, c // G, h, w)
            mean = jnp.mean(xg, axis=(2, 3, 4), keepdims=True)
            var = jnp.var(xg, axis=(2, 3, 4), keepdims=True)
            xg = (xg - mean) * jax.lax.rsqrt(var + EPS)
            x = xg.reshape(b, c, h, w)
            return x * scale[None, :, None, None] + bias[None, :, None, None]

        def _conv1x1(x, w, bias):
            return jnp.einsum('oc,bchw->bohw', w, x) + bias[None, :, None, None]
        key = jax.random.key(seed)
        ks = jax.random.split(key, 12)
        x = jax.random.normal(ks[0], (2, C, 64, 64), dtype=jnp.float32)
        s = 1.0 / np.sqrt(C)
        params = {'gn_scale': jnp.ones((C,), jnp.float32), 'gn_bias': jnp.zeros((C,), jnp.float32), 'wq': jax.random.normal(ks[1], (C, C), jnp.float32) * s, 'bq': jax.random.normal(ks[2], (C,), jnp.float32) * 0.01, 'wk': jax.random.normal(ks[3], (C, C), jnp.float32) * s, 'bk': jax.random.normal(ks[4], (C,), jnp.float32) * 0.01, 'wv': jax.random.normal(ks[5], (C, C), jnp.float32) * s, 'bv': jax.random.normal(ks[6], (C,), jnp.float32) * 0.01, 'wp': jax.random.normal(ks[7], (C, C), jnp.float32) * s, 'bp': jax.random.normal(ks[8], (C,), jnp.float32) * 0.01}
        return {'x': x, **params}
    _L1_conv_all = _L1_conv_setup()
    _L1_conv_in = {k: v for k, v in _L1_conv_all.items() if k in ('gn_scale', 'gn_bias', 'wq', 'bq', 'wk', 'bk', 'wv', 'bv', 'wp', 'bp', )}
    del _L1_conv_all

    return {
        "x": x,
        "L0_conv_gn_w": _L0_conv_in["gn_w"],
        "L0_conv_gn_b": _L0_conv_in["gn_b"],
        "L0_conv_qkv_w": _L0_conv_in["qkv_w"],
        "L0_conv_out_w": _L0_conv_in["out_w"],
        "L0_conv_out_b": _L0_conv_in["out_b"],
        "L1_conv_gn_scale": _L1_conv_in["gn_scale"],
        "L1_conv_gn_bias": _L1_conv_in["gn_bias"],
        "L1_conv_wq": _L1_conv_in["wq"],
        "L1_conv_bq": _L1_conv_in["bq"],
        "L1_conv_wk": _L1_conv_in["wk"],
        "L1_conv_bk": _L1_conv_in["bk"],
        "L1_conv_wv": _L1_conv_in["wv"],
        "L1_conv_bv": _L1_conv_in["bv"],
        "L1_conv_wp": _L1_conv_in["wp"],
        "L1_conv_bp": _L1_conv_in["bp"],
    }

def reference(x, L0_conv_gn_w, L0_conv_gn_b, L0_conv_qkv_w, L0_conv_out_w, L0_conv_out_b, L1_conv_gn_scale, L1_conv_gn_bias, L1_conv_wq, L1_conv_bq, L1_conv_wk, L1_conv_bk, L1_conv_wv, L1_conv_bv, L1_conv_wp, L1_conv_bp):
    import jax
    import jax.numpy as jnp
    def _L0_conv_ref(x, gn_w, gn_b, qkv_w, out_w, out_b):
        import jax, jax.numpy as jnp
        import numpy as np
        N_HEAD = 8
        GROUPS = 32
        EPS = 1e-05

        def _group_norm(x, w, b):
            B, C, H, W = x.shape
            xg = x.reshape(B, GROUPS, C // GROUPS, H, W)
            mu = xg.mean(axis=(2, 3, 4), keepdims=True)
            var = xg.var(axis=(2, 3, 4), keepdims=True)
            xn = ((xg - mu) * jax.lax.rsqrt(var + EPS)).reshape(B, C, H, W)
            return xn * w[None, :, None, None] + b[None, :, None, None]
        B, C, H, W = x.shape
        hd = C // N_HEAD
        n = _group_norm(x, gn_w, gn_b)
        qkv = jnp.einsum('dc,bchw->bdhw', qkv_w, n).reshape(B, N_HEAD, 3 * hd, H, W)
        q, k, v = jnp.split(qkv, 3, axis=2)
        scale = 1.0 / jnp.sqrt(jnp.float32(C))
        attn = jnp.einsum('bnchw,bncyx->bnhwyx', q, k) * scale
        attn = jax.nn.softmax(attn.reshape(B, N_HEAD, H, W, H * W), axis=-1)
        attn = attn.reshape(B, N_HEAD, H, W, H, W)
        o = jnp.einsum('bnhwyx,bncyx->bnchw', attn, v).reshape(B, C, H, W)
        o = jnp.einsum('dc,bchw->bdhw', out_w, o) + out_b[None, :, None, None]
        return o + x

    def _L1_conv_ref(x, gn_scale, gn_bias, wq, bq, wk, bk, wv, bv, wp, bp):
        import jax, jax.numpy as jnp
        import numpy as np
        C = 512
        G = 32
        EPS = 1e-06

        def _group_norm(x, scale, bias):
            b, c, h, w = x.shape
            xg = x.reshape(b, G, c // G, h, w)
            mean = jnp.mean(xg, axis=(2, 3, 4), keepdims=True)
            var = jnp.var(xg, axis=(2, 3, 4), keepdims=True)
            xg = (xg - mean) * jax.lax.rsqrt(var + EPS)
            x = xg.reshape(b, c, h, w)
            return x * scale[None, :, None, None] + bias[None, :, None, None]

        def _conv1x1(x, w, bias):
            return jnp.einsum('oc,bchw->bohw', w, x) + bias[None, :, None, None]
        h = _group_norm(x, gn_scale, gn_bias)
        q = _conv1x1(h, wq, bq)
        k = _conv1x1(h, wk, bk)
        v = _conv1x1(h, wv, bv)
        b, c, h_, w_ = q.shape
        n = h_ * w_
        q = q.reshape(b, c, n)
        k = k.reshape(b, c, n)
        v = v.reshape(b, c, n)
        attn = jnp.einsum('bci,bcj->bij', q, k) * c ** (-0.5)
        attn = jax.nn.softmax(attn, axis=2)
        out = jnp.einsum('bcj,bij->bci', v, attn)
        out = out.reshape(b, c, h_, w_)
        out = _conv1x1(out, wp, bp)
        return x + out

    def _gn(v, G=32, eps=1e-5):
        B_, C_, H_, W_ = v.shape
        g = v.reshape(B_, G, C_ // G, H_, W_)
        m = jnp.mean(g, axis=(2, 3, 4), keepdims=True)
        s = jnp.var(g, axis=(2, 3, 4), keepdims=True)
        return ((g - m) / jnp.sqrt(s + eps)).reshape(v.shape)

    def _ln_c(v, eps=1e-6):
        m = jnp.mean(v, axis=1, keepdims=True)
        s = jnp.var(v, axis=1, keepdims=True)
        return (v - m) / jnp.sqrt(s + eps)

    def _ln_t(v, eps=1e-5):
        m = jnp.mean(v, axis=-1, keepdims=True)
        s = jnp.var(v, axis=-1, keepdims=True)
        return (v - m) / jnp.sqrt(s + eps)

    def _to_tokens(v):
        B_, C_, H_, W_ = v.shape
        return v.reshape(B_, C_, H_ * W_).transpose(0, 2, 1)
    def _from_tokens(t, like):
        B_, C_, H_, W_ = like.shape
        return t.transpose(0, 2, 1).reshape(B_, C_, H_, W_)

    x = _L0_conv_ref(x, L0_conv_gn_w, L0_conv_gn_b, L0_conv_qkv_w, L0_conv_out_w, L0_conv_out_b)
    x = _L1_conv_ref(x, L1_conv_gn_scale, L1_conv_gn_bias, L1_conv_wq, L1_conv_bq, L1_conv_wk, L1_conv_bk, L1_conv_wv, L1_conv_bv, L1_conv_wp, L1_conv_bp)
    return x


_drawn_inputs = setup_inputs


def setup_inputs(seed=0):
    import zlib

    import numpy as np

    out = dict(_drawn_inputs(seed))
    spreads = {'L0_conv_gn_w': (1.0, 0.6),
     'L0_conv_gn_b': (0.0, 0.281),
     'L0_conv_out_b': (0.0, 0.1),
     'L1_conv_gn_scale': (1.0, 0.2),
     'L1_conv_gn_bias': (0.0, 0.1)}
    factors = {'L1_conv_bq': 64.0, 'L1_conv_bk': 64.0, 'L1_conv_bv': 5.612, 'L1_conv_bp': 6.033}
    for name, (base, spread) in spreads.items():
        noise = np.random.default_rng([zlib.crc32(name.encode()), seed]).standard_normal(out[name].shape)
        drawn = base * np.exp(spread * noise) if base else spread * noise
        out[name] = jnp.asarray(drawn.astype(out[name].dtype))
    for name, factor in factors.items():
        out[name] = (out[name] * factor).astype(out[name].dtype)
    return out
```

```python
from contextlib import ExitStack

import concourse.bass as bass
from concourse import mybir

ALU = mybir.AluOpType
ACT = mybir.ActivationFunctionType
F32 = mybir.dt.float32
F32R = mybir.dt.float32r
AX_X = mybir.AxisListType.X

P = 128
B, C, N = 8, 512, 1024
KT = C // P
JT = N // P
HEADS, HD = 8, 64
PAIRS = HEADS // 2
QU = 256
TILES = QU // P
UNITS = N // QU
HALF = 512
TURNS = JT // 2
PROBS = 4
SCALE = float(C) ** -0.5
EPS0, EPS1 = 1e-5, 1e-6
GROUPS = 32

V_GNW, V_GNB, V_OB, V_GS, V_GB, V_BQ, V_BK, V_BV, V_BP = range(9)
W_QK, W_V, W_O, W_Q1, W_K1, W_P1, W_V1 = 0, 8, 12, 16, 20, 24, 28
S_QK, S_V, S_O, S_Q1, S_K1, S_M1 = 0, 8, 12, 16, 20, 24
CHUNKS = 28


def f(ap):
    return ap.bitcast(F32)


def wait(eng, sem, value):
    if isinstance(value, int) and value <= 0:
        return
    eng.wait_ge(sem, value)


def wait_apart(eng, sem, value, passed):
    eng.wait_ge(sem, value)
    eng.sem_inc(passed, 1)


class Slots:

    def __init__(self, items, act_kinds, dve_kinds, before, whole=None):
        self.items, self.before = items, before
        self.act_kinds, self.dve_kinds = act_kinds, dve_kinds
        self.pos = {it: n for n, it in enumerate(items)}
        self.act, self.dve = [0], [0]
        for it in items:
            self.act.append(self.act[-1] + (it[0] in act_kinds))
            self.dve.append(self.dve[-1] + (it[0] in dve_kinds))
        w = whole or self
        self.per_full, self.per_act, self.per_dve = len(w.items), w.act[-1], w.dve[-1]

    def slot(self, it):
        return self.pos[it] % 2

    def full(self, b, it):
        return b * self.per_full + (self.before + self.pos[it] + 1)

    def act_done(self, b, it):
        return b * self.per_act + self.act[self.pos[it] + 1]

    def dve_done(self, b, it):
        return b * self.per_dve + (self.before + self.dve[self.pos[it] + 1])

    def wait_free(self, eng, act_released, dve_released, b, it):
        n = self.pos[it] - 2
        kind = self.items[n][0]
        if n < 0 and isinstance(b, int) and b == 0:
            wait(eng, dve_released, self.before + n + 1)
            return
        act = self.act[n + 1] if n >= 0 else self.act[len(self.items) + n + 1] - self.act[-1]
        dve = self.dve[n + 1] if n >= 0 else self.dve[len(self.items) + n + 1] - self.dve[-1]
        if kind in self.act_kinds:
            wait(eng, act_released, b * self.per_act + act)
        if kind in self.dve_kinds:
            wait(eng, dve_released, b * self.per_dve + (self.before + dve))


def over_batches(eng, body):
    body(0, False)
    with eng.Fori(1, B - 1, 1) as b:
        body(b, False)
    body(B - 1, True)


def split_weights(nc, w_in, scratch, vecs, b2):
    with ExitStack() as ctx:
        def sb(name, shape, dt=F32):
            return ctx.enter_context(nc.sbuf_tensor(name, shape, dt))

        def sem(name):
            return ctx.enter_context(nc.semaphore(name))

        raw = sb("w_raw", [P, 2, 4, HALF])
        wv = sb("w_v1", [P, KT, C])
        wp = sb("w_p1", [P, KT, C])
        both = sb("w_split", [P, 2, 4, 2, HALF], F32R)
        prod = ctx.enter_context(nc.psum_tensor("w_prod", [P, KT, HALF], F32))
        bias = ctx.enter_context(nc.psum_tensor("w_bias", [P, HALF], F32))
        loaded = [sem("w_loaded0"), sem("w_loaded1")]
        stored = [sem("w_stored0"), sem("w_stored1")]
        pair_in, hi_done, lo_done = sem("w_pair_in"), sem("w_hi"), sem("w_lo")
        prod_done, bias_done, b2_done = sem("w_prod_done"), sem("w_bias_done"), sem("w_b2")
        groups = CHUNKS // 4
        block = ctx.enter_context(nc.Block())

        def source(g):
            return raw[:, g % 2] if g < groups - 1 else prod[:, :, :]

        @block.sync
        def _(sp):
            for g in range(groups):
                if g < groups - 1:
                    if g >= 2:
                        sp.wait_ge(lo_done, g - 1)
                    sp.dma_start(raw[:, g % 2], w_in[:, 4 * g:4 * g + 4, :]).then_inc(loaded[g % 2], 16)
                if g == 1:
                    sp.dma_start(wv[:], w_in[:, W_V1:W_V1 + KT, :]).then_inc(pair_in, 16)
                    sp.dma_start(wp[:], w_in[:, W_P1:W_P1 + KT, :]).then_inc(pair_in, 16)
                if g >= 1:
                    sp.wait_ge(lo_done, g)
                    sp.dma_start(scratch[:, 4 * g - 4:4 * g], f(both[:, (g - 1) % 2])).then_inc(stored[(g - 1) % 2], 16)
            sp.wait_ge(lo_done, groups)
            sp.dma_start(scratch[:, CHUNKS - 4:CHUNKS], f(both[:, (groups - 1) % 2])).then_inc(stored[(groups - 1) % 2], 16)
            sp.wait_ge(stored[0], 16 * ((groups + 1) // 2))
            sp.wait_ge(stored[1], 16 * (groups // 2))

        @block.scalar
        def _(act):
            for g in range(groups):
                if g < groups - 1:
                    act.wait_ge(loaded[g % 2], 16 * (g // 2 + 1))
                else:
                    act.wait_ge(prod_done, 1)
                if g >= 2:
                    act.wait_ge(stored[g % 2], 16 * (g // 2))
                nc.scalar.activation(both[:, g % 2, :, 0, :], source(g), ACT.Copy).then_inc(hi_done, 1)

        @block.vector
        def _(dve):
            for g in range(groups):
                dve.wait_ge(hi_done, g + 1)
                nc.vector.tensor_tensor(both[:, g % 2, :, 1, :], source(g), f(both[:, g % 2, :, 0, :]),
                                        ALU.subtract).then_inc(lo_done, 1)
            dve.wait_ge(bias_done, 1)
            nc.vector.tensor_tensor(b2[:], bias[:, 0:KT], vecs[:, V_BP, :], ALU.add).then_inc(b2_done, 1)
            dve.wait_ge(b2_done, 1)

        @block.tensor
        def _(pe):
            pe.wait_ge(pair_in, 32)
            for ct in range(KT):
                for mt in range(KT):
                    last = nc.tensor.matmul(prod[:, ct, :], wv[:, mt, ct * P:(ct + 1) * P], wp[:, mt, :],
                                            start=(mt == 0), stop=(mt == KT - 1))
            last.then_inc(prod_done, 1)
            for ot in range(KT):
                for mt in range(KT):
                    last = nc.tensor.matmul(bias[:, ot:ot + 1], wp[:, mt, ot * P:(ot + 1) * P],
                                            vecs[:, V_BV, mt:mt + 1], start=(mt == 0), stop=(mt == KT - 1))
            last.then_inc(bias_done, 1)


class Norm:

    CHAIN = 6

    def __init__(self, nc, tag, sb, sem, eps, weight, shift, averager, minus_half):
        self.nc, self.eps, self.weight, self.shift = nc, eps, weight, shift
        self.averager, self.minus_half = averager, minus_half
        self.stats = sb(f"{tag}_stats", [P, KT, 2, 6])
        self.mv = sb(f"{tag}_mean_var", [P, KT, 2])
        self.gmean = sb(f"{tag}_group_mean", [P, KT])
        self.dev = sb(f"{tag}_deviation", [P, KT])
        self.var = sb(f"{tag}_var", [P, KT])
        self.vareps = sb(f"{tag}_var_eps", [P, KT])
        self.rstd = sb(f"{tag}_rstd", [P, KT])
        self.a = sb(f"{tag}_a", [P, KT])
        self.ma = sb(f"{tag}_mean_a", [P, KT])
        self.b = sb(f"{tag}_b", [P, KT])
        self.halves = sem(f"{tag}_halves")
        self.passed = sem(f"{tag}_passed")
        self.tiles = sem(f"{tag}_tiles")
        self.chain = sem(f"{tag}_chain")
        self.rstd_ready = sem(f"{tag}_rstd_ready")
        self.hi_done = sem(f"{tag}_hi_done")
        self.mid_done = sem(f"{tag}_mid_done")
        self.lo_done = sem(f"{tag}_lo_done")

    def tile_stats(self, dve, n, ct, x):
        v = self.nc.vector
        for k in range(2):
            v.bn_stats(self.stats[:, ct, k, :], x[:, k * HALF:(k + 1) * HALF]).then_inc(self.halves, 1)
        wait_apart(dve, self.halves, n * (2 * KT) + (2 * ct + 2), self.passed)
        v.bn_aggr(self.mv[:, ct, :], self.stats[:, ct].rearrange("p a b -> p (a b)")).then_inc(self.tiles, 1)

    def mean_matmul(self, pe, n, out):
        pe.wait_ge(self.tiles, n * KT + KT)
        return self.nc.tensor.matmul(out, self.averager, self.mv[:, :, 0], start=True, stop=True)

    def after_means(self, dve, n, psum, released, released_count):
        v = self.nc.vector
        v.tensor_copy(self.gmean[:], psum).then_inc(released, 1)
        dve.wait_ge(released, released_count)
        dve.wait_ge(self.tiles, n * KT + KT)
        v.tensor_tensor(self.dev[:], self.mv[:, :, 0], self.gmean[:], ALU.subtract).then_inc(self.chain, 1)
        dve.wait_ge(self.chain, n * self.CHAIN + 1)
        v.tensor_tensor(self.var[:], self.dev[:], self.dev[:], ALU.mult).then_inc(self.chain, 1)
        dve.wait_ge(self.chain, n * self.CHAIN + 2)
        v.tensor_tensor(self.var[:], self.var[:], self.mv[:, :, 1], ALU.add).then_inc(self.chain, 1)

    def var_matmul(self, pe, n, out):
        pe.wait_ge(self.chain, n * self.CHAIN + 3)
        return self.nc.tensor.matmul(out, self.averager, self.var[:], start=True, stop=True)

    def after_vars(self, psum, released):
        self.nc.vector.tensor_scalar(self.vareps[:], psum, self.eps, None, ALU.add).then_inc(released, 1)

    def power(self, pool, released, released_count):
        pool.wait_ge(released, released_count)
        self.nc.gpsimd.tensor_tensor(self.rstd[:], self.vareps[:], self.minus_half, ALU.pow
                                     ).then_inc(self.rstd_ready, 1)

    def coefficients(self, dve, n):
        v = self.nc.vector
        dve.wait_ge(self.rstd_ready, n + 1)
        v.tensor_tensor(self.a[:], self.rstd[:], self.weight, ALU.mult).then_inc(self.chain, 1)
        dve.wait_ge(self.chain, n * self.CHAIN + 4)
        v.tensor_tensor(self.ma[:], self.gmean[:], self.a[:], ALU.mult).then_inc(self.chain, 1)
        dve.wait_ge(self.chain, n * self.CHAIN + 5)
        v.tensor_tensor(self.b[:], self.shift, self.ma[:], ALU.subtract).then_inc(self.chain, 1)

    def tile_hi(self, act, n, ct, x, out):
        act.wait_ge(self.chain, n * self.CHAIN + 6)
        self.nc.scalar.activation(out, x, ACT.Identity, bias=self.b[:, ct:ct + 1],
                                  scale=self.a[:, ct:ct + 1]).then_inc(self.hi_done, 1)

    def tile_mid(self, dve, n, ct, x):
        dve.wait_ge(self.chain, n * self.CHAIN + 6)
        dve.wait_ge(self.hi_done, n * KT + (ct + 1))
        self.nc.vector.tensor_scalar(x, x, self.a[:, ct:ct + 1], self.b[:, ct:ct + 1], ALU.mult, ALU.add
                                     ).then_inc(self.mid_done, 1)

    def tile_lo(self, pool, n, ct, x, hi, out):
        pool.wait_ge(self.mid_done, n * KT + (ct + 1))
        self.nc.gpsimd.tensor_tensor(out, x, f(hi), ALU.subtract).then_inc(self.lo_done, 1)


def three(nc, out, w_hi, w_lo, m_hi, m_lo, first, last):
    nc.tensor.matmul(out, w_hi, m_hi, start=first, stop=False)
    nc.tensor.matmul(out, w_hi, m_lo, start=False, stop=False)
    return nc.tensor.matmul(out, w_lo, m_hi, start=False, stop=last)


def attend_heads(nc, x, x1, scratch, vecs, tables):
    with ExitStack() as ctx:
        def sb(name, shape, dt=F32):
            return ctx.enter_context(nc.sbuf_tensor(name, shape, dt))

        def sem(name):
            return ctx.enter_context(nc.semaphore(name))

        ident = tables[:, 0:P]
        norm = Norm(nc, "gn0", sb, sem, EPS0, vecs[:, V_GNW, :], vecs[:, V_GNB, :], tables[:, P:2 * P],
                    tables[:, 2 * P:2 * P + KT])
        w_qk = sb("w_qk", [P, 2, 2, KT, P], F32R)
        w_vo = sb("w_vo", [P, 4, 2, HALF], F32R)
        n_hi = sb("n_hi", [P, KT, N], F32R)
        n_lo = sb("n_lo", [P, KT, N], F32R)
        vt = sb("vt", [P, JT, HEADS, P], F32R)
        q_st = sb("q_st", [P, 2, N], F32R)
        k_hi = sb("k_hi", [P, 2, N], F32R)
        k_lo = sb("k_lo", [P, 2, N], F32R)
        probs = sb("probs", [P, PROBS, N])
        pt_hi = sb("pt_hi", [P, 2, JT, QU], F32R)
        pt_lo = sb("pt_lo", [P, 2, JT, QU], F32R)
        side = sb("side", [P, 2, QU])
        o_mid = sb("o_mid", [P, N])
        o_hi = sb("o_hi", [P, PAIRS, N], F32R)
        o_lo = sb("o_lo", [P, PAIRS, N], F32R)
        x_in = sb("x_in", [P, 2, N])
        neg_max = sb("neg_max", [P, PROBS])
        total = sb("total", [P, PROBS])
        inverse = sb("inverse", [P, PROBS])
        slot = ctx.enter_context(nc.psum_tensor("slot", [P, 2, 2 * HALF], F32))
        turn = ctx.enter_context(nc.psum_tensor("turn", [P, 2, 2, QU], F32))
        mix = ctx.enter_context(nc.psum_tensor("mix", [P, 2, HALF], F32))

        x_loaded = [sem("x_loaded0"), sem("x_loaded1")]
        qk_loaded = [sem("wqk_loaded0"), sem("wqk_loaded1")]
        v_loaded = [sem(f"wv_loaded{i}") for i in range(4)]
        o_loaded = [sem(f"wo_loaded{i}") for i in range(4)]
        y_stored = [sem(f"y_stored{i}") for i in range(KT)]
        scale_passed = sem("scale_passed")
        zeroed = sem("zeroed")
        slot_full = sem("slot_full")
        act_released = sem("act_released")
        dve_released = sem("dve_released")
        max_ready = sem("max_ready")
        inverse_ready = sem("inverse_ready")
        probs_ready = sem("probs_ready")
        turn_full = sem("turn_full")
        turn_hi = sem("turn_hi")
        turn_lo = sem("turn_lo")
        mix_full = sem("mix_full")
        side_ready = sem("side_ready")
        mix_added = sem("mix_added")
        pair_hi = sem("pair_hi")
        pair_lo = sem("pair_lo")
        U = HEADS * UNITS
        STATS_AT, MEANS_AT, VARS_AT, COEF_AT, NORM_AT = 1, 6, 8, 9, 27

        def order(last):
            items = [("V", i) for i in range(JT // 2)] + [("QK", 0)]
            for s in range(U):
                items += [("S", s, 0), ("S", s, 1)]
                if s % UNITS == 1 and s // UNITS + 1 < HEADS:
                    items.append(("QK", s // UNITS + 1))
                if not last and s in (MEANS_AT, VARS_AT):
                    items.append(("GN", s))
            return items + [("OUT", m) for m in range(KT)]

        ring = Slots(order(False), ("V", "QK", "S"), ("V", "QK", "GN", "OUT"), 2)
        ring_last = Slots(order(True), ring.act_kinds, ring.dve_kinds, 2, ring)

        def x_count(b, k):
            return b * (8 * 3 * KT) + 16 * (KT + k // 2 + 1)

        def residual_load(last, m):
            return m if last else 2 * KT + m

        block = ctx.enter_context(nc.Block())

        @block.sync
        def _(sp):
            def load_x(b, i):
                sp.dma_start(x_in[:, i % 2], x[b, i * P:(i + 1) * P, :]).then_inc(x_loaded[i % 2], 16)

            def load_qk(h):
                sp.dma_start(f(w_qk[:, h % 2].rearrange("p a k m -> p (a k m)")),
                             scratch[:, S_QK + h].rearrange("p a n -> p (a n)")).then_inc(qk_loaded[h % 2], 16)

            def load_vo(c, chunk, loaded):
                sp.dma_start(f(w_vo[:, c]), scratch[:, chunk + c]).then_inc(loaded[c], 16)

            for i in range(KT):
                if i >= 2:
                    sp.wait_ge(norm.tiles, i - 1)
                load_x(0, i)
            for i in range(KT):
                if i < 2:
                    sp.wait_ge(norm.tiles, KT - 1 + i)
                else:
                    sp.wait_ge(norm.lo_done, i - 1)
                load_x(0, i)
            for c in range(4):
                load_vo(c, S_V, v_loaded)
            load_qk(0)

            def body(b, last):
                r = ring_last if last else ring

                def store(m):
                    sp.wait_ge(dve_released, r.dve_done(b, ("OUT", m)))
                    sp.dma_start(x1[b, m * P:(m + 1) * P, :], probs[:, m, :]).then_inc(y_stored[m], 16)

                def next_v(c):
                    if not last:
                        sp.wait_ge(slot_full, r.full(b, ("OUT", c)))
                        load_vo(c, S_V, v_loaded)

                sp.wait_ge(slot_full, r.full(b, ("V", JT // 2 - 1)))
                load_qk(1)
                for c in range(4):
                    load_vo(c, S_O, o_loaded)
                sp.wait_ge(slot_full, r.full(b, ("QK", 0)))
                load_qk(2)
                if not last:
                    for i in range(KT):
                        if i >= 2:
                            sp.wait_ge(norm.tiles, b * KT + (KT + i - 1))
                        elif isinstance(b, int):
                            sp.wait_ge(norm.lo_done, KT - 1 + i)
                        else:
                            sp.wait_ge(dve_released, b * ring.per_dve + (ring.dve_done(0, ("OUT", i + 2)) - ring.per_dve))
                        load_x(b + 1, i)
                    for i in range(2):
                        sp.wait_ge(norm.tiles, b * KT + (2 * KT - 1 + i))
                        load_x(b + 1, i)
                for h in range(3, HEADS):
                    sp.wait_ge(slot_full, r.full(b, ("QK", h - 2)))
                    load_qk(h)
                if not last:
                    sp.wait_ge(slot_full, r.full(b, ("QK", HEADS - 2)))
                    load_qk(0)
                    for i in range(2, KT):
                        sp.wait_ge(norm.lo_done, b * KT + (KT + i - 1))
                        load_x(b + 1, i)
                for m in range(KT):
                    if m >= 2 or last:
                        sp.wait_ge(dve_released, r.dve_done(b, ("OUT", m - 2)) if m >= 2 else
                                   b * ring.per_dve + (ring.dve_done(0, ("OUT", m + 2)) - ring.per_dve))
                    else:
                        sp.wait_ge(norm.lo_done, b * KT + (2 * KT - 1 + m))
                    load_x(b, m)
                    if m >= 2:
                        next_v(m - 2)
                        store(m - 2)
                for m in (2, 3):
                    next_v(m)
                    store(m)

            over_batches(sp, body)
            for m in range(KT):
                sp.wait_ge(y_stored[m], 16 * B)

        @block.tensor
        def _(pe):
            norm.mean_matmul(pe, 0, slot[:, 0, 0:KT]).then_inc(slot_full, 1)
            norm.var_matmul(pe, 0, slot[:, 1, 0:KT]).then_inc(slot_full, 1)
            pe.wait_ge(zeroed, 1)

            def body(b, last):
                r = ring_last if last else ring

                def project_v(i):
                    r.wait_free(pe, act_released, dve_released, b, ("V", i))
                    for jj in range(2):
                        j = 2 * i + jj
                        for kt in range(KT):
                            if j == 0:
                                pe.wait_ge(norm.lo_done, b * KT + (kt + 1))
                                pe.wait_ge(v_loaded[kt], b * 16 + 16)
                            mm = three(nc, slot[:, r.slot(("V", i)), jj * HALF:(jj + 1) * HALF],
                                       n_hi[:, kt, j * P:(j + 1) * P], n_lo[:, kt, j * P:(j + 1) * P],
                                       w_vo[:, kt, 0, :], w_vo[:, kt, 1, :], kt == 0, kt == KT - 1)
                    mm.then_inc(slot_full, 1)

                def project_qk(h):
                    r.wait_free(pe, act_released, dve_released, b, ("QK", h))
                    pe.wait_ge(qk_loaded[h % 2], b * (8 * HEADS) + 16 * (h // 2 + 1))
                    for half in range(2):
                        cols = slice(half * HALF, (half + 1) * HALF)
                        for kt in range(KT):
                            mm = three(nc, slot[:, r.slot(("QK", h)), cols], w_qk[:, h % 2, 0, kt], w_qk[:, h % 2, 1, kt],
                                       n_hi[:, kt, cols], n_lo[:, kt, cols], kt == 0, kt == KT - 1)
                    mm.then_inc(slot_full, 1)

                def scores(u, t):
                    h = u // UNITS
                    r.wait_free(pe, act_released, dve_released, b, ("S", u, t))
                    if u % UNITS == 0 and t == 0:
                        pe.wait_ge(act_released, r.act_done(b, ("QK", h)))
                        pe.wait_ge(dve_released, r.dve_done(b, ("QK", h)))
                    at = (u % UNITS) * QU + t * P
                    for half in range(2):
                        cols = slice(half * HALF, (half + 1) * HALF)
                        out = slot[:, r.slot(("S", u, t)), cols]
                        nc.tensor.matmul(out, q_st[:, h % 2, at:at + P], k_hi[:, h % 2, cols], start=True, stop=False)
                        mm = nc.tensor.matmul(out, q_st[:, h % 2, at:at + P], k_lo[:, h % 2, cols],
                                              start=False, stop=True)
                    mm.then_inc(slot_full, 1)

                def turns(u, items):
                    pe.wait_ge(probs_ready, b * (TILES * U) + TILES * (u + 1))
                    for a in items:
                        wait(pe, turn_lo, b * (TURNS * U) + (TURNS * u + a - 1))
                        for jj in range(2):
                            for t in range(TILES):
                                mm = nc.tensor.transpose(turn[:, a % 2, jj, t * P:(t + 1) * P],
                                                         probs[:, (TILES * u + t) % PROBS,
                                                               (2 * a + jj) * P:(2 * a + jj + 1) * P], ident)
                        mm.then_inc(turn_full, 1)

                def mixes(u):
                    pe.wait_ge(turn_lo, b * (TURNS * U) + TURNS * (u + 1))
                    wait(pe, mix_added, b * U + (u - 1))
                    for n, part in enumerate((pt_hi, pt_lo)):
                        for j in range(JT):
                            mm = nc.tensor.matmul(mix[:, u % 2, 0:QU], vt[:, j, u // UNITS, :], part[:, u % 2, j, :],
                                                  start=(n == 0 and j == 0), stop=(n == 1 and j == JT - 1))
                    mm.then_inc(mix_full, 1)

                def project_out(m):
                    r.wait_free(pe, act_released, dve_released, b, ("OUT", m))
                    pe.wait_ge(o_loaded[m], b * 16 + 16)
                    w = w_vo[:, m].rearrange("p a (k m) -> p a k m", k=KT)
                    for half in range(2):
                        cols = slice(half * HALF, (half + 1) * HALF)
                        for kt in range(PAIRS):
                            if m == 0 and half == 0:
                                pe.wait_ge(pair_lo, b * PAIRS + (kt + 1))
                            mm = three(nc, slot[:, r.slot(("OUT", m)), cols], w[:, 0, kt], w[:, 1, kt],
                                       o_hi[:, kt, cols], o_lo[:, kt, cols], kt == 0, kt == PAIRS - 1)
                    mm.then_inc(slot_full, 1)

                def group_stats(s, product):
                    r.wait_free(pe, act_released, dve_released, b, ("GN", s))
                    product(pe, b + 1, slot[:, r.slot(("GN", s)), 0:KT]).then_inc(slot_full, 1)

                for i in range(JT // 2):
                    project_v(i)
                project_qk(0)
                for s in range(U + 2):
                    if s < U:
                        scores(s, 0)
                    if 1 <= s <= U:
                        turns(s - 1, (0, 1))
                    if s < U:
                        scores(s, 1)
                    if 1 <= s <= U:
                        turns(s - 1, (2, 3))
                    if s < U and s % UNITS == 1 and s // UNITS + 1 < HEADS:
                        project_qk(s // UNITS + 1)
                    if not last and s == MEANS_AT:
                        group_stats(s, norm.mean_matmul)
                    if not last and s == VARS_AT:
                        group_stats(s, norm.var_matmul)
                    if s >= 2:
                        mixes(s - 2)
                for m in range(KT):
                    project_out(m)

            over_batches(pe, body)

        @block.scalar
        def _(act):
            for ct in range(KT):
                act.wait_ge(x_loaded[ct % 2], 16 * (2 + ct // 2 + 1))
                norm.tile_hi(act, 0, ct, x_in[:, ct % 2], n_hi[:, ct])

            def body(b, last):
                r = ring_last if last else ring

                def v_hi(i):
                    act.wait_ge(slot_full, r.full(b, ("V", i)))
                    for jj in range(2):
                        src = slot[:, r.slot(("V", i)), jj * HALF:(jj + 1) * HALF].rearrange("p (g e d) -> p g e d", g=PAIRS, e=2)
                        dst = vt[:, 2 * i + jj].rearrange("p (g e) (w d) -> p g (e w) d", e=2, w=2)[:, :, 0:4:3]
                        done = nc.scalar.activation(dst, src, ACT.Copy)
                    done.then_inc(act_released, 1)

                def qk_hi(h):
                    act.wait_ge(slot_full, r.full(b, ("QK", h)))
                    s = slot[:, r.slot(("QK", h)), :]
                    nc.scalar.activation(q_st[0:HD, h % 2, :], s[0:HD], ACT.Copy, scale=SCALE)
                    nc.scalar.activation(k_hi[HD:P, h % 2, :], s[HD:P], ACT.Copy)
                    nc.scalar.activation(k_hi[0:HD, h % 2, :], s[HD:P], ACT.Copy).then_inc(act_released, 1)

                def exponentials(u, t):
                    i = TILES * u + t
                    act.wait_ge(max_ready, b * (TILES * U) + (i + 1))
                    wait(act, turn_full, b * (TURNS * U) + TURNS * (u - 1))
                    if i < PROBS:
                        wait(act, y_stored[i], b * 16)
                    k = i % PROBS
                    nc.scalar.activation(probs[:, k, :], slot[:, r.slot(("S", u, t)), :], ACT.Exp,
                                         bias=neg_max[:, k:k + 1], accum_out=total[:, k:k + 1]).then_inc(act_released, 1)

                def turn_his(u, items):
                    for a in items:
                        act.wait_ge(turn_full, b * (TURNS * U) + (TURNS * u + a + 1))
                        if a == 0:
                            wait(act, mix_full, b * U + (u - 1))
                        nc.scalar.activation(pt_hi[:, u % 2, 2 * a:2 * a + 2, :], turn[:, a % 2], ACT.Copy
                                             ).then_inc(turn_hi, 1)

                def sides(u):
                    odd = (u // UNITS) % 2
                    to, frm = (slice(HD, P), slice(0, HD)) if odd else (slice(0, HD), slice(HD, P))
                    act.wait_ge(mix_full, b * U + (u + 1))
                    wait(act, mix_added, b * U + (u - 1))
                    nc.scalar.activation(side[to, u % 2, :], mix[frm, u % 2, 0:QU], ACT.Copy).then_inc(side_ready, 1)

                def pair_his(u):
                    act.wait_ge(mix_added, b * U + (u + 1))
                    nc.scalar.activation(o_hi[:, u // (2 * UNITS), :], o_mid[:, :], ACT.Copy).then_inc(pair_hi, 1)

                for i in range(JT // 2):
                    v_hi(i)
                qk_hi(0)
                for s in range(U + 4):
                    if 3 <= s < U + 3:
                        sides(s - 3)
                    if s >= 4 and (s - 4) % (2 * UNITS) == 2 * UNITS - 1:
                        pair_his(s - 4)
                    if s < U:
                        exponentials(s, 0)
                    if 1 <= s <= U:
                        turn_his(s - 1, (0, 1))
                    if s < U:
                        exponentials(s, 1)
                    if 1 <= s <= U:
                        turn_his(s - 1, (2, 3))
                    if s < U and s % UNITS == 1 and s // UNITS + 1 < HEADS:
                        qk_hi(s // UNITS + 1)
                    if not last and NORM_AT <= s < NORM_AT + KT:
                        ct = s - NORM_AT
                        act.wait_ge(x_loaded[ct % 2], x_count(b, KT + ct))
                        norm.tile_hi(act, b + 1, ct, x_in[:, ct % 2], n_hi[:, ct])

            over_batches(act, body)

        @block.vector
        def _(dve):
            nc.vector.memset(f(k_lo[HD:P, :, :]), 0.0).then_inc(zeroed, 1)
            for ct in range(KT):
                dve.wait_ge(x_loaded[ct % 2], 16 * (ct // 2 + 1))
                norm.tile_stats(dve, 0, ct, x_in[:, ct % 2])
            dve.wait_ge(slot_full, 1)
            norm.after_means(dve, 0, slot[:, 0, 0:KT], dve_released, 1)
            dve.wait_ge(slot_full, 2)
            norm.after_vars(slot[:, 1, 0:KT], dve_released)
            norm.coefficients(dve, 0)
            for ct in range(KT):
                norm.tile_mid(dve, 0, ct, x_in[:, ct % 2])

            def body(b, last):
                r = ring_last if last else ring

                def v_lo(i):
                    dve.wait_ge(act_released, r.act_done(b, ("V", i)))
                    for jj in range(2):
                        src = slot[:, r.slot(("V", i)), jj * HALF:(jj + 1) * HALF].rearrange("p (g e d) -> p g e d", g=PAIRS, e=2)
                        heads = vt[:, 2 * i + jj].rearrange("p (g e) (w d) -> p g (e w) d", e=2, w=2)
                        done = nc.vector.tensor_tensor(heads[:, :, 1:3], src, f(heads[:, :, 0:4:3]), ALU.subtract)
                    done.then_inc(dve_released, 1)

                def qk_lo(h):
                    dve.wait_ge(act_released, r.act_done(b, ("QK", h)))
                    s = slot[:, r.slot(("QK", h)), :]
                    nc.vector.scalar_tensor_tensor(q_st[HD:P, h % 2, :], s[0:HD], SCALE, f(q_st[0:HD, h % 2, :]),
                                                   ALU.mult, ALU.subtract)
                    nc.vector.tensor_tensor(k_lo[0:HD, h % 2, :], s[HD:P], f(k_hi[HD:P, h % 2, :]), ALU.subtract
                                            ).then_inc(dve_released, 1)

                def maxima(u, t):
                    k = (TILES * u + t) % PROBS
                    dve.wait_ge(slot_full, r.full(b, ("S", u, t)))
                    nc.vector.tensor_reduce(neg_max[:, k:k + 1], slot[:, r.slot(("S", u, t)), :], AX_X, ALU.max,
                                            negate=True).then_inc(max_ready, 1)

                def inverses(u, t):
                    k = (TILES * u + t) % PROBS
                    dve.wait_ge(act_released, r.act_done(b, ("S", u, t)))
                    nc.vector.reciprocal(inverse[:, k:k + 1], total[:, k:k + 1]).then_inc(inverse_ready, 1)

                def turn_los(u, items):
                    for a in items:
                        dve.wait_ge(turn_hi, b * (TURNS * U) + (TURNS * u + a + 1))
                        nc.vector.tensor_tensor(pt_lo[:, u % 2, 2 * a:2 * a + 2, :], turn[:, a % 2],
                                                f(pt_hi[:, u % 2, 2 * a:2 * a + 2, :]), ALU.subtract).then_inc(turn_lo, 1)

                def add_sides(u):
                    own = slice(HD, P) if (u // UNITS) % 2 else slice(0, HD)
                    at = (u % UNITS) * QU
                    dve.wait_ge(side_ready, b * U + (u + 1))
                    if u % (2 * UNITS) == 0:
                        wait(dve, pair_lo, b * PAIRS + u // (2 * UNITS))
                    nc.vector.tensor_tensor(o_mid[own, at:at + QU], mix[own, u % 2, 0:QU], side[own, u % 2, :], ALU.add
                                            ).then_inc(mix_added, 1)

                def residual(m):
                    dve.wait_ge(slot_full, r.full(b, ("OUT", m)))
                    dve.wait_ge(x_loaded[m % 2], x_count(b, residual_load(last, m)))
                    nc.vector.scalar_tensor_tensor(probs[:, m, :], slot[:, r.slot(("OUT", m)), :], vecs[:, V_OB, m:m + 1],
                                                   x_in[:, m % 2], ALU.add, ALU.add).then_inc(dve_released, 1)

                for i in range(JT // 2):
                    v_lo(i)
                qk_lo(0)
                for s in range(U + 4):
                    if 3 <= s < U + 3:
                        add_sides(s - 3)
                    if s < U:
                        maxima(s, 0)
                    if 1 <= s <= U:
                        turn_los(s - 1, (0, 1))
                    if s < U:
                        inverses(s, 0)
                        maxima(s, 1)
                    if 1 <= s <= U:
                        turn_los(s - 1, (2,))
                    if s < U:
                        inverses(s, 1)
                    if 1 <= s <= U:
                        turn_los(s - 1, (3,))
                    if s < U and s % UNITS == 1 and s // UNITS + 1 < HEADS:
                        qk_lo(s // UNITS + 1)
                    if last:
                        continue
                    if STATS_AT <= s < STATS_AT + KT:
                        ct = s - STATS_AT
                        dve.wait_ge(x_loaded[ct % 2], x_count(b, ct))
                        norm.tile_stats(dve, b + 1, ct, x_in[:, ct % 2])
                    if s == MEANS_AT:
                        dve.wait_ge(slot_full, r.full(b, ("GN", s)))
                        norm.after_means(dve, b + 1, slot[:, r.slot(("GN", s)), 0:KT], dve_released,
                                         r.dve_done(b, ("GN", s)))
                    if s == VARS_AT:
                        dve.wait_ge(slot_full, r.full(b, ("GN", s)))
                        norm.after_vars(slot[:, r.slot(("GN", s)), 0:KT], dve_released)
                    if s == COEF_AT:
                        norm.coefficients(dve, b + 1)
                    if NORM_AT <= s < NORM_AT + KT:
                        norm.tile_mid(dve, b + 1, s - NORM_AT, x_in[:, (s - NORM_AT) % 2])
                for m in range(KT):
                    residual(m)

            over_batches(dve, body)

        @block.gpsimd
        def _(pool):
            norm.power(pool, dve_released, 2)
            for ct in range(KT):
                norm.tile_lo(pool, 0, ct, x_in[:, ct % 2], n_hi[:, ct], n_lo[:, ct])

            def body(b, last):
                r = ring_last if last else ring

                def normalise(u, t):
                    k = (TILES * u + t) % PROBS
                    wait_apart(pool, inverse_ready, b * (TILES * U) + (TILES * u + t + 1), scale_passed)
                    nc.gpsimd.tensor_scalar(probs[:, k, :], probs[:, k, :], inverse[:, k:k + 1], 1.0,
                                            ALU.mult, ALU.mult).then_inc(probs_ready, 1)

                def pair_los(u):
                    g = u // (2 * UNITS)
                    pool.wait_ge(pair_hi, b * PAIRS + (g + 1))
                    nc.gpsimd.tensor_tensor(o_lo[:, g, :], o_mid[:, :], f(o_hi[:, g, :]), ALU.subtract
                                            ).then_inc(pair_lo, 1)

                for s in range(U + 4):
                    if s >= 4 and (s - 4) % (2 * UNITS) == 2 * UNITS - 1:
                        pair_los(s - 4)
                    if s < U:
                        normalise(s, 0)
                        normalise(s, 1)
                    if not last and s == VARS_AT:
                        norm.power(pool, dve_released, r.dve_done(b, ("GN", s)))
                    if not last and NORM_AT <= s < NORM_AT + KT:
                        ct = s - NORM_AT
                        norm.tile_lo(pool, b + 1, ct, x_in[:, ct % 2], n_hi[:, ct], n_lo[:, ct])

            over_batches(pool, body)


def attend_single(nc, x1, out, scratch, vecs, b2, tables):
    with ExitStack() as ctx:
        def sb(name, shape, dt=F32):
            return ctx.enter_context(nc.sbuf_tensor(name, shape, dt))

        def sem(name):
            return ctx.enter_context(nc.semaphore(name))

        ident = tables[:, 0:P]
        norm = Norm(nc, "gn1", sb, sem, EPS1, vecs[:, V_GS, :], vecs[:, V_GB, :], tables[:, P:2 * P],
                    tables[:, 2 * P:2 * P + KT])
        w_q = sb("w_q", [P, KT, 2, HALF], F32R)
        w_k = sb("w_k", [P, KT, 2, HALF], F32R)
        w_m = sb("w_m", [P, KT, 2, HALF], F32R)
        n_hi = sb("n1_hi", [P, KT, N], F32R)
        n_lo = sb("n1_lo", [P, KT, N], F32R)
        k_hi = sb("k1_hi", [P, KT, N], F32R)
        k_lo = sb("k1_lo", [P, KT, N], F32R)
        v_hi = sb("v1_hi", [P, JT, C], F32R)
        v_lo = sb("v1_lo", [P, JT, C], F32R)
        q_hi = sb("q1_hi", [P, 2, KT, QU], F32R)
        q_lo = sb("q1_lo", [P, 2, KT, QU], F32R)
        probs = sb("probs1", [P, PROBS, N])
        pt_hi = sb("pt1_hi", [P, JT, QU], F32R)
        pt_lo = sb("pt1_lo", [P, JT, QU], F32R)
        x_in = sb("x1_in", [P, 2, N])
        neg_raw = sb("neg_raw", [P, PROBS])
        neg_max = sb("neg_max1", [P, PROBS])
        total = sb("total1", [P, PROBS])
        inverse = sb("inverse1", [P, PROBS])
        slot = ctx.enter_context(nc.psum_tensor("slot1", [P, 2, 2 * HALF], F32))
        turn = ctx.enter_context(nc.psum_tensor("turn1", [P, 2, 2, QU], F32))
        mix = ctx.enter_context(nc.psum_tensor("mix1", [P, 2, HALF], F32))

        x_loaded = [sem("x1_loaded0"), sem("x1_loaded1")]
        w_loaded = {k: sem(f"w1_loaded_{k}") for k in "qkm"}
        y_stored = [sem("y1_stored0"), sem("y1_stored1")]
        slot_full = sem("slot1_full")
        act_released = sem("act1_released")
        dve_released = sem("dve1_released")
        scale_passed = sem("scale1_passed")
        raw_ready = sem("raw_ready")
        max_ready = sem("max1_ready")
        inverse_ready = sem("inverse1_ready")
        probs_ready = sem("probs1_ready")
        turn_full = sem("turn1_full")
        turn_hi = sem("turn1_hi")
        turn_lo = sem("turn1_lo")
        mix_full = sem("mix1_full")
        mix_added = sem("mix1_added")
        U = UNITS
        MEANS_AT, VARS_AT, COEF_AT, NORM_AT = 0, 1, 2, 3
        X_STATS, X_NORM = 0, 6

        def order(last):
            items = [("K", m) for m in range(KT)] + [("V", i) for i in range(JT // 2)] + [("Q", 0)]
            for s in range(U):
                items += [("S", s, 0), ("S", s, 1)]
                if s + 1 < U:
                    items.append(("Q", s + 1))
                if not last and s in (MEANS_AT, VARS_AT):
                    items.append(("GN", s))
            return items

        ring = Slots(order(False), ("K", "V", "Q", "S"), ("K", "V", "Q", "GN"), 2)
        ring_last = Slots(order(True), ring.act_kinds, ring.dve_kinds, 2, ring)

        def x_count(b, k):
            return b * (8 * 3 * KT) + 16 * (KT + k // 2 + 1)

        def residual_load(last, u):
            return u if last else (4, 5, 10, 11)[u]

        block = ctx.enter_context(nc.Block())

        @block.sync
        def _(sp):
            def load_x(b, i):
                sp.dma_start(x_in[:, i % 2], x1[b, i * P:(i + 1) * P, :]).then_inc(x_loaded[i % 2], 16)

            for i in range(KT):
                if i >= 2:
                    sp.wait_ge(norm.tiles, i - 1)
                load_x(0, i)
            for w, k, chunk in ((w_k, "k", S_K1), (w_m, "m", S_M1), (w_q, "q", S_Q1)):
                sp.dma_start(f(w[:]), scratch[:, chunk:chunk + KT]).then_inc(w_loaded[k], 16)
            for i in range(KT):
                if i < 2:
                    sp.wait_ge(norm.tiles, KT - 1 + i)
                else:
                    sp.wait_ge(norm.lo_done, i - 1)
                load_x(0, i)

            def body(b, last):
                def residual(u):
                    sp.dma_start(x_in[:, u % 2].rearrange("p (k n) -> p k n", k=KT),
                                 x1[b, :, u * QU:(u + 1) * QU].rearrange("(k p) n -> p k n", p=P)
                                 ).then_inc(x_loaded[u % 2], 16)

                def store(u):
                    sp.wait_ge(mix_added, b * (KT * U) + KT * (u + 1))
                    sp.dma_start(out[b, :, u * QU:(u + 1) * QU].rearrange("(k p) n -> p k n", p=P),
                                 x_in[:, u % 2].rearrange("p (k n) -> p k n", k=KT)).then_inc(y_stored[u % 2], 16)

                if last:
                    for u in range(U):
                        wait(sp, y_stored[u % 2], b * 32 + 16 * (u // 2))
                        residual(u)
                        if u >= 1:
                            store(u - 1)
                    store(U - 1)
                    return
                for i in range(KT):
                    if i >= 2:
                        sp.wait_ge(norm.tiles, b * KT + (KT + i - 1))
                    elif isinstance(b, int):
                        sp.wait_ge(norm.lo_done, KT - 1 + i)
                    else:
                        sp.wait_ge(y_stored[i], b * 32)
                    load_x(b + 1, i)
                for u in range(2):
                    sp.wait_ge(norm.tiles, b * KT + (2 * KT - 1 + u))
                    residual(u)
                for u in range(2):
                    store(u)
                for i in range(KT):
                    if i < 2:
                        sp.wait_ge(y_stored[i], b * 32 + 16)
                    else:
                        sp.wait_ge(norm.lo_done, b * KT + (KT + i - 1))
                    load_x(b + 1, i)
                for u in (2, 3):
                    sp.wait_ge(norm.lo_done, b * KT + (KT + u + 1))
                    residual(u)
                for u in (2, 3):
                    store(u)

            over_batches(sp, body)
            for k in range(2):
                sp.wait_ge(y_stored[k], 32 * B)

        @block.tensor
        def _(pe):
            norm.mean_matmul(pe, 0, slot[:, 0, 0:KT]).then_inc(slot_full, 1)
            norm.var_matmul(pe, 0, slot[:, 1, 0:KT]).then_inc(slot_full, 1)
            for k in "kmq":
                pe.wait_ge(w_loaded[k], 16)

            def body(b, last):
                r = ring_last if last else ring

                def project_k(m):
                    r.wait_free(pe, act_released, dve_released, b, ("K", m))
                    for half in range(2):
                        cols = slice(half * HALF, (half + 1) * HALF)
                        for kt in range(KT):
                            if m == 0 and half == 0:
                                pe.wait_ge(norm.lo_done, b * KT + (kt + 1))
                            ms = slice(m * P, (m + 1) * P)
                            mm = three(nc, slot[:, r.slot(("K", m)), cols], w_k[:, kt, 0, ms], w_k[:, kt, 1, ms],
                                       n_hi[:, kt, cols], n_lo[:, kt, cols], kt == 0, kt == KT - 1)
                    mm.then_inc(slot_full, 1)

                def project_v(i):
                    r.wait_free(pe, act_released, dve_released, b, ("V", i))
                    for jj in range(2):
                        js = slice((2 * i + jj) * P, (2 * i + jj + 1) * P)
                        for kt in range(KT):
                            mm = three(nc, slot[:, r.slot(("V", i)), jj * HALF:(jj + 1) * HALF],
                                       n_hi[:, kt, js], n_lo[:, kt, js], w_m[:, kt, 0, :], w_m[:, kt, 1, :],
                                       kt == 0, kt == KT - 1)
                    mm.then_inc(slot_full, 1)

                def project_q(u):
                    r.wait_free(pe, act_released, dve_released, b, ("Q", u))
                    cols = slice(u * QU, (u + 1) * QU)
                    for m in range(KT):
                        for kt in range(KT):
                            ms = slice(m * P, (m + 1) * P)
                            mm = three(nc, slot[:, r.slot(("Q", u)), m * QU:(m + 1) * QU],
                                       w_q[:, kt, 0, ms], w_q[:, kt, 1, ms],
                                       n_hi[:, kt, cols], n_lo[:, kt, cols], kt == 0, kt == KT - 1)
                    mm.then_inc(slot_full, 1)

                def scores(u, t):
                    r.wait_free(pe, act_released, dve_released, b, ("S", u, t))
                    if t == 0:
                        pe.wait_ge(act_released, r.act_done(b, ("Q", u)))
                        pe.wait_ge(dve_released, r.dve_done(b, ("Q", u)))
                    qs = slice(t * P, (t + 1) * P)
                    for half in range(2):
                        cols = slice(half * HALF, (half + 1) * HALF)
                        for kt in range(KT):
                            mm = three(nc, slot[:, r.slot(("S", u, t)), cols], q_hi[:, u % 2, kt, qs], q_lo[:, u % 2, kt, qs],
                                       k_hi[:, kt, cols], k_lo[:, kt, cols], kt == 0, kt == KT - 1)
                    mm.then_inc(slot_full, 1)

                def turns(u):
                    pe.wait_ge(probs_ready, b * (TILES * U) + TILES * (u + 1))
                    for a in range(TURNS):
                        wait(pe, turn_lo, b * (TURNS * U) + (TURNS * u + a - 1))
                        for jj in range(2):
                            for t in range(TILES):
                                mm = nc.tensor.transpose(turn[:, a % 2, jj, t * P:(t + 1) * P],
                                                         probs[:, (TILES * u + t) % PROBS,
                                                               (2 * a + jj) * P:(2 * a + jj + 1) * P], ident)
                        mm.then_inc(turn_full, 1)

                def mixes(u):
                    pe.wait_ge(turn_lo, b * (TURNS * U) + TURNS * (u + 1))
                    for ot in range(KT):
                        wait(pe, mix_added, b * (KT * U) + (KT * u + ot - 1))
                        os = slice(ot * P, (ot + 1) * P)
                        for j in range(JT):
                            mm = three(nc, mix[:, ot % 2, 0:QU], v_hi[:, j, os], v_lo[:, j, os], pt_hi[:, j, :], pt_lo[:, j, :],
                                       j == 0, j == JT - 1)
                        mm.then_inc(mix_full, 1)

                def group_stats(s, product):
                    r.wait_free(pe, act_released, dve_released, b, ("GN", s))
                    product(pe, b + 1, slot[:, r.slot(("GN", s)), 0:KT]).then_inc(slot_full, 1)

                for m in range(KT):
                    project_k(m)
                for i in range(JT // 2):
                    project_v(i)
                project_q(0)
                for s in range(U + 1):
                    if s < U:
                        scores(s, 0)
                    if s >= 1:
                        turns(s - 1)
                    if s < U:
                        scores(s, 1)
                    if s + 1 < U:
                        project_q(s + 1)
                    if not last and s == MEANS_AT:
                        group_stats(s, norm.mean_matmul)
                    if not last and s == VARS_AT:
                        group_stats(s, norm.var_matmul)
                    if s >= 1:
                        mixes(s - 1)

            over_batches(pe, body)

        @block.scalar
        def _(act):
            for ct in range(KT):
                act.wait_ge(x_loaded[ct % 2], 16 * (2 + ct // 2 + 1))
                norm.tile_hi(act, 0, ct, x_in[:, ct % 2], n_hi[:, ct])

            def body(b, last):
                r = ring_last if last else ring

                def k_his(m):
                    act.wait_ge(slot_full, r.full(b, ("K", m)))
                    nc.scalar.activation(k_hi[:, m], slot[:, r.slot(("K", m)), :], ACT.Identity,
                                         bias=vecs[:, V_BK, m:m + 1]).then_inc(act_released, 1)

                def v_his(i):
                    act.wait_ge(slot_full, r.full(b, ("V", i)))
                    nc.scalar.activation(v_hi[:, 2 * i:2 * i + 2].rearrange("p j c -> p (j c)"),
                                         slot[:, r.slot(("V", i)), :], ACT.Copy).then_inc(act_released, 1)

                def q_his(u):
                    act.wait_ge(slot_full, r.full(b, ("Q", u)))
                    for m in range(KT):
                        done = nc.scalar.activation(q_hi[:, u % 2, m], slot[:, r.slot(("Q", u)), m * QU:(m + 1) * QU],
                                                    ACT.Identity, bias=vecs[:, V_BQ, m:m + 1])
                    done.then_inc(act_released, 1)

                def exponentials(u, t):
                    k = (TILES * u + t) % PROBS
                    act.wait_ge(max_ready, b * (TILES * U) + (TILES * u + t + 1))
                    wait(act, turn_full, b * (TURNS * U) + TURNS * (u - 1))
                    nc.scalar.activation(probs[:, k, :], slot[:, r.slot(("S", u, t)), :], ACT.Exp, scale=SCALE,
                                         bias=neg_max[:, k:k + 1], accum_out=total[:, k:k + 1]).then_inc(act_released, 1)

                def turn_his(u):
                    for a in range(TURNS):
                        act.wait_ge(turn_full, b * (TURNS * U) + (TURNS * u + a + 1))
                        if a == 0:
                            wait(act, mix_full, b * (KT * U) + KT * u)
                        nc.scalar.activation(pt_hi[:, 2 * a:2 * a + 2, :], turn[:, a % 2], ACT.Copy).then_inc(turn_hi, 1)

                for m in range(KT):
                    k_his(m)
                for i in range(JT // 2):
                    v_his(i)
                q_his(0)
                for s in range(U + 1):
                    if s < U:
                        exponentials(s, 0)
                    if s >= 1:
                        turn_his(s - 1)
                    if s < U:
                        exponentials(s, 1)
                    if s + 1 < U:
                        q_his(s + 1)
                    if not last and s == NORM_AT:
                        for ct in range(KT):
                            act.wait_ge(x_loaded[ct % 2], x_count(b, X_NORM + ct))
                            norm.tile_hi(act, b + 1, ct, x_in[:, ct % 2], n_hi[:, ct])

            over_batches(act, body)

        @block.vector
        def _(dve):
            for ct in range(KT):
                dve.wait_ge(x_loaded[ct % 2], 16 * (ct // 2 + 1))
                norm.tile_stats(dve, 0, ct, x_in[:, ct % 2])
            dve.wait_ge(slot_full, 1)
            norm.after_means(dve, 0, slot[:, 0, 0:KT], dve_released, 1)
            dve.wait_ge(slot_full, 2)
            norm.after_vars(slot[:, 1, 0:KT], dve_released)
            norm.coefficients(dve, 0)
            for ct in range(KT):
                norm.tile_mid(dve, 0, ct, x_in[:, ct % 2])

            def body(b, last):
                r = ring_last if last else ring

                def k_los(m):
                    dve.wait_ge(act_released, r.act_done(b, ("K", m)))
                    nc.vector.scalar_tensor_tensor(k_lo[:, m], slot[:, r.slot(("K", m)), :], vecs[:, V_BK, m:m + 1],
                                                   f(k_hi[:, m]), ALU.add, ALU.subtract).then_inc(dve_released, 1)

                def v_los(i):
                    dve.wait_ge(act_released, r.act_done(b, ("V", i)))
                    nc.vector.tensor_tensor(v_lo[:, 2 * i:2 * i + 2].rearrange("p j c -> p (j c)"),
                                            slot[:, r.slot(("V", i)), :],
                                            f(v_hi[:, 2 * i:2 * i + 2].rearrange("p j c -> p (j c)")),
                                            ALU.subtract).then_inc(dve_released, 1)

                def q_los(u):
                    dve.wait_ge(act_released, r.act_done(b, ("Q", u)))
                    for m in range(KT):
                        done = nc.vector.scalar_tensor_tensor(
                            q_lo[:, u % 2, m], slot[:, r.slot(("Q", u)), m * QU:(m + 1) * QU], vecs[:, V_BQ, m:m + 1],
                            f(q_hi[:, u % 2, m]), ALU.add, ALU.subtract)
                    done.then_inc(dve_released, 1)

                def maxima(u, t):
                    k = (TILES * u + t) % PROBS
                    n = b * (TILES * U) + (TILES * u + t + 1)
                    dve.wait_ge(slot_full, r.full(b, ("S", u, t)))
                    nc.vector.tensor_reduce(neg_raw[:, k:k + 1], slot[:, r.slot(("S", u, t)), :], AX_X, ALU.max,
                                            negate=True).then_inc(raw_ready, 1)
                    dve.wait_ge(raw_ready, n)
                    nc.vector.tensor_scalar(neg_max[:, k:k + 1], neg_raw[:, k:k + 1], SCALE, None, ALU.mult
                                            ).then_inc(max_ready, 1)

                def inverses(u, t):
                    k = (TILES * u + t) % PROBS
                    dve.wait_ge(act_released, r.act_done(b, ("S", u, t)))
                    nc.vector.reciprocal(inverse[:, k:k + 1], total[:, k:k + 1]).then_inc(inverse_ready, 1)

                def turn_los(u):
                    for a in range(TURNS):
                        dve.wait_ge(turn_hi, b * (TURNS * U) + (TURNS * u + a + 1))
                        nc.vector.tensor_tensor(pt_lo[:, 2 * a:2 * a + 2, :], turn[:, a % 2],
                                                f(pt_hi[:, 2 * a:2 * a + 2, :]), ALU.subtract).then_inc(turn_lo, 1)

                def finish(u):
                    dve.wait_ge(x_loaded[u % 2], x_count(b, residual_load(last, u)))
                    for ot in range(KT):
                        dve.wait_ge(mix_full, b * (KT * U) + (KT * u + ot + 1))
                        y = x_in[:, u % 2, ot * QU:(ot + 1) * QU]
                        nc.vector.scalar_tensor_tensor(y, mix[:, ot % 2, 0:QU], b2[:, ot:ot + 1], y, ALU.add, ALU.add
                                                       ).then_inc(mix_added, 1)

                for m in range(KT):
                    k_los(m)
                for i in range(JT // 2):
                    v_los(i)
                    if not last:
                        dve.wait_ge(x_loaded[i % 2], x_count(b, X_STATS + i))
                        norm.tile_stats(dve, b + 1, i, x_in[:, i % 2])
                q_los(0)
                for s in range(U + 1):
                    if s < U:
                        maxima(s, 0)
                        inverses(s, 0)
                    if s >= 1:
                        turn_los(s - 1)
                    if s < U:
                        maxima(s, 1)
                        inverses(s, 1)
                    if s + 1 < U:
                        q_los(s + 1)
                    if not last and s == MEANS_AT:
                        dve.wait_ge(slot_full, r.full(b, ("GN", s)))
                        norm.after_means(dve, b + 1, slot[:, r.slot(("GN", s)), 0:KT], dve_released,
                                         r.dve_done(b, ("GN", s)))
                    if not last and s == VARS_AT:
                        dve.wait_ge(slot_full, r.full(b, ("GN", s)))
                        norm.after_vars(slot[:, r.slot(("GN", s)), 0:KT], dve_released)
                    if not last and s == COEF_AT:
                        norm.coefficients(dve, b + 1)
                    if not last and s == NORM_AT:
                        for ct in range(KT):
                            norm.tile_mid(dve, b + 1, ct, x_in[:, ct % 2])
                    if s >= 1:
                        finish(s - 1)

            over_batches(dve, body)

        @block.gpsimd
        def _(pool):
            norm.power(pool, dve_released, 2)
            for ct in range(KT):
                norm.tile_lo(pool, 0, ct, x_in[:, ct % 2], n_hi[:, ct], n_lo[:, ct])

            def body(b, last):
                r = ring_last if last else ring
                for s in range(U):
                    for t in range(TILES):
                        k = (TILES * s + t) % PROBS
                        wait_apart(pool, inverse_ready, b * (TILES * U) + (TILES * s + t + 1), scale_passed)
                        nc.gpsimd.tensor_scalar(probs[:, k, :], probs[:, k, :], inverse[:, k:k + 1], 1.0,
                                                ALU.mult, ALU.mult).then_inc(probs_ready, 1)
                    if not last and s == VARS_AT:
                        norm.power(pool, dve_released, r.dve_done(b, ("GN", s)))
                    if not last and s == NORM_AT:
                        for ct in range(KT):
                            norm.tile_lo(pool, b + 1, ct, x_in[:, ct % 2], n_hi[:, ct], n_lo[:, ct])

            over_batches(pool, body)


def two_attentions(nc, x, w_in, v_in, t_in, out):
    x1 = nc.dram_tensor("x1", (B, C, N), F32, kind="Internal").ap()
    scratch = nc.dram_tensor("w_split_dram", (P, CHUNKS, 2, HALF), F32, kind="Internal").ap()
    with ExitStack() as ctx:
        vecs = ctx.enter_context(nc.sbuf_tensor("vecs", [P, 9, KT], F32))
        tables = ctx.enter_context(nc.sbuf_tensor("tables", [P, 2 * P + KT], F32))
        b2 = ctx.enter_context(nc.sbuf_tensor("b2", [P, KT], F32))
        small_in = ctx.enter_context(nc.semaphore("small_in"))
        with nc.Block() as block:
            @block.sync
            def _(sp):
                sp.dma_start(vecs[:], v_in).then_inc(small_in, 16)
                sp.dma_start(tables[:], t_in).then_inc(small_in, 16)
                sp.wait_ge(small_in, 32)
        split_weights(nc, w_in, scratch, vecs, b2)
        attend_heads(nc, x, x1, scratch, vecs, tables)
        attend_single(nc, x1, out, scratch, vecs, b2, tables)


def kernel(**inputs):
    import numpy as np
    import concourse.bacc as bacc
    from concourse.bass_utils import run_bass_kernel_spmd as run

    def host(name):
        return np.asarray(inputs[name])

    def contraction_first(wt):
        return wt.reshape(KT, P, -1).transpose(1, 0, 2)

    qkv = host("L0_conv_qkv_w").reshape(HEADS, 3, HD, C)
    w_qk = qkv[:, 0:2].reshape(HEADS, P, KT, P).transpose(3, 0, 2, 1).reshape(P, HEADS, HALF)
    w_v = contraction_first(qkv[:, 2].reshape(C, C).T)
    w_o = host("L0_conv_out_w").reshape(KT, P, KT, P).transpose(3, 0, 2, 1).reshape(P, KT, HALF)
    w_in = np.ascontiguousarray(np.concatenate([
        w_qk, w_v, w_o, contraction_first(host("L1_conv_wq").T), contraction_first(host("L1_conv_wk").T),
        contraction_first(host("L1_conv_wp").T), contraction_first(host("L1_conv_wv"))], axis=1))
    v_in = np.ascontiguousarray(np.stack([host(n).reshape(KT, P).T for n in (
        "L0_conv_gn_w", "L0_conv_gn_b", "L0_conv_out_b", "L1_conv_gn_scale", "L1_conv_gn_bias",
        "L1_conv_bq", "L1_conv_bk", "L1_conv_bv", "L1_conv_bp")], axis=1))
    size = C // GROUPS
    averager = np.kron(np.eye(P // size), np.full((size, size), 1.0 / size))
    t_in = np.concatenate([np.eye(P), averager, np.full((P, KT), -0.5)], axis=1).astype(np.float32)
    x = host("x").reshape(B, C, N)

    nc = bacc.Bacc("TRN2", target_bir_lowering=False, num_devices=1)
    arrays, args = {}, []
    for name, a in (("x", x), ("w_in", w_in), ("v_in", v_in), ("t_in", t_in)):
        arrays[name] = np.ascontiguousarray(a)
        args.append(nc.dram_tensor(name, a.shape, mybir.dt.from_np(a.dtype), kind="ExternalInput").ap())
    out = nc.dram_tensor("out", (B, C, N), F32, kind="ExternalOutput").ap()
    two_attentions(nc, *args, out)
    r = run(nc, [arrays], core_ids=[0])
    return r.results[0]["out"].reshape(B, C, 32, 32)
```

```python
from contextlib import ExitStack

import concourse.bass as bass
from concourse import mybir

ALU = mybir.AluOpType
ACT = mybir.ActivationFunctionType
F32 = mybir.dt.float32
F32R = mybir.dt.float32r
AX_X = mybir.AxisListType.X

P = 128
B, C, N = 8, 512, 1024
KT = C // P
JT = N // P
HEADS, HD = 8, 64
PAIRS = HEADS // 2
QU = 256
TILES = QU // P
UNITS = N // QU
HALF = 512
TURNS = JT // 2
PROBS = 4
SCALE = float(C) ** -0.5
EPS0, EPS1 = 1e-5, 1e-6
GROUPS = 32

V_GNW, V_GNB, V_OB, V_GS, V_GB, V_BQ, V_BK, V_BV, V_BP = range(9)
W_QK, W_V, W_O, W_Q1, W_K1, W_P1, W_V1 = 0, 8, 12, 16, 20, 24, 28
S_QK, S_V, S_O, S_Q1, S_K1, S_M1 = 0, 8, 12, 16, 20, 24
CHUNKS = 28


def f(ap):
    return ap.bitcast(F32)


def wait(eng, sem, value):
    if isinstance(value, int) and value <= 0:
        return
    eng.wait_ge(sem, value)


def wait_apart(eng, sem, value, passed):
    eng.wait_ge(sem, value)
    eng.sem_inc(passed, 1)


class Slots:

    def __init__(self, pre, items, act_kinds, dve_kinds, whole=None):
        self.pre, self.items = pre, items
        self.act_kinds, self.dve_kinds = act_kinds, dve_kinds
        self.pos = {it: n for n, it in enumerate(items)}
        self.act = self.running(items, act_kinds)
        self.dve = self.running(items, dve_kinds)
        self.pre_act = self.running(pre, act_kinds)
        self.pre_dve = self.running(pre, dve_kinds)
        w = whole or self
        self.per_full, self.per_act, self.per_dve = len(w.items), w.act[-1], w.dve[-1]

    @staticmethod
    def running(items, kinds):
        counts = [0]
        for it in items:
            counts.append(counts[-1] + (it[0] in kinds))
        return counts

    def slot(self, it):
        return self.pos[it] % 2

    def full(self, b, it):
        return b * self.per_full + (len(self.pre) + self.pos[it] + 1)

    def act_done(self, b, it):
        return b * self.per_act + (self.pre_act[-1] + self.act[self.pos[it] + 1])

    def dve_done(self, b, it):
        return b * self.per_dve + (self.pre_dve[-1] + self.dve[self.pos[it] + 1])

    def act_before(self, b):
        return b * self.per_act + self.pre_act[-1]

    def dve_before(self, b):
        return b * self.per_dve + self.pre_dve[-1]

    def wait_free(self, eng, act_released, dve_released, b, it):
        n = self.pos[it] - 2
        if n < 0 and isinstance(b, int) and b == 0:
            kind = self.pre[n][0]
            n += len(self.pre)
            act, dve = self.pre_act[n + 1], self.pre_dve[n + 1]
        else:
            kind = self.items[n][0]
            back = 0 if n >= 0 else len(self.items)
            act = self.pre_act[-1] + self.act[n + back + 1] - (self.act[-1] if back else 0)
            dve = self.pre_dve[-1] + self.dve[n + back + 1] - (self.dve[-1] if back else 0)
        if kind in self.act_kinds:
            wait(eng, act_released, b * self.per_act + act)
        if kind in self.dve_kinds:
            wait(eng, dve_released, b * self.per_dve + dve)


def over_batches(eng, body):
    body(0, False)
    with eng.Fori(1, B - 1, 1) as b:
        body(b, False)
    body(B - 1, True)


def split_weights(nc, w_in, scratch, vecs, b2):
    with ExitStack() as ctx:
        def sb(name, shape, dt=F32):
            return ctx.enter_context(nc.sbuf_tensor(name, shape, dt))

        def sem(name):
            return ctx.enter_context(nc.semaphore(name))

        raw = sb("w_raw", [P, 2, 4, HALF])
        wv = sb("w_v1", [P, KT, C])
        wp = sb("w_p1", [P, KT, C])
        both = sb("w_split", [P, 2, 4, 2, HALF], F32R)
        prod = ctx.enter_context(nc.psum_tensor("w_prod", [P, KT, HALF], F32))
        bias = ctx.enter_context(nc.psum_tensor("w_bias", [P, HALF], F32))
        loaded = [sem("w_loaded0"), sem("w_loaded1")]
        stored = [sem("w_stored0"), sem("w_stored1")]
        pair_in, hi_done, lo_done = sem("w_pair_in"), sem("w_hi"), sem("w_lo")
        prod_done, bias_done, b2_done = sem("w_prod_done"), sem("w_bias_done"), sem("w_b2")
        groups = CHUNKS // 4
        block = ctx.enter_context(nc.Block())

        def source(g):
            return raw[:, g % 2] if g < groups - 1 else prod[:, :, :]

        @block.sync
        def _(sp):
            for g in range(groups):
                if g < groups - 1:
                    if g >= 2:
                        sp.wait_ge(lo_done, g - 1)
                    sp.dma_start(raw[:, g % 2], w_in[:, 4 * g:4 * g + 4, :]).then_inc(loaded[g % 2], 16)
                if g == 1:
                    sp.dma_start(wv[:], w_in[:, W_V1:W_V1 + KT, :]).then_inc(pair_in, 16)
                    sp.dma_start(wp[:], w_in[:, W_P1:W_P1 + KT, :]).then_inc(pair_in, 16)
                if g >= 1:
                    sp.wait_ge(lo_done, g)
                    sp.dma_start(scratch[:, 4 * g - 4:4 * g], f(both[:, (g - 1) % 2])).then_inc(stored[(g - 1) % 2], 16)
            sp.wait_ge(lo_done, groups)
            sp.dma_start(scratch[:, CHUNKS - 4:CHUNKS], f(both[:, (groups - 1) % 2])).then_inc(stored[(groups - 1) % 2], 16)
            sp.wait_ge(stored[0], 16 * ((groups + 1) // 2))
            sp.wait_ge(stored[1], 16 * (groups // 2))

        @block.scalar
        def _(act):
            for g in range(groups):
                if g < groups - 1:
                    act.wait_ge(loaded[g % 2], 16 * (g // 2 + 1))
                else:
                    act.wait_ge(prod_done, 1)
                if g >= 2:
                    act.wait_ge(stored[g % 2], 16 * (g // 2))
                nc.scalar.activation(both[:, g % 2, :, 0, :], source(g), ACT.Copy).then_inc(hi_done, 1)

        @block.vector
        def _(dve):
            for g in range(groups):
                dve.wait_ge(hi_done, g + 1)
                nc.vector.tensor_tensor(both[:, g % 2, :, 1, :], source(g), f(both[:, g % 2, :, 0, :]),
                                        ALU.subtract).then_inc(lo_done, 1)
            dve.wait_ge(bias_done, 1)
            nc.vector.tensor_tensor(b2[:], bias[:, 0:KT], vecs[:, V_BP, :], ALU.add).then_inc(b2_done, 1)
            dve.wait_ge(b2_done, 1)

        @block.tensor
        def _(pe):
            pe.wait_ge(pair_in, 32)
            for ct in range(KT):
                for mt in range(KT):
                    last = nc.tensor.matmul(prod[:, ct, :], wv[:, mt, ct * P:(ct + 1) * P], wp[:, mt, :],
                                            start=(mt == 0), stop=(mt == KT - 1))
            last.then_inc(prod_done, 1)
            for ot in range(KT):
                for mt in range(KT):
                    last = nc.tensor.matmul(bias[:, ot:ot + 1], wp[:, mt, ot * P:(ot + 1) * P],
                                            vecs[:, V_BV, mt:mt + 1], start=(mt == 0), stop=(mt == KT - 1))
            last.then_inc(bias_done, 1)


class Norm:

    CHAIN = 6

    def __init__(self, nc, tag, sb, sem, eps, weight, shift, averager, minus_half):
        self.nc, self.eps, self.weight, self.shift = nc, eps, weight, shift
        self.averager, self.minus_half = averager, minus_half
        self.stats = sb(f"{tag}_stats", [P, KT, 2, 6])
        self.mv = sb(f"{tag}_mean_var", [P, KT, 2])
        self.gmean = sb(f"{tag}_group_mean", [P, KT])
        self.dev = sb(f"{tag}_deviation", [P, KT])
        self.var = sb(f"{tag}_var", [P, KT])
        self.vareps = sb(f"{tag}_var_eps", [P, KT])
        self.rstd = sb(f"{tag}_rstd", [P, KT])
        self.a = sb(f"{tag}_a", [P, KT])
        self.ma = sb(f"{tag}_mean_a", [P, KT])
        self.b = sb(f"{tag}_b", [P, KT])
        self.halves = sem(f"{tag}_halves")
        self.passed = sem(f"{tag}_passed")
        self.tiles = sem(f"{tag}_tiles")
        self.chain = sem(f"{tag}_chain")
        self.rstd_ready = sem(f"{tag}_rstd_ready")
        self.hi_done = sem(f"{tag}_hi_done")
        self.mid_done = sem(f"{tag}_mid_done")
        self.lo_done = sem(f"{tag}_lo_done")

    def tile_stats(self, dve, n, ct, x):
        v = self.nc.vector
        for k in range(2):
            v.bn_stats(self.stats[:, ct, k, :], x[:, k * HALF:(k + 1) * HALF]).then_inc(self.halves, 1)
        wait_apart(dve, self.halves, n * (2 * KT) + (2 * ct + 2), self.passed)
        v.bn_aggr(self.mv[:, ct, :], self.stats[:, ct].rearrange("p a b -> p (a b)")).then_inc(self.tiles, 1)

    def mean_matmul(self, pe, n, out):
        pe.wait_ge(self.tiles, n * KT + KT)
        return self.nc.tensor.matmul(out, self.averager, self.mv[:, :, 0], start=True, stop=True)

    def after_means(self, dve, n, psum, released, released_count):
        v = self.nc.vector
        v.tensor_copy(self.gmean[:], psum).then_inc(released, 1)
        dve.wait_ge(released, released_count)
        dve.wait_ge(self.tiles, n * KT + KT)
        v.tensor_tensor(self.dev[:], self.mv[:, :, 0], self.gmean[:], ALU.subtract).then_inc(self.chain, 1)
        dve.wait_ge(self.chain, n * self.CHAIN + 1)
        v.tensor_tensor(self.var[:], self.dev[:], self.dev[:], ALU.mult).then_inc(self.chain, 1)
        dve.wait_ge(self.chain, n * self.CHAIN + 2)
        v.tensor_tensor(self.var[:], self.var[:], self.mv[:, :, 1], ALU.add).then_inc(self.chain, 1)

    def var_matmul(self, pe, n, out):
        pe.wait_ge(self.chain, n * self.CHAIN + 3)
        return self.nc.tensor.matmul(out, self.averager, self.var[:], start=True, stop=True)

    def after_vars(self, psum, released):
        self.nc.vector.tensor_scalar(self.vareps[:], psum, self.eps, None, ALU.add).then_inc(released, 1)

    def power(self, pool, released, released_count):
        pool.wait_ge(released, released_count)
        self.nc.gpsimd.tensor_tensor(self.rstd[:], self.vareps[:], self.minus_half, ALU.pow
                                     ).then_inc(self.rstd_ready, 1)

    def coefficients(self, dve, n):
        v = self.nc.vector
        dve.wait_ge(self.rstd_ready, n + 1)
        v.tensor_tensor(self.a[:], self.rstd[:], self.weight, ALU.mult).then_inc(self.chain, 1)
        dve.wait_ge(self.chain, n * self.CHAIN + 4)
        v.tensor_tensor(self.ma[:], self.gmean[:], self.a[:], ALU.mult).then_inc(self.chain, 1)
        dve.wait_ge(self.chain, n * self.CHAIN + 5)
        v.tensor_tensor(self.b[:], self.shift, self.ma[:], ALU.subtract).then_inc(self.chain, 1)

    def tile_hi(self, act, n, ct, x, out):
        act.wait_ge(self.chain, n * self.CHAIN + 6)
        self.nc.scalar.activation(out, x, ACT.Identity, bias=self.b[:, ct:ct + 1],
                                  scale=self.a[:, ct:ct + 1]).then_inc(self.hi_done, 1)

    def tile_mid(self, dve, n, ct, x):
        dve.wait_ge(self.chain, n * self.CHAIN + 6)
        dve.wait_ge(self.hi_done, n * KT + (ct + 1))
        self.nc.vector.tensor_scalar(x, x, self.a[:, ct:ct + 1], self.b[:, ct:ct + 1], ALU.mult, ALU.add
                                     ).then_inc(self.mid_done, 1)

    def tile_lo(self, pool, n, ct, x, hi, out):
        pool.wait_ge(self.mid_done, n * KT + (ct + 1))
        self.nc.gpsimd.tensor_tensor(out, x, f(hi), ALU.subtract).then_inc(self.lo_done, 1)


def three(nc, out, w_hi, w_lo, m_hi, m_lo, first, last):
    nc.tensor.matmul(out, w_hi, m_hi, start=first, stop=False)
    nc.tensor.matmul(out, w_hi, m_lo, start=False, stop=False)
    return nc.tensor.matmul(out, w_lo, m_hi, start=False, stop=last)


def attend_heads(nc, x, x1, scratch, vecs, tables):
    with ExitStack() as ctx:
        def sb(name, shape, dt=F32):
            return ctx.enter_context(nc.sbuf_tensor(name, shape, dt))

        def sem(name):
            return ctx.enter_context(nc.semaphore(name))

        U = HEADS * UNITS
        TILES_KEPT = 6
        LAG = 2
        BEHIND = 3
        ident = tables[:, 0:P]
        norm = Norm(nc, "gn0", sb, sem, EPS0, vecs[:, V_GNW, :], vecs[:, V_GNB, :], tables[:, P:2 * P],
                    tables[:, 2 * P:2 * P + KT])
        w_qk = sb("w_qk", [P, 2, 2, KT, P], F32R)
        w_vo = sb("w_vo", [P, 4, 2, HALF], F32R)
        n_hi = sb("n_hi", [P, KT, N], F32R)
        n_lo = sb("n_lo", [P, KT, N], F32R)
        vt = sb("vt", [P, JT, HEADS, P], F32R)
        q_st = sb("q_st", [P, 2, N], F32R)
        k_hi = sb("k_hi", [P, 2, N], F32R)
        k_lo = sb("k_lo", [P, 2, N], F32R)
        probs = sb("probs", [P, TILES_KEPT, N])
        pt_hi = sb("pt_hi", [P, TURNS, 2, QU], F32R)
        pt_lo = sb("pt_lo", [P, TURNS, 2, QU], F32R)
        side = sb("side", [P, 2, QU])
        o_mid = sb("o_mid", [P, 2, N])
        o_hi = sb("o_hi", [P, PAIRS, N], F32R)
        o_lo = sb("o_lo", [P, PAIRS, N], F32R)
        x_in = sb("x_in", [P, 2, N])
        neg_max = sb("neg_max", [P, TILES_KEPT])
        total = sb("total", [P, TILES_KEPT])
        inverse = sb("inverse", [P, TILES_KEPT])
        slot = ctx.enter_context(nc.psum_tensor("slot", [P, 2, 2 * HALF], F32))
        turn = ctx.enter_context(nc.psum_tensor("turn", [P, 2, 2, QU], F32))
        mix = ctx.enter_context(nc.psum_tensor("mix", [P, 2, HALF], F32))

        x_loaded = [sem("x_loaded0"), sem("x_loaded1")]
        qk_loaded = [sem("wqk_loaded0"), sem("wqk_loaded1")]
        v_loaded = [sem(f"wv_loaded{i}") for i in range(4)]
        o_loaded = [sem(f"wo_loaded{i}") for i in range(4)]
        r_loaded = [sem(f"residual_loaded{i}") for i in range(KT)]
        y_stored = [sem(f"y_stored{i}") for i in range(KT)]
        scale_passed = sem("scale_passed")
        zeroed = sem("zeroed")
        slot_full = sem("slot_full")
        act_released = sem("act_released")
        dve_released = sem("dve_released")
        q_hi_ready = sem("q_hi_ready")
        k_hi_twice = sem("k_hi_twice")
        max_ready = sem("max_ready")
        inverse_ready = sem("inverse_ready")
        probs_ready = sem("probs_ready")
        turn_full = sem("turn_full")
        turn_hi = sem("turn_hi")
        turn_lo = sem("turn_lo")
        mixed = sem("mixed")
        side_ready = sem("side_ready")
        mix_added = sem("mix_added")
        pair_hi = sem("pair_hi")
        pair_lo = sem("pair_lo")
        STATS_AT, MEANS_AT, VARS_AT, COEF_AT, NORM_AT = 1, 6, 8, 9, 27

        def projected_at(s):
            if s >= U:
                return HEADS, s - U
            if s % 2 == 0 and s // UNITS + 1 < HEADS:
                return s // UNITS + 1, (s % UNITS) // 2
            return None

        def order(last):
            items = []
            for s in range(U):
                items.append(("S", s, 0))
                if projected_at(s):
                    items.append(("QK",) + projected_at(s))
                items.append(("S", s, 1))
                if s < LAG:
                    items += [("V", 2 * s), ("V", 2 * s + 1)]
                if not last and s in (MEANS_AT, VARS_AT):
                    items.append(("GN", s))
            if not last:
                items += [("QK", HEADS, 0), ("QK", HEADS, 1)]
            return items + [("OUT", m) for m in range(KT)]

        pre = [("GN", "means"), ("GN", "vars"), ("QK", 0, 0), ("QK", 0, 1)]
        ring = Slots(pre, order(False), ("V", "QK", "S"), ("V", "QK", "GN", "OUT"))
        ring_last = Slots(pre, order(True), ring.act_kinds, ring.dve_kinds, ring)

        def x_count(b, k):
            return b * (8 * 2 * KT) + 16 * (KT + k // 2 + 1)

        def x1_tile(m):
            return (4, 5, 2, 3)[m]

        block = ctx.enter_context(nc.Block())

        @block.sync
        def _(sp):
            def load_x(b, i):
                sp.dma_start(x_in[:, i % 2], x[b, i * P:(i + 1) * P, :]).then_inc(x_loaded[i % 2], 16)

            def load_qk(h):
                sp.dma_start(f(w_qk[:, h % 2].rearrange("p a k m -> p (a k m)")),
                             scratch[:, S_QK + h % HEADS].rearrange("p a n -> p (a n)")).then_inc(qk_loaded[h % 2], 16)

            def load_vo(c, chunk, loaded):
                sp.dma_start(f(w_vo[:, c]), scratch[:, chunk + c]).then_inc(loaded[c], 16)

            for i in range(KT):
                if i >= 2:
                    sp.wait_ge(norm.tiles, i - 1)
                load_x(0, i)
            for c in range(2):
                load_qk(c)
            for i in range(2):
                sp.wait_ge(norm.tiles, KT - 1 + i)
                load_x(0, i)
            for c in range(4):
                load_vo(c, S_V, v_loaded)
            for i in range(2, KT):
                sp.wait_ge(norm.lo_done, i - 1)
                load_x(0, i)

            def body(b, last):
                r = ring_last if last else ring

                def store(m):
                    sp.wait_ge(dve_released, r.dve_done(b, ("OUT", m)))
                    sp.dma_start(x1[b, m * P:(m + 1) * P, :], probs[:, x1_tile(m), :]).then_inc(y_stored[m], 16)

                if isinstance(b, int) and b == 0:
                    sp.wait_ge(slot_full, len(pre))
                else:
                    sp.wait_ge(slot_full, b * ring.per_full + (ring.full(0, ("QK", HEADS, 1)) - ring.per_full))
                load_qk(2)
                if not last:
                    for i in range(2):
                        sp.wait_ge(norm.lo_done, b * KT + (KT - 1 + i))
                        load_x(b + 1, i)
                sp.wait_ge(slot_full, r.full(b, ("V", JT // 2 - 1)))
                for c in range(4):
                    load_vo(c, S_O, o_loaded)
                if not last:
                    for i in range(2, KT):
                        sp.wait_ge(norm.tiles, b * KT + (KT + i - 1))
                        load_x(b + 1, i)
                sp.wait_ge(slot_full, r.full(b, ("QK", 1, 1)))
                load_qk(3)
                if not last:
                    for i in range(2):
                        sp.wait_ge(norm.tiles, b * KT + (2 * KT - 1 + i))
                        load_x(b + 1, i)
                for h in range(4, HEADS if last else HEADS + 2):
                    sp.wait_ge(slot_full, r.full(b, ("QK", h - 2, 1)))
                    load_qk(h)
                if not last:
                    for i in range(2, KT):
                        sp.wait_ge(norm.lo_done, b * KT + (KT + i - 1))
                        load_x(b + 1, i)
                for m in range(KT):
                    sp.wait_ge(turn_full, b * (TURNS * U) + TURNS * (U - (2 if m < 2 else 0)))
                    sp.dma_start(probs[:, x1_tile(m), :], x[b, m * P:(m + 1) * P, :]).then_inc(r_loaded[m], 16)
                for m in range(KT):
                    if not last:
                        sp.wait_ge(slot_full, r.full(b, ("OUT", m)))
                        load_vo(m, S_V, v_loaded)
                    if m >= 1:
                        store(m - 1)
                store(KT - 1)

            over_batches(sp, body)
            for m in range(KT):
                sp.wait_ge(y_stored[m], 16 * B)

        @block.tensor
        def _(pe):
            def project_qk(r, b, h, half, kts):
                item = ("QK", h, half)
                cols = slice(half * HALF, (half + 1) * HALF)
                at = r.slot(item) if h else half
                for kt in kts:
                    if kt == 0 and half == 0:
                        pe.wait_ge(qk_loaded[h % 2], b * (8 * HEADS) + 16 * (h // 2 + 1))
                    if kt == 0 and h == 0:
                        pe.wait_ge(dve_released, half + 1)
                    if kt == 0 and h:
                        r.wait_free(pe, act_released, dve_released, b, item)
                    if h % HEADS == 0 and half == 0:
                        pe.wait_ge(norm.lo_done, (b + (h // HEADS)) * KT + (kt + 1))
                    mm = three(nc, slot[:, at, 0:HALF], w_qk[:, h % 2, 0, kt], w_qk[:, h % 2, 1, kt],
                               n_hi[:, kt, cols], n_lo[:, kt, cols], kt == 0, kt == KT - 1)
                if kt == KT - 1:
                    mm.then_inc(slot_full, 1)

            norm.mean_matmul(pe, 0, slot[:, 0, 0:KT]).then_inc(slot_full, 1)
            norm.var_matmul(pe, 0, slot[:, 1, 0:KT]).then_inc(slot_full, 1)
            pe.wait_ge(zeroed, 1)
            for half in range(2):
                project_qk(ring, 0, 0, half, range(KT))

            def body(b, last):
                r = ring_last if last else ring

                def project_v(i):
                    r.wait_free(pe, act_released, dve_released, b, ("V", i))
                    for kt in range(KT):
                        if i == 0:
                            pe.wait_ge(v_loaded[kt], b * 16 + 16)
                        for jj in range(2):
                            js = slice((2 * i + jj) * P, (2 * i + jj + 1) * P)
                            mm = three(nc, slot[:, r.slot(("V", i)), jj * HALF:(jj + 1) * HALF],
                                       n_hi[:, kt, js], n_lo[:, kt, js],
                                       w_vo[:, kt, 0, :], w_vo[:, kt, 1, :], kt == 0, kt == KT - 1)
                    mm.then_inc(slot_full, 1)

                def scores(u, t):
                    h = u // UNITS
                    at = (u % UNITS) * QU + t * P
                    r.wait_free(pe, act_released, dve_released, b, ("S", u, t))
                    if u == 0 and t == 0:
                        pe.wait_ge(act_released, r.act_before(b))
                        pe.wait_ge(dve_released, r.dve_before(b))
                    elif u % UNITS == 0 and t == 0:
                        pe.wait_ge(act_released, r.act_done(b, ("QK", h, 1)))
                        pe.wait_ge(dve_released, r.dve_done(b, ("QK", h, 1)))
                    if u % UNITS == 0 and t == 0:
                        pe.wait_ge(k_hi_twice, b * (2 * HEADS) + (2 * h + 2))
                    for half in range(2):
                        cols = slice(half * HALF, (half + 1) * HALF)
                        out = slot[:, r.slot(("S", u, t)), cols]
                        nc.tensor.matmul(out, q_st[:, h % 2, at:at + P], k_hi[:, h % 2, cols], start=True, stop=False)
                        mm = nc.tensor.matmul(out, q_st[:, h % 2, at:at + P], k_lo[:, h % 2, cols],
                                              start=False, stop=True)
                    mm.then_inc(slot_full, 1)

                def turn_item(u, a):
                    if a == 0:
                        pe.wait_ge(probs_ready, b * (TILES * U) + TILES * (u + 1))
                    wait(pe, turn_lo, b * (TURNS * U) + (TURNS * u + a - 1))
                    for jj in range(2):
                        for t in range(TILES):
                            mm = nc.tensor.transpose(turn[:, a % 2, jj, t * P:(t + 1) * P],
                                                     probs[:, (TILES * u + t) % TILES_KEPT,
                                                           (2 * a + jj) * P:(2 * a + jj + 1) * P], ident)
                    mm.then_inc(turn_full, 1)

                def mix_item(k):
                    u, a = k // TURNS, k % TURNS
                    pe.wait_ge(turn_lo, b * (TURNS * U) + (k + 1))
                    if k == 0:
                        pe.wait_ge(dve_released, r.dve_done(b, ("V", JT // 2 - 1)))
                    if a == 0:
                        wait(pe, mix_added, b * U + (u - 1))
                    for n, part in enumerate((pt_hi, pt_lo)):
                        for jj in range(2):
                            mm = nc.tensor.matmul(mix[:, u % 2, 0:QU], vt[:, 2 * a + jj, u // UNITS, :], part[:, a, jj, :],
                                                  start=(n == 0 and a + jj == 0),
                                                  stop=(n == 1 and a == TURNS - 1 and jj == 1))
                    mm.then_inc(mixed, 1)

                def project_out(m, pairs):
                    if 0 in pairs:
                        r.wait_free(pe, act_released, dve_released, b, ("OUT", m))
                        pe.wait_ge(o_loaded[m], b * 16 + 16)
                    w = w_vo[:, m].rearrange("p a (k m) -> p a k m", k=KT)
                    for kt in pairs:
                        if m == 0:
                            pe.wait_ge(pair_lo, b * PAIRS + (kt + 1))
                        for half in range(2):
                            cols = slice(half * HALF, (half + 1) * HALF)
                            mm = three(nc, slot[:, r.slot(("OUT", m)), cols], w[:, 0, kt], w[:, 1, kt],
                                       o_hi[:, kt, cols], o_lo[:, kt, cols], kt == 0, kt == PAIRS - 1)
                    if PAIRS - 1 in pairs:
                        mm.then_inc(slot_full, 1)

                def group_stats(s, product):
                    r.wait_free(pe, act_released, dve_released, b, ("GN", s))
                    product(pe, b + 1, slot[:, r.slot(("GN", s)), 0:KT]).then_inc(slot_full, 1)

                for s in range(U + LAG):
                    part = projected_at(s)
                    for a in range(TURNS):
                        if s >= LAG:
                            turn_item(s - LAG, a)
                            k = TURNS * (s - LAG) + a - BEHIND
                            if k >= 0:
                                mix_item(k)
                        if s >= U:
                            if not last:
                                project_qk(r, b, *part, [a])
                        elif a == 0 or a == (3 if part else 2):
                            scores(s, int(a > 0))
                        elif part and a < 3:
                            project_qk(r, b, *part, [2 * a - 2, 2 * a - 1])
                    if s < LAG:
                        project_v(2 * s)
                        project_v(2 * s + 1)
                    if not last and s == MEANS_AT:
                        group_stats(s, norm.mean_matmul)
                    if not last and s == VARS_AT:
                        group_stats(s, norm.var_matmul)
                for k in range(TURNS * U - BEHIND, TURNS * U):
                    mix_item(k)
                for m in range(2):
                    project_out(m, range(PAIRS - 1))
                for m in range(2):
                    project_out(m, [PAIRS - 1])
                for m in range(2, KT):
                    project_out(m, range(PAIRS))

            over_batches(pe, body)

        @block.scalar
        def _(act):
            for ct in range(KT):
                act.wait_ge(x_loaded[ct % 2], 16 * (2 + ct // 2 + 1))
                norm.tile_hi(act, 0, ct, x_in[:, ct % 2], n_hi[:, ct])

            def qk_hi(r, b, h, half):
                at = r.slot(("QK", h, half)) if h else half
                act.wait_ge(slot_full, r.full(b, ("QK", h, half)) if h else 3 + half)
                cols = slice(half * HALF, (half + 1) * HALF)
                nc.scalar.activation(q_st[0:HD, h % 2, cols], slot[0:HD, at, 0:HALF], ACT.Copy, scale=SCALE
                                     ).then_inc(q_hi_ready, 1)
                nc.scalar.activation(k_hi[HD:P, h % 2, cols], slot[HD:P, at, 0:HALF], ACT.Copy).then_inc(act_released, 1)

            def k_hi_again(r, b, h, half):
                cols = slice(half * HALF, (half + 1) * HALF)
                act.wait_ge(act_released, r.act_done(b, ("QK", h, half)) if h else 1 + half)
                nc.scalar.activation(k_hi[0:HD, h % 2, cols], f(k_hi[HD:P, h % 2, cols]), ACT.Copy).then_inc(k_hi_twice, 1)

            for half in range(2):
                qk_hi(ring, 0, 0, half)
                k_hi_again(ring, 0, 0, half)

            def body(b, last):
                r = ring_last if last else ring

                def v_hi(i):
                    act.wait_ge(slot_full, r.full(b, ("V", i)))
                    for jj in range(2):
                        src = slot[:, r.slot(("V", i)), jj * HALF:(jj + 1) * HALF].rearrange("p (g e d) -> p g e d", g=PAIRS, e=2)
                        dst = vt[:, 2 * i + jj].rearrange("p (g e) (w d) -> p g (e w) d", e=2, w=2)[:, :, 0:4:3]
                        done = nc.scalar.activation(dst, src, ACT.Copy)
                    done.then_inc(act_released, 1)

                def exponentials(u, t):
                    i = TILES * u + t
                    act.wait_ge(max_ready, b * (TILES * U) + (i + 1))
                    wait(act, turn_full, b * (TURNS * U) + TURNS * (u - 2))
                    k = i % TILES_KEPT
                    for m in range(KT):
                        if i == x1_tile(m):
                            wait(act, y_stored[m], b * 16)
                    nc.scalar.activation(probs[:, k, :], slot[:, r.slot(("S", u, t)), :], ACT.Exp,
                                         bias=neg_max[:, k:k + 1], accum_out=total[:, k:k + 1]).then_inc(act_released, 1)

                def turn_his(u, a):
                    act.wait_ge(turn_full, b * (TURNS * U) + (TURNS * u + a + 1))
                    wait(act, mixed, b * (TURNS * U) + (TURNS * (u - 1) + a + 1))
                    nc.scalar.activation(pt_hi[:, a], turn[:, a % 2], ACT.Copy).then_inc(turn_hi, 1)

                def sides(u):
                    odd = (u // UNITS) % 2
                    to, frm = (slice(HD, P), slice(0, HD)) if odd else (slice(0, HD), slice(HD, P))
                    act.wait_ge(mixed, b * (TURNS * U) + TURNS * (u + 1))
                    wait(act, mix_added, b * U + (u - 1))
                    nc.scalar.activation(side[to, u % 2, :], mix[frm, u % 2, 0:QU], ACT.Copy).then_inc(side_ready, 1)

                def pair_his(u):
                    g = u // (2 * UNITS)
                    act.wait_ge(mix_added, b * U + (u + 1))
                    nc.scalar.activation(o_hi[:, g, :], o_mid[:, g % 2], ACT.Copy).then_inc(pair_hi, 1)

                for s in range(U + LAG + 2):
                    turned = LAG <= s < U + LAG
                    part = projected_at(s) if s < U + (0 if last else LAG) else None
                    if turned:
                        turn_his(s - LAG, 0)
                    if LAG < s <= U:
                        exponentials(s - 1, 1)
                    if turned:
                        turn_his(s - LAG, 1)
                    if s < U and part:
                        exponentials(s, 0)
                    if turned:
                        turn_his(s - LAG, 2)
                    if 0 <= s - LAG - 1 < U:
                        sides(s - LAG - 1)
                    if s < U and not part:
                        exponentials(s, 0)
                    if part:
                        qk_hi(r, b, *part)
                    if turned:
                        turn_his(s - LAG, 3)
                    if part:
                        k_hi_again(r, b, *part)
                    if s < LAG:
                        exponentials(s, 1)
                        v_hi(2 * s)
                        v_hi(2 * s + 1)
                    if s >= LAG + 1 and (s - LAG - 1) % (2 * UNITS) == 2 * UNITS - 1:
                        pair_his(s - LAG - 1)
                    if not last and NORM_AT <= s < NORM_AT + KT:
                        ct = s - NORM_AT
                        act.wait_ge(x_loaded[ct % 2], x_count(b, KT + ct))
                        norm.tile_hi(act, b + 1, ct, x_in[:, ct % 2], n_hi[:, ct])

            over_batches(act, body)

        @block.vector
        def _(dve):
            nc.vector.memset(f(k_lo[HD:P, :, :]), 0.0).then_inc(zeroed, 1)
            for ct in range(KT):
                dve.wait_ge(x_loaded[ct % 2], 16 * (ct // 2 + 1))
                norm.tile_stats(dve, 0, ct, x_in[:, ct % 2])
            dve.wait_ge(slot_full, 1)
            norm.after_means(dve, 0, slot[:, 0, 0:KT], dve_released, 1)
            dve.wait_ge(slot_full, 2)
            norm.after_vars(slot[:, 1, 0:KT], dve_released)
            norm.coefficients(dve, 0)
            for ct in range(KT):
                norm.tile_mid(dve, 0, ct, x_in[:, ct % 2])

            def qk_lo(r, b, h, half):
                at = r.slot(("QK", h, half)) if h else half
                dve.wait_ge(q_hi_ready, b * (2 * HEADS) + (2 * h + half + 1))
                s = slot[:, at, 0:HALF]
                cols = slice(half * HALF, (half + 1) * HALF)
                nc.vector.scalar_tensor_tensor(q_st[HD:P, h % 2, cols], s[0:HD], SCALE, f(q_st[0:HD, h % 2, cols]),
                                               ALU.mult, ALU.subtract)
                dve.wait_ge(act_released, r.act_done(b, ("QK", h, half)) if h else 1 + half)
                nc.vector.tensor_tensor(k_lo[0:HD, h % 2, cols], s[HD:P], f(k_hi[HD:P, h % 2, cols]), ALU.subtract
                                        ).then_inc(dve_released, 1)

            for half in range(2):
                qk_lo(ring, 0, 0, half)

            def body(b, last):
                r = ring_last if last else ring

                def v_lo(i):
                    dve.wait_ge(act_released, r.act_done(b, ("V", i)))
                    for jj in range(2):
                        src = slot[:, r.slot(("V", i)), jj * HALF:(jj + 1) * HALF].rearrange("p (g e d) -> p g e d", g=PAIRS, e=2)
                        heads = vt[:, 2 * i + jj].rearrange("p (g e) (w d) -> p g (e w) d", e=2, w=2)
                        done = nc.vector.tensor_tensor(heads[:, :, 1:3], src, f(heads[:, :, 0:4:3]), ALU.subtract)
                    done.then_inc(dve_released, 1)

                def maxima(u, t):
                    k = (TILES * u + t) % TILES_KEPT
                    dve.wait_ge(slot_full, r.full(b, ("S", u, t)))
                    nc.vector.tensor_reduce(neg_max[:, k:k + 1], slot[:, r.slot(("S", u, t)), :], AX_X, ALU.max,
                                            negate=True).then_inc(max_ready, 1)

                def inverses(u, t):
                    k = (TILES * u + t) % TILES_KEPT
                    dve.wait_ge(act_released, r.act_done(b, ("S", u, t)))
                    nc.vector.reciprocal(inverse[:, k:k + 1], total[:, k:k + 1]).then_inc(inverse_ready, 1)

                def turn_los(u, a):
                    dve.wait_ge(turn_hi, b * (TURNS * U) + (TURNS * u + a + 1))
                    nc.vector.tensor_tensor(pt_lo[:, a], turn[:, a % 2], f(pt_hi[:, a]), ALU.subtract).then_inc(turn_lo, 1)

                def add_sides(u):
                    own = slice(HD, P) if (u // UNITS) % 2 else slice(0, HD)
                    at = (u % UNITS) * QU
                    dve.wait_ge(side_ready, b * U + (u + 1))
                    g = u // (2 * UNITS)
                    if u % (2 * UNITS) == 0:
                        wait(dve, pair_lo, b * PAIRS + (g - 1))
                    nc.vector.tensor_tensor(o_mid[own, g % 2, at:at + QU], mix[own, u % 2, 0:QU], side[own, u % 2, :], ALU.add
                                            ).then_inc(mix_added, 1)

                def residual(m):
                    dve.wait_ge(slot_full, r.full(b, ("OUT", m)))
                    dve.wait_ge(r_loaded[m], b * 16 + 16)
                    y = probs[:, x1_tile(m), :]
                    nc.vector.scalar_tensor_tensor(y, slot[:, r.slot(("OUT", m)), :], vecs[:, V_OB, m:m + 1], y,
                                                   ALU.add, ALU.add).then_inc(dve_released, 1)

                for s in range(U + LAG + 2):
                    turned = LAG <= s < U + LAG
                    part = projected_at(s) if s < U + (0 if last else LAG) else None
                    if turned:
                        turn_los(s - LAG, 0)
                    if LAG < s <= U:
                        inverses(s - 1, 1)
                    if s < U:
                        maxima(s, 0)
                    if turned:
                        turn_los(s - LAG, 1)
                        if s < U and part:
                            inverses(s, 0)
                        turn_los(s - LAG, 2)
                    if 0 <= s - LAG - 1 < U:
                        add_sides(s - LAG - 1)
                    if s < U and not (part and turned):
                        inverses(s, 0)
                    if LAG <= s < U and not part:
                        maxima(s, 1)
                    if part:
                        qk_lo(r, b, *part)
                    if turned:
                        turn_los(s - LAG, 3)
                    if LAG <= s < U and part:
                        maxima(s, 1)
                    if s < LAG:
                        maxima(s, 1)
                        inverses(s, 1)
                        v_lo(2 * s)
                        v_lo(2 * s + 1)
                    if last:
                        continue
                    if STATS_AT <= s < STATS_AT + KT:
                        ct = s - STATS_AT
                        dve.wait_ge(x_loaded[ct % 2], x_count(b, ct))
                        norm.tile_stats(dve, b + 1, ct, x_in[:, ct % 2])
                    if s == MEANS_AT:
                        dve.wait_ge(slot_full, r.full(b, ("GN", s)))
                        norm.after_means(dve, b + 1, slot[:, r.slot(("GN", s)), 0:KT], dve_released,
                                         r.dve_done(b, ("GN", s)))
                    if s == VARS_AT:
                        dve.wait_ge(slot_full, r.full(b, ("GN", s)))
                        norm.after_vars(slot[:, r.slot(("GN", s)), 0:KT], dve_released)
                    if s == COEF_AT:
                        norm.coefficients(dve, b + 1)
                    if NORM_AT <= s < NORM_AT + KT:
                        norm.tile_mid(dve, b + 1, s - NORM_AT, x_in[:, (s - NORM_AT) % 2])
                for m in range(KT):
                    residual(m)

            over_batches(dve, body)

        @block.gpsimd
        def _(pool):
            norm.power(pool, dve_released, 2)
            for ct in range(KT):
                norm.tile_lo(pool, 0, ct, x_in[:, ct % 2], n_hi[:, ct], n_lo[:, ct])

            def body(b, last):
                r = ring_last if last else ring

                def normalise(u, t):
                    k = (TILES * u + t) % TILES_KEPT
                    wait_apart(pool, inverse_ready, b * (TILES * U) + (TILES * u + t + 1), scale_passed)
                    nc.gpsimd.tensor_scalar(probs[:, k, :], probs[:, k, :], inverse[:, k:k + 1], 1.0,
                                            ALU.mult, ALU.mult).then_inc(probs_ready, 1)

                def pair_los(u):
                    g = u // (2 * UNITS)
                    pool.wait_ge(pair_hi, b * PAIRS + (g + 1))
                    nc.gpsimd.tensor_tensor(o_lo[:, g, :], o_mid[:, g % 2], f(o_hi[:, g, :]), ALU.subtract
                                            ).then_inc(pair_lo, 1)

                for s in range(U + LAG + 2):
                    if LAG < s <= U:
                        normalise(s - 1, 1)
                    if s < U:
                        normalise(s, 0)
                    if s < LAG:
                        normalise(s, 1)
                    if s >= LAG + 2 and (s - LAG - 2) % (2 * UNITS) == 2 * UNITS - 1:
                        pair_los(s - LAG - 2)
                    if not last and s == VARS_AT:
                        norm.power(pool, dve_released, r.dve_done(b, ("GN", s)))
                    if not last and NORM_AT <= s < NORM_AT + KT:
                        ct = s - NORM_AT
                        norm.tile_lo(pool, b + 1, ct, x_in[:, ct % 2], n_hi[:, ct], n_lo[:, ct])

            over_batches(pool, body)


def attend_single(nc, x1, out, scratch, vecs, b2, tables):
    with ExitStack() as ctx:
        def sb(name, shape, dt=F32):
            return ctx.enter_context(nc.sbuf_tensor(name, shape, dt))

        def sem(name):
            return ctx.enter_context(nc.semaphore(name))

        ident = tables[:, 0:P]
        norm = Norm(nc, "gn1", sb, sem, EPS1, vecs[:, V_GS, :], vecs[:, V_GB, :], tables[:, P:2 * P],
                    tables[:, 2 * P:2 * P + KT])
        w_q = sb("w_q", [P, KT, 2, HALF], F32R)
        w_k = sb("w_k", [P, KT, 2, HALF], F32R)
        w_m = sb("w_m", [P, KT, 2, HALF], F32R)
        n_hi = sb("n1_hi", [P, KT, N], F32R)
        n_lo = sb("n1_lo", [P, KT, N], F32R)
        k_hi = sb("k1_hi", [P, KT, N], F32R)
        k_lo = sb("k1_lo", [P, KT, N], F32R)
        v_hi = sb("v1_hi", [P, JT, C], F32R)
        v_lo = sb("v1_lo", [P, JT, C], F32R)
        q_hi = sb("q1_hi", [P, 2, KT, QU], F32R)
        q_lo = sb("q1_lo", [P, 2, KT, QU], F32R)
        probs = sb("probs1", [P, PROBS, N])
        pt_hi = sb("pt1_hi", [P, JT, QU], F32R)
        pt_lo = sb("pt1_lo", [P, JT, QU], F32R)
        x_in = sb("x1_in", [P, 2, N])
        neg_raw = sb("neg_raw", [P, PROBS])
        neg_max = sb("neg_max1", [P, PROBS])
        total = sb("total1", [P, PROBS])
        inverse = sb("inverse1", [P, PROBS])
        slot = ctx.enter_context(nc.psum_tensor("slot1", [P, 2, 2 * HALF], F32))
        turn = ctx.enter_context(nc.psum_tensor("turn1", [P, 2, 2, QU], F32))
        mix = ctx.enter_context(nc.psum_tensor("mix1", [P, 2, HALF], F32))

        x_loaded = [sem("x1_loaded0"), sem("x1_loaded1")]
        w_loaded = {k: sem(f"w1_loaded_{k}") for k in "qkm"}
        y_stored = [sem("y1_stored0"), sem("y1_stored1")]
        slot_full = sem("slot1_full")
        act_released = sem("act1_released")
        dve_released = sem("dve1_released")
        scale_passed = sem("scale1_passed")
        raw_ready = sem("raw_ready")
        max_ready = sem("max1_ready")
        inverse_ready = sem("inverse1_ready")
        probs_ready = sem("probs1_ready")
        turn_full = sem("turn1_full")
        turn_hi = sem("turn1_hi")
        turn_lo = sem("turn1_lo")
        mix_full = sem("mix1_full")
        mix_added = sem("mix1_added")
        U = UNITS
        MEANS_AT, VARS_AT, COEF_AT, NORM_AT = 0, 1, 2, 3
        X_STATS, X_NORM = 0, 6

        def order(last):
            items = [("K", m) for m in range(KT)] + [("V", i) for i in range(JT // 2)] + [("Q", 0)]
            for s in range(U):
                items += [("S", s, 0), ("S", s, 1)]
                if s + 1 < U:
                    items.append(("Q", s + 1))
                if not last and s in (MEANS_AT, VARS_AT):
                    items.append(("GN", s))
            return items

        pre = [("GN", "means"), ("GN", "vars")]
        ring = Slots(pre, order(False), ("K", "V", "Q", "S"), ("K", "V", "Q", "GN"))
        ring_last = Slots(pre, order(True), ring.act_kinds, ring.dve_kinds, ring)

        def x_count(b, k):
            return b * (8 * 3 * KT) + 16 * (KT + k // 2 + 1)

        def residual_load(last, u):
            return u if last else (4, 5, 10, 11)[u]

        block = ctx.enter_context(nc.Block())

        @block.sync
        def _(sp):
            def load_x(b, i):
                sp.dma_start(x_in[:, i % 2], x1[b, i * P:(i + 1) * P, :]).then_inc(x_loaded[i % 2], 16)

            for i in range(KT):
                if i >= 2:
                    sp.wait_ge(norm.tiles, i - 1)
                load_x(0, i)
            for w, k, chunk in ((w_k, "k", S_K1), (w_m, "m", S_M1), (w_q, "q", S_Q1)):
                sp.dma_start(f(w[:]), scratch[:, chunk:chunk + KT]).then_inc(w_loaded[k], 16)
            for i in range(KT):
                if i < 2:
                    sp.wait_ge(norm.tiles, KT - 1 + i)
                else:
                    sp.wait_ge(norm.lo_done, i - 1)
                load_x(0, i)

            def body(b, last):
                def residual(u):
                    sp.dma_start(x_in[:, u % 2].rearrange("p (k n) -> p k n", k=KT),
                                 x1[b, :, u * QU:(u + 1) * QU].rearrange("(k p) n -> p k n", p=P)
                                 ).then_inc(x_loaded[u % 2], 16)

                def store(u):
                    sp.wait_ge(mix_added, b * (KT * U) + KT * (u + 1))
                    sp.dma_start(out[b, :, u * QU:(u + 1) * QU].rearrange("(k p) n -> p k n", p=P),
                                 x_in[:, u % 2].rearrange("p (k n) -> p k n", k=KT)).then_inc(y_stored[u % 2], 16)

                if last:
                    for u in range(U):
                        wait(sp, y_stored[u % 2], b * 32 + 16 * (u // 2))
                        residual(u)
                        if u >= 1:
                            store(u - 1)
                    store(U - 1)
                    return
                for i in range(KT):
                    if i >= 2:
                        sp.wait_ge(norm.tiles, b * KT + (KT + i - 1))
                    elif isinstance(b, int):
                        sp.wait_ge(norm.lo_done, KT - 1 + i)
                    else:
                        sp.wait_ge(y_stored[i], b * 32)
                    load_x(b + 1, i)
                for u in range(2):
                    sp.wait_ge(norm.tiles, b * KT + (2 * KT - 1 + u))
                    residual(u)
                for u in range(2):
                    store(u)
                for i in range(KT):
                    if i < 2:
                        sp.wait_ge(y_stored[i], b * 32 + 16)
                    else:
                        sp.wait_ge(norm.lo_done, b * KT + (KT + i - 1))
                    load_x(b + 1, i)
                for u in (2, 3):
                    sp.wait_ge(norm.lo_done, b * KT + (KT + u + 1))
                    residual(u)
                for u in (2, 3):
                    store(u)

            over_batches(sp, body)
            for k in range(2):
                sp.wait_ge(y_stored[k], 32 * B)

        @block.tensor
        def _(pe):
            norm.mean_matmul(pe, 0, slot[:, 0, 0:KT]).then_inc(slot_full, 1)
            norm.var_matmul(pe, 0, slot[:, 1, 0:KT]).then_inc(slot_full, 1)
            for k in "kmq":
                pe.wait_ge(w_loaded[k], 16)

            def body(b, last):
                r = ring_last if last else ring

                def project_k(m):
                    r.wait_free(pe, act_released, dve_released, b, ("K", m))
                    for half in range(2):
                        cols = slice(half * HALF, (half + 1) * HALF)
                        for kt in range(KT):
                            if m == 0 and half == 0:
                                pe.wait_ge(norm.lo_done, b * KT + (kt + 1))
                            ms = slice(m * P, (m + 1) * P)
                            mm = three(nc, slot[:, r.slot(("K", m)), cols], w_k[:, kt, 0, ms], w_k[:, kt, 1, ms],
                                       n_hi[:, kt, cols], n_lo[:, kt, cols], kt == 0, kt == KT - 1)
                    mm.then_inc(slot_full, 1)

                def project_v(i):
                    r.wait_free(pe, act_released, dve_released, b, ("V", i))
                    for jj in range(2):
                        js = slice((2 * i + jj) * P, (2 * i + jj + 1) * P)
                        for kt in range(KT):
                            mm = three(nc, slot[:, r.slot(("V", i)), jj * HALF:(jj + 1) * HALF],
                                       n_hi[:, kt, js], n_lo[:, kt, js], w_m[:, kt, 0, :], w_m[:, kt, 1, :],
                                       kt == 0, kt == KT - 1)
                    mm.then_inc(slot_full, 1)

                def project_q(u):
                    r.wait_free(pe, act_released, dve_released, b, ("Q", u))
                    cols = slice(u * QU, (u + 1) * QU)
                    for m in range(KT):
                        for kt in range(KT):
                            ms = slice(m * P, (m + 1) * P)
                            mm = three(nc, slot[:, r.slot(("Q", u)), m * QU:(m + 1) * QU],
                                       w_q[:, kt, 0, ms], w_q[:, kt, 1, ms],
                                       n_hi[:, kt, cols], n_lo[:, kt, cols], kt == 0, kt == KT - 1)
                    mm.then_inc(slot_full, 1)

                def scores(u, t):
                    r.wait_free(pe, act_released, dve_released, b, ("S", u, t))
                    if t == 0:
                        pe.wait_ge(act_released, r.act_done(b, ("Q", u)))
                        pe.wait_ge(dve_released, r.dve_done(b, ("Q", u)))
                    qs = slice(t * P, (t + 1) * P)
                    for half in range(2):
                        cols = slice(half * HALF, (half + 1) * HALF)
                        for kt in range(KT):
                            mm = three(nc, slot[:, r.slot(("S", u, t)), cols], q_hi[:, u % 2, kt, qs], q_lo[:, u % 2, kt, qs],
                                       k_hi[:, kt, cols], k_lo[:, kt, cols], kt == 0, kt == KT - 1)
                    mm.then_inc(slot_full, 1)

                def turns(u):
                    pe.wait_ge(probs_ready, b * (TILES * U) + TILES * (u + 1))
                    for a in range(TURNS):
                        wait(pe, turn_lo, b * (TURNS * U) + (TURNS * u + a - 1))
                        for jj in range(2):
                            for t in range(TILES):
                                mm = nc.tensor.transpose(turn[:, a % 2, jj, t * P:(t + 1) * P],
                                                         probs[:, (TILES * u + t) % PROBS,
                                                               (2 * a + jj) * P:(2 * a + jj + 1) * P], ident)
                        mm.then_inc(turn_full, 1)

                def mixes(u):
                    pe.wait_ge(turn_lo, b * (TURNS * U) + TURNS * (u + 1))
                    for ot in range(KT):
                        wait(pe, mix_added, b * (KT * U) + (KT * u + ot - 1))
                        os = slice(ot * P, (ot + 1) * P)
                        for j in range(JT):
                            mm = three(nc, mix[:, ot % 2, 0:QU], v_hi[:, j, os], v_lo[:, j, os], pt_hi[:, j, :], pt_lo[:, j, :],
                                       j == 0, j == JT - 1)
                        mm.then_inc(mix_full, 1)

                def group_stats(s, product):
                    r.wait_free(pe, act_released, dve_released, b, ("GN", s))
                    product(pe, b + 1, slot[:, r.slot(("GN", s)), 0:KT]).then_inc(slot_full, 1)

                for m in range(KT):
                    project_k(m)
                for i in range(JT // 2):
                    project_v(i)
                project_q(0)
                for s in range(U + 1):
                    if s < U:
                        scores(s, 0)
                    if s >= 1:
                        turns(s - 1)
                    if s < U:
                        scores(s, 1)
                    if s + 1 < U:
                        project_q(s + 1)
                    if not last and s == MEANS_AT:
                        group_stats(s, norm.mean_matmul)
                    if not last and s == VARS_AT:
                        group_stats(s, norm.var_matmul)
                    if s >= 1:
                        mixes(s - 1)

            over_batches(pe, body)

        @block.scalar
        def _(act):
            for ct in range(KT):
                act.wait_ge(x_loaded[ct % 2], 16 * (2 + ct // 2 + 1))
                norm.tile_hi(act, 0, ct, x_in[:, ct % 2], n_hi[:, ct])

            def body(b, last):
                r = ring_last if last else ring

                def k_his(m):
                    act.wait_ge(slot_full, r.full(b, ("K", m)))
                    nc.scalar.activation(k_hi[:, m], slot[:, r.slot(("K", m)), :], ACT.Identity,
                                         bias=vecs[:, V_BK, m:m + 1]).then_inc(act_released, 1)

                def v_his(i):
                    act.wait_ge(slot_full, r.full(b, ("V", i)))
                    nc.scalar.activation(v_hi[:, 2 * i:2 * i + 2].rearrange("p j c -> p (j c)"),
                                         slot[:, r.slot(("V", i)), :], ACT.Copy).then_inc(act_released, 1)

                def q_his(u):
                    act.wait_ge(slot_full, r.full(b, ("Q", u)))
                    for m in range(KT):
                        done = nc.scalar.activation(q_hi[:, u % 2, m], slot[:, r.slot(("Q", u)), m * QU:(m + 1) * QU],
                                                    ACT.Identity, bias=vecs[:, V_BQ, m:m + 1])
                    done.then_inc(act_released, 1)

                def exponentials(u, t):
                    k = (TILES * u + t) % PROBS
                    act.wait_ge(max_ready, b * (TILES * U) + (TILES * u + t + 1))
                    wait(act, turn_full, b * (TURNS * U) + TURNS * (u - 1))
                    nc.scalar.activation(probs[:, k, :], slot[:, r.slot(("S", u, t)), :], ACT.Exp, scale=SCALE,
                                         bias=neg_max[:, k:k + 1], accum_out=total[:, k:k + 1]).then_inc(act_released, 1)

                def turn_his(u):
                    for a in range(TURNS):
                        act.wait_ge(turn_full, b * (TURNS * U) + (TURNS * u + a + 1))
                        if a == 0:
                            wait(act, mix_full, b * (KT * U) + KT * u)
                        nc.scalar.activation(pt_hi[:, 2 * a:2 * a + 2, :], turn[:, a % 2], ACT.Copy).then_inc(turn_hi, 1)

                for m in range(KT):
                    k_his(m)
                for i in range(JT // 2):
                    v_his(i)
                q_his(0)
                for s in range(U + 1):
                    if s < U:
                        exponentials(s, 0)
                    if s >= 1:
                        turn_his(s - 1)
                    if s < U:
                        exponentials(s, 1)
                    if s + 1 < U:
                        q_his(s + 1)
                    if not last and s == NORM_AT:
                        for ct in range(KT):
                            act.wait_ge(x_loaded[ct % 2], x_count(b, X_NORM + ct))
                            norm.tile_hi(act, b + 1, ct, x_in[:, ct % 2], n_hi[:, ct])

            over_batches(act, body)

        @block.vector
        def _(dve):
            for ct in range(KT):
                dve.wait_ge(x_loaded[ct % 2], 16 * (ct // 2 + 1))
                norm.tile_stats(dve, 0, ct, x_in[:, ct % 2])
            dve.wait_ge(slot_full, 1)
            norm.after_means(dve, 0, slot[:, 0, 0:KT], dve_released, 1)
            dve.wait_ge(slot_full, 2)
            norm.after_vars(slot[:, 1, 0:KT], dve_released)
            norm.coefficients(dve, 0)
            for ct in range(KT):
                norm.tile_mid(dve, 0, ct, x_in[:, ct % 2])

            def body(b, last):
                r = ring_last if last else ring

                def k_los(m):
                    dve.wait_ge(act_released, r.act_done(b, ("K", m)))
                    nc.vector.scalar_tensor_tensor(k_lo[:, m], slot[:, r.slot(("K", m)), :], vecs[:, V_BK, m:m + 1],
                                                   f(k_hi[:, m]), ALU.add, ALU.subtract).then_inc(dve_released, 1)

                def v_los(i):
                    dve.wait_ge(act_released, r.act_done(b, ("V", i)))
                    nc.vector.tensor_tensor(v_lo[:, 2 * i:2 * i + 2].rearrange("p j c -> p (j c)"),
                                            slot[:, r.slot(("V", i)), :],
                                            f(v_hi[:, 2 * i:2 * i + 2].rearrange("p j c -> p (j c)")),
                                            ALU.subtract).then_inc(dve_released, 1)

                def q_los(u):
                    dve.wait_ge(act_released, r.act_done(b, ("Q", u)))
                    for m in range(KT):
                        done = nc.vector.scalar_tensor_tensor(
                            q_lo[:, u % 2, m], slot[:, r.slot(("Q", u)), m * QU:(m + 1) * QU], vecs[:, V_BQ, m:m + 1],
                            f(q_hi[:, u % 2, m]), ALU.add, ALU.subtract)
                    done.then_inc(dve_released, 1)

                def maxima(u, t):
                    k = (TILES * u + t) % PROBS
                    n = b * (TILES * U) + (TILES * u + t + 1)
                    dve.wait_ge(slot_full, r.full(b, ("S", u, t)))
                    nc.vector.tensor_reduce(neg_raw[:, k:k + 1], slot[:, r.slot(("S", u, t)), :], AX_X, ALU.max,
                                            negate=True).then_inc(raw_ready, 1)
                    dve.wait_ge(raw_ready, n)
                    nc.vector.tensor_scalar(neg_max[:, k:k + 1], neg_raw[:, k:k + 1], SCALE, None, ALU.mult
                                            ).then_inc(max_ready, 1)

                def inverses(u, t):
                    k = (TILES * u + t) % PROBS
                    dve.wait_ge(act_released, r.act_done(b, ("S", u, t)))
                    nc.vector.reciprocal(inverse[:, k:k + 1], total[:, k:k + 1]).then_inc(inverse_ready, 1)

                def turn_los(u):
                    for a in range(TURNS):
                        dve.wait_ge(turn_hi, b * (TURNS * U) + (TURNS * u + a + 1))
                        nc.vector.tensor_tensor(pt_lo[:, 2 * a:2 * a + 2, :], turn[:, a % 2],
                                                f(pt_hi[:, 2 * a:2 * a + 2, :]), ALU.subtract).then_inc(turn_lo, 1)

                def finish(u):
                    dve.wait_ge(x_loaded[u % 2], x_count(b, residual_load(last, u)))
                    for ot in range(KT):
                        dve.wait_ge(mix_full, b * (KT * U) + (KT * u + ot + 1))
                        y = x_in[:, u % 2, ot * QU:(ot + 1) * QU]
                        nc.vector.scalar_tensor_tensor(y, mix[:, ot % 2, 0:QU], b2[:, ot:ot + 1], y, ALU.add, ALU.add
                                                       ).then_inc(mix_added, 1)

                for m in range(KT):
                    k_los(m)
                for i in range(JT // 2):
                    v_los(i)
                    if not last:
                        dve.wait_ge(x_loaded[i % 2], x_count(b, X_STATS + i))
                        norm.tile_stats(dve, b + 1, i, x_in[:, i % 2])
                q_los(0)
                for s in range(U + 1):
                    if s < U:
                        maxima(s, 0)
                        inverses(s, 0)
                    if s >= 1:
                        turn_los(s - 1)
                    if s < U:
                        maxima(s, 1)
                        inverses(s, 1)
                    if s + 1 < U:
                        q_los(s + 1)
                    if not last and s == MEANS_AT:
                        dve.wait_ge(slot_full, r.full(b, ("GN", s)))
                        norm.after_means(dve, b + 1, slot[:, r.slot(("GN", s)), 0:KT], dve_released,
                                         r.dve_done(b, ("GN", s)))
                    if not last and s == VARS_AT:
                        dve.wait_ge(slot_full, r.full(b, ("GN", s)))
                        norm.after_vars(slot[:, r.slot(("GN", s)), 0:KT], dve_released)
                    if not last and s == COEF_AT:
                        norm.coefficients(dve, b + 1)
                    if not last and s == NORM_AT:
                        for ct in range(KT):
                            norm.tile_mid(dve, b + 1, ct, x_in[:, ct % 2])
                    if s >= 1:
                        finish(s - 1)

            over_batches(dve, body)

        @block.gpsimd
        def _(pool):
            norm.power(pool, dve_released, 2)
            for ct in range(KT):
                norm.tile_lo(pool, 0, ct, x_in[:, ct % 2], n_hi[:, ct], n_lo[:, ct])

            def body(b, last):
                r = ring_last if last else ring
                for s in range(U):
                    for t in range(TILES):
                        k = (TILES * s + t) % PROBS
                        wait_apart(pool, inverse_ready, b * (TILES * U) + (TILES * s + t + 1), scale_passed)
                        nc.gpsimd.tensor_scalar(probs[:, k, :], probs[:, k, :], inverse[:, k:k + 1], 1.0,
                                                ALU.mult, ALU.mult).then_inc(probs_ready, 1)
                    if not last and s == VARS_AT:
                        norm.power(pool, dve_released, r.dve_done(b, ("GN", s)))
                    if not last and s == NORM_AT:
                        for ct in range(KT):
                            norm.tile_lo(pool, b + 1, ct, x_in[:, ct % 2], n_hi[:, ct], n_lo[:, ct])

            over_batches(pool, body)


def two_attentions(nc, x, w_in, v_in, t_in, out):
    x1 = nc.dram_tensor("x1", (B, C, N), F32, kind="Internal").ap()
    scratch = nc.dram_tensor("w_split_dram", (P, CHUNKS, 2, HALF), F32, kind="Internal").ap()
    with ExitStack() as ctx:
        vecs = ctx.enter_context(nc.sbuf_tensor("vecs", [P, 9, KT], F32))
        tables = ctx.enter_context(nc.sbuf_tensor("tables", [P, 2 * P + KT], F32))
        b2 = ctx.enter_context(nc.sbuf_tensor("b2", [P, KT], F32))
        small_in = ctx.enter_context(nc.semaphore("small_in"))
        with nc.Block() as block:
            @block.sync
            def _(sp):
                sp.dma_start(vecs[:], v_in).then_inc(small_in, 16)
                sp.dma_start(tables[:], t_in).then_inc(small_in, 16)
                sp.wait_ge(small_in, 32)
        split_weights(nc, w_in, scratch, vecs, b2)
        attend_heads(nc, x, x1, scratch, vecs, tables)
        attend_single(nc, x1, out, scratch, vecs, b2, tables)


def kernel(**inputs):
    import numpy as np
    import concourse.bacc as bacc
    from concourse.bass_utils import run_bass_kernel_spmd as run

    def host(name):
        return np.asarray(inputs[name])

    def contraction_first(wt):
        return wt.reshape(KT, P, -1).transpose(1, 0, 2)

    qkv = host("L0_conv_qkv_w").reshape(HEADS, 3, HD, C)
    w_qk = qkv[:, 0:2].reshape(HEADS, P, KT, P).transpose(3, 0, 2, 1).reshape(P, HEADS, HALF)
    w_v = contraction_first(qkv[:, 2].reshape(C, C).T)
    w_o = host("L0_conv_out_w").reshape(KT, P, KT, P).transpose(3, 0, 2, 1).reshape(P, KT, HALF)
    w_in = np.ascontiguousarray(np.concatenate([
        w_qk, w_v, w_o, contraction_first(host("L1_conv_wq").T), contraction_first(host("L1_conv_wk").T),
        contraction_first(host("L1_conv_wp").T), contraction_first(host("L1_conv_wv"))], axis=1))
    v_in = np.ascontiguousarray(np.stack([host(n).reshape(KT, P).T for n in (
        "L0_conv_gn_w", "L0_conv_gn_b", "L0_conv_out_b", "L1_conv_gn_scale", "L1_conv_gn_bias",
        "L1_conv_bq", "L1_conv_bk", "L1_conv_bv", "L1_conv_bp")], axis=1))
    size = C // GROUPS
    averager = np.kron(np.eye(P // size), np.full((size, size), 1.0 / size))
    t_in = np.concatenate([np.eye(P), averager, np.full((P, KT), -0.5)], axis=1).astype(np.float32)
    x = host("x").reshape(B, C, N)

    nc = bacc.Bacc("TRN2", target_bir_lowering=False, num_devices=1)
    arrays, args = {}, []
    for name, a in (("x", x), ("w_in", w_in), ("v_in", v_in), ("t_in", t_in)):
        arrays[name] = np.ascontiguousarray(a)
        args.append(nc.dram_tensor(name, a.shape, mybir.dt.from_np(a.dtype), kind="ExternalInput").ap())
    out = nc.dram_tensor("out", (B, C, N), F32, kind="ExternalOutput").ap()
    two_attentions(nc, *args, out)
    r = run(nc, [arrays], core_ids=[0])
    return r.results[0]["out"].reshape(B, C, 32, 32)
```

```python
from contextlib import ExitStack

import concourse.bass as bass
from concourse import mybir

ALU = mybir.AluOpType
ACT = mybir.ActivationFunctionType
F32 = mybir.dt.float32
F32R = mybir.dt.float32r
AX_X = mybir.AxisListType.X

P = 128
B, C, N = 8, 512, 1024
KT = C // P
JT = N // P
HEADS, HD = 8, 64
PAIRS = HEADS // 2
QU = 256
TILES = QU // P
UNITS = N // QU
HALF = 512
TURNS = JT // 2
PROBS = 4
SCALE = float(C) ** -0.5
EPS0, EPS1 = 1e-5, 1e-6
GROUPS = 32

V_GNW, V_GNB, V_OB, V_GS, V_GB, V_BQ, V_BK, V_BV, V_BP = range(9)
W_QK, W_V, W_O, W_Q1, W_K1, W_P1, W_V1 = 0, 8, 12, 16, 20, 24, 28
CHUNKS = W_Q1


def f(ap):
    return ap.bitcast(F32)


def wait(eng, sem, value):
    if isinstance(value, int) and value <= 0:
        return
    eng.wait_ge(sem, value)


def wait_apart(eng, sem, value, passed):
    eng.wait_ge(sem, value)
    eng.sem_inc(passed, 1)


class Slots:

    def __init__(self, pre, items, act_kinds, dve_kinds, whole=None):
        self.pre, self.items = pre, items
        self.act_kinds, self.dve_kinds = act_kinds, dve_kinds
        self.pos = {it: n for n, it in enumerate(items)}
        self.act = self.running(items, act_kinds)
        self.dve = self.running(items, dve_kinds)
        self.pre_act = self.running(pre, act_kinds)
        self.pre_dve = self.running(pre, dve_kinds)
        w = whole or self
        self.per_full, self.per_act, self.per_dve = len(w.items), w.act[-1], w.dve[-1]

    @staticmethod
    def running(items, kinds):
        counts = [0]
        for it in items:
            counts.append(counts[-1] + (it[0] in kinds))
        return counts

    def slot(self, it):
        return self.pos[it] % 2

    def full(self, b, it):
        return b * self.per_full + (len(self.pre) + self.pos[it] + 1)

    def act_done(self, b, it):
        return b * self.per_act + (self.pre_act[-1] + self.act[self.pos[it] + 1])

    def dve_done(self, b, it):
        return b * self.per_dve + (self.pre_dve[-1] + self.dve[self.pos[it] + 1])

    def act_before(self, b):
        return b * self.per_act + self.pre_act[-1]

    def dve_before(self, b):
        return b * self.per_dve + self.pre_dve[-1]

    def wait_free(self, eng, act_released, dve_released, b, it):
        n = self.pos[it] - 2
        if n < 0 and isinstance(b, int) and b == 0:
            kind = self.pre[n][0]
            n += len(self.pre)
            act, dve = self.pre_act[n + 1], self.pre_dve[n + 1]
        else:
            kind = self.items[n][0]
            back = 0 if n >= 0 else len(self.items)
            act = self.pre_act[-1] + self.act[n + back + 1] - (self.act[-1] if back else 0)
            dve = self.pre_dve[-1] + self.dve[n + back + 1] - (self.dve[-1] if back else 0)
        if kind in self.act_kinds:
            wait(eng, act_released, b * self.per_act + act)
        if kind in self.dve_kinds:
            wait(eng, dve_released, b * self.per_dve + dve)


def over_batches(eng, body):
    body(0, False)
    with eng.Fori(1, B - 1, 1) as b:
        body(b, False)
    body(B - 1, True)


def split_weights(nc, x, w_in, v_in, t_in, scratch, w_m_dram, vecs, tables, b2, norm, n_hi, n_lo):
    with ExitStack() as ctx:
        def sb(name, shape, dt=F32):
            return ctx.enter_context(nc.sbuf_tensor(name, shape, dt))

        def sem(name):
            return ctx.enter_context(nc.semaphore(name))

        GROUPS_OF_4 = CHUNKS // 4
        first_x = sb("first_x", [P, KT, N])
        raw = sb("w_raw", [P, 2, 4, HALF])
        wv = sb("w_v1", [P, KT, C])
        wp = sb("w_p1", [P, KT, C])
        w_m = sb("w_m_raw", [P, KT, C])
        both = sb("w_split", [P, 2, 4, 2, HALF], F32R)
        prod = ctx.enter_context(nc.psum_tensor("w_prod", [P, KT, HALF], F32))
        bias = ctx.enter_context(nc.psum_tensor("w_bias", [P, HALF], F32))
        group = ctx.enter_context(nc.psum_tensor("first_group", [P, 2, HALF], F32))
        small_in = sem("small_in")
        x_loaded = [sem(f"first_x_loaded{i}") for i in range(KT)]
        loaded = [sem("w_loaded0"), sem("w_loaded1")]
        stored = [sem("w_stored0"), sem("w_stored1")]
        pair_in, hi_done, lo_done = sem("w_pair_in"), sem("w_hi"), sem("w_lo")
        prod_done, bias_done, b2_done = sem("w_prod_done"), sem("w_bias_done"), sem("w_b2")
        prod_copied, prod_stored = sem("w_prod_copied"), sem("w_prod_stored")
        group_full, group_read = sem("first_group_full"), sem("first_group_read")
        block = ctx.enter_context(nc.Block())

        @block.sync
        def _(sp):
            def load(g):
                sp.dma_start(raw[:, g % 2], w_in[:, 4 * g:4 * g + 4, :]).then_inc(loaded[g % 2], 16)

            def store(g):
                sp.wait_ge(lo_done, g + 1)
                sp.dma_start(scratch[:, 4 * g:4 * g + 4], f(both[:, g % 2])).then_inc(stored[g % 2], 16)

            load(0)
            for i in range(KT):
                sp.dma_start(first_x[:, i], x[0, i * P:(i + 1) * P, :]).then_inc(x_loaded[i], 16)
            sp.dma_start(vecs[:], v_in).then_inc(small_in, 16)
            sp.dma_start(tables[:], t_in).then_inc(small_in, 16)
            load(1)
            sp.dma_start(wv[:], w_in[:, W_V1:W_V1 + KT, :]).then_inc(pair_in, 16)
            sp.dma_start(wp[:], w_in[:, W_P1:W_P1 + KT, :]).then_inc(pair_in, 16)
            for g in range(GROUPS_OF_4):
                store(g)
                if g + 2 < GROUPS_OF_4:
                    load(g + 2)
            sp.wait_ge(prod_copied, 1)
            sp.dma_start(w_m_dram, w_m[:]).then_inc(prod_stored, 16)
            for k in range(2):
                sp.wait_ge(stored[k], 16 * (GROUPS_OF_4 // 2))
            sp.wait_ge(prod_stored, 16)

        @block.scalar
        def _(act):
            def hi(g):
                act.wait_ge(loaded[g % 2], 16 * (g // 2 + 1))
                if g >= 2:
                    act.wait_ge(stored[g % 2], 16 * (g // 2))
                nc.scalar.activation(both[:, g % 2, :, 0, :], raw[:, g % 2], ACT.Copy).then_inc(hi_done, 1)

            hi(0)
            hi(1)
            for ct in range(KT):
                norm.tile_hi(act, 0, ct, first_x[:, ct], n_hi[:, ct])
            for g in range(2, GROUPS_OF_4):
                hi(g)
            act.wait_ge(prod_done, 1)
            nc.scalar.activation(w_m[:], prod[:, :, :], ACT.Copy).then_inc(prod_copied, 1)

        @block.vector
        def _(dve):
            def lo(g):
                dve.wait_ge(hi_done, g + 1)
                nc.vector.tensor_tensor(both[:, g % 2, :, 1, :], raw[:, g % 2], f(both[:, g % 2, :, 0, :]),
                                        ALU.subtract).then_inc(lo_done, 1)

            lo(0)
            for ct in range(KT):
                dve.wait_ge(x_loaded[ct], 16)
                norm.tile_stats(dve, 0, ct, first_x[:, ct])
            dve.wait_ge(group_full, 1)
            norm.after_means(dve, 0, group[:, 0, 0:KT], group_read, 1)
            dve.wait_ge(group_full, 2)
            norm.after_vars(0, group[:, 1, 0:KT], group_read)
            lo(1)
            norm.coefficients(dve, 0, 0)
            for ct in range(KT):
                norm.tile_mid(dve, 0, ct, first_x[:, ct])
            for g in range(2, GROUPS_OF_4):
                lo(g)
            dve.wait_ge(bias_done, 1)
            nc.vector.tensor_tensor(b2[:], bias[:, 0:KT], vecs[:, V_BP, :], ALU.add).then_inc(b2_done, 1)
            dve.wait_ge(b2_done, 1)

        @block.tensor
        def _(pe):
            pe.wait_ge(small_in, 32)
            norm.mean_matmul(pe, 0, group[:, 0, 0:KT]).then_inc(group_full, 1)
            norm.var_matmul(pe, 0, group[:, 1, 0:KT]).then_inc(group_full, 1)
            pe.wait_ge(pair_in, 32)
            for ct in range(KT):
                for mt in range(KT):
                    last = nc.tensor.matmul(prod[:, ct, :], wv[:, mt, ct * P:(ct + 1) * P], wp[:, mt, :],
                                            start=(mt == 0), stop=(mt == KT - 1))
            last.then_inc(prod_done, 1)
            for ot in range(KT):
                for mt in range(KT):
                    last = nc.tensor.matmul(bias[:, ot:ot + 1], wp[:, mt, ot * P:(ot + 1) * P],
                                            vecs[:, V_BV, mt:mt + 1], start=(mt == 0), stop=(mt == KT - 1))
            last.then_inc(bias_done, 1)

        @block.gpsimd
        def _(pool):
            pool.wait_ge(small_in, 32)
            norm.power(pool, group_read, 2)
            for ct in range(KT):
                norm.tile_lo(pool, 0, ct, first_x[:, ct], n_hi[:, ct], n_lo[:, ct])


class Norm:

    CHAIN = 6

    def __init__(self, nc, sb, sem, affine, averager, minus_half):
        self.nc, self.affine = nc, affine
        self.averager, self.minus_half = averager, minus_half
        self.stats = sb("norm_stats", [P, KT, 2, 6])
        self.mv = sb("norm_mean_var", [P, KT, 2])
        self.gmean = sb("norm_group_mean", [P, KT])
        self.dev = sb("norm_deviation", [P, KT])
        self.var = sb("norm_var", [P, KT])
        self.vareps = sb("norm_var_eps", [P, KT])
        self.rstd = sb("norm_rstd", [P, KT])
        self.a = sb("norm_a", [P, KT])
        self.ma = sb("norm_mean_a", [P, KT])
        self.b = sb("norm_b", [P, KT])
        self.halves = sem("norm_halves")
        self.passed = sem("norm_passed")
        self.tiles = sem("norm_tiles")
        self.chain = sem("norm_chain")
        self.rstd_ready = sem("norm_rstd_ready")
        self.hi_done = sem("norm_hi_done")
        self.mid_done = sem("norm_mid_done")
        self.lo_done = sem("norm_lo_done")

    def half_stats(self, ct, k, x):
        self.nc.vector.bn_stats(self.stats[:, ct, k, :], x[:, k * HALF:(k + 1) * HALF]).then_inc(self.halves, 1)

    def join_halves(self, dve, n, ct):
        v = self.nc.vector
        wait_apart(dve, self.halves, n * (2 * KT) + (2 * ct + 2), self.passed)
        v.bn_aggr(self.mv[:, ct, :], self.stats[:, ct].rearrange("p a b -> p (a b)")).then_inc(self.tiles, 1)

    def tile_stats(self, dve, n, ct, x):
        for k in range(2):
            self.half_stats(ct, k, x)
        self.join_halves(dve, n, ct)

    def mean_matmul(self, pe, n, out):
        pe.wait_ge(self.tiles, n * KT + KT)
        return self.nc.tensor.matmul(out, self.averager, self.mv[:, :, 0], start=True, stop=True)

    def after_means(self, dve, n, psum, released, released_count):
        v = self.nc.vector
        v.tensor_copy(self.gmean[:], psum).then_inc(released, 1)
        dve.wait_ge(released, released_count)
        dve.wait_ge(self.tiles, n * KT + KT)
        v.tensor_tensor(self.dev[:], self.mv[:, :, 0], self.gmean[:], ALU.subtract).then_inc(self.chain, 1)
        dve.wait_ge(self.chain, n * self.CHAIN + 1)
        v.tensor_tensor(self.var[:], self.dev[:], self.dev[:], ALU.mult).then_inc(self.chain, 1)
        dve.wait_ge(self.chain, n * self.CHAIN + 2)
        v.tensor_tensor(self.var[:], self.var[:], self.mv[:, :, 1], ALU.add).then_inc(self.chain, 1)

    def var_matmul(self, pe, n, out):
        pe.wait_ge(self.chain, n * self.CHAIN + 3)
        return self.nc.tensor.matmul(out, self.averager, self.var[:], start=True, stop=True)

    def after_vars(self, second, psum, released):
        self.nc.vector.tensor_scalar(self.vareps[:], psum, self.affine[second][2], None, ALU.add).then_inc(released, 1)

    def power(self, pool, released, released_count):
        pool.wait_ge(released, released_count)
        self.nc.gpsimd.tensor_tensor(self.rstd[:], self.vareps[:], self.minus_half, ALU.pow
                                     ).then_inc(self.rstd_ready, 1)

    def coefficients(self, dve, n, second):
        v = self.nc.vector
        weight, shift, _ = self.affine[second]
        dve.wait_ge(self.rstd_ready, n + 1)
        v.tensor_tensor(self.a[:], self.rstd[:], weight, ALU.mult).then_inc(self.chain, 1)
        dve.wait_ge(self.chain, n * self.CHAIN + 4)
        v.tensor_tensor(self.ma[:], self.gmean[:], self.a[:], ALU.mult).then_inc(self.chain, 1)
        dve.wait_ge(self.chain, n * self.CHAIN + 5)
        v.tensor_tensor(self.b[:], shift, self.ma[:], ALU.subtract).then_inc(self.chain, 1)

    def tile_hi(self, act, n, ct, x, out):
        act.wait_ge(self.chain, n * self.CHAIN + 6)
        self.nc.scalar.activation(out, x, ACT.Identity, bias=self.b[:, ct:ct + 1],
                                  scale=self.a[:, ct:ct + 1]).then_inc(self.hi_done, 1)

    def tile_mid(self, dve, n, ct, x):
        dve.wait_ge(self.chain, n * self.CHAIN + 6)
        dve.wait_ge(self.hi_done, n * KT + (ct + 1))
        self.nc.vector.tensor_scalar(x, x, self.a[:, ct:ct + 1], self.b[:, ct:ct + 1], ALU.mult, ALU.add
                                     ).then_inc(self.mid_done, 1)

    def tile_lo(self, pool, n, ct, x, hi, out):
        pool.wait_ge(self.mid_done, n * KT + (ct + 1))
        self.nc.gpsimd.tensor_tensor(out, x, f(hi), ALU.subtract).then_inc(self.lo_done, 1)


def three(nc, out, w_hi, w_lo, m_hi, m_lo, first, last):
    nc.tensor.matmul(out, w_hi, m_hi, start=first, stop=False)
    nc.tensor.matmul(out, w_hi, m_lo, start=False, stop=False)
    return nc.tensor.matmul(out, w_lo, m_hi, start=False, stop=last)


def attend_heads(nc, x, x1, scratch, vecs, ident, norm, n_hi, n_lo):
    with ExitStack() as ctx:
        def sb(name, shape, dt=F32):
            return ctx.enter_context(nc.sbuf_tensor(name, shape, dt))

        def sem(name):
            return ctx.enter_context(nc.semaphore(name))

        U = HEADS * UNITS
        TILES_KEPT = 6
        LAG = 2
        BEHIND = 3
        w_qk = sb("w_qk", [P, 2, 2, KT, P], F32R)
        w_vo = sb("w_vo", [P, 4, 2, HALF], F32R)
        vt = sb("vt", [P, JT, HEADS, P], F32R)
        q_st = sb("q_st", [P, 2, N], F32R)
        k_hi = sb("k_hi", [P, 2, N], F32R)
        k_lo = sb("k_lo", [P, 2, N], F32R)
        probs = sb("probs", [P, TILES_KEPT, N])
        pt_hi = sb("pt_hi", [P, TURNS, 2, QU], F32R)
        pt_lo = sb("pt_lo", [P, TURNS, 2, QU], F32R)
        side = sb("side", [P, N])
        o_mid = sb("o_mid", [P, 2, N])
        o_hi = sb("o_hi", [P, PAIRS, N], F32R)
        o_lo = sb("o_lo", [P, PAIRS, N], F32R)
        x_in = sb("x_in", [P, 2, N])
        neg_max = sb("neg_max", [P, TILES_KEPT])
        total = sb("total", [P, TILES_KEPT])
        inverse = sb("inverse", [P, TILES_KEPT])
        slot = ctx.enter_context(nc.psum_tensor("slot", [P, 2, 2 * HALF], F32))
        turn = ctx.enter_context(nc.psum_tensor("turn", [P, 2, 2, QU], F32))
        mix = ctx.enter_context(nc.psum_tensor("mix", [P, 2, HALF], F32))

        x_loaded = [sem("x_loaded0"), sem("x_loaded1")]
        qk_loaded = [sem("wqk_loaded0"), sem("wqk_loaded1")]
        v_loaded = [sem(f"wv_loaded{i}") for i in range(4)]
        o_loaded = [sem(f"wo_loaded{i}") for i in range(4)]
        r_loaded = [sem(f"residual_loaded{i}") for i in range(KT)]
        y_stored = [sem(f"y_stored{i}") for i in range(KT)]
        scale_passed = sem("scale_passed")
        zeroed = sem("zeroed")
        slot_full = sem("slot_full")
        act_released = sem("act_released")
        dve_released = sem("dve_released")
        q_hi_ready = sem("q_hi_ready")
        k_hi_twice = sem("k_hi_twice")
        max_ready = sem("max_ready")
        inverse_ready = sem("inverse_ready")
        probs_ready = sem("probs_ready")
        turn_full = sem("turn_full")
        turn_hi = sem("turn_hi")
        turn_lo = sem("turn_lo")
        mixed = sem("mixed")
        mix_read = sem("mix_read")
        mix_added = sem("mix_added")
        pair_hi = sem("pair_hi")
        pair_lo = sem("pair_lo")
        STATS_AT, MEANS_AT, VARS_AT, COEF_AT, NORM_AT = 4, 22, 24, 25, 27

        def projected_at(s, last):
            if s < U:
                return [(s // UNITS + 1, s % UNITS)] if s // UNITS + 1 < HEADS else []
            if s >= U + LAG or last:
                return []
            return [(HEADS, 2 * (s - U)), (HEADS, 2 * (s - U) + 1)]

        def order(last):
            items = []
            for s in range(U):
                items.append(("S", s, 0))
                items += [("QK",) + part for part in projected_at(s, last)]
                if s in (MEANS_AT, VARS_AT):
                    items.append(("GN", s))
                items.append(("S", s, 1))
                if s < LAG:
                    items += [("V", 2 * s), ("V", 2 * s + 1)]
            for s in range(U, U + LAG):
                items += [("QK",) + part for part in projected_at(s, last)]
            return items + [("OUT", m) for m in range(KT)]

        pre = [("QK", 0, i) for i in range(UNITS)]
        ring = Slots(pre, order(False), ("V", "QK", "S"), ("V", "QK", "GN", "OUT"))
        ring_last = Slots(pre, order(True), ring.act_kinds, ring.dve_kinds, ring)

        def x_count(b, k):
            return b * (8 * 2 * KT) + 16 * (k // 2 + 1)

        def x1_tile(m):
            return (4, 5, 2, 3)[m]

        block = ctx.enter_context(nc.Block())

        @block.sync
        def _(sp):
            def load_x(b, last, i):
                if last:
                    sp.wait_ge(y_stored[i], 16)
                source = x1[0] if last else x[b + 1]
                sp.dma_start(x_in[:, i % 2], source[i * P:(i + 1) * P, :]).then_inc(x_loaded[i % 2], 16)

            def load_qk(h):
                sp.dma_start(f(w_qk[:, h % 2].rearrange("p a k m -> p (a k m)")),
                             scratch[:, W_QK + h % HEADS].rearrange("p a n -> p (a n)")).then_inc(qk_loaded[h % 2], 16)

            def load_vo(c, chunk, loaded):
                sp.dma_start(f(w_vo[:, c]), scratch[:, chunk + c]).then_inc(loaded[c], 16)

            for c in range(2):
                load_qk(c)
            for c in range(4):
                load_vo(c, W_V, v_loaded)

            def body(b, last):
                r = ring_last if last else ring

                def store(m):
                    sp.wait_ge(dve_released, r.dve_done(b, ("OUT", m)))
                    sp.dma_start(x1[b, m * P:(m + 1) * P, :], probs[:, x1_tile(m), :]).then_inc(y_stored[m], 16)

                if isinstance(b, int) and b == 0:
                    sp.wait_ge(slot_full, len(pre))
                else:
                    sp.wait_ge(slot_full, b * ring.per_full + (ring.full(0, ("QK", HEADS, UNITS - 1)) - ring.per_full))
                load_qk(2)
                for i in range(2):
                    sp.wait_ge(norm.lo_done, b * KT + (KT - 1 + i))
                    load_x(b, last, i)
                sp.wait_ge(slot_full, r.full(b, ("V", JT // 2 - 1)))
                for c in range(4):
                    load_vo(c, W_O, o_loaded)
                sp.wait_ge(slot_full, r.full(b, ("QK", 1, UNITS - 1)))
                load_qk(3)
                for h in range(4, HEADS if last else HEADS + 2):
                    sp.wait_ge(slot_full, r.full(b, ("QK", h - 2, UNITS - 1)))
                    load_qk(h)
                    if h in (4, 5):
                        i = h - 2
                        sp.wait_ge(norm.tiles, b * KT + (KT + i - 1))
                        load_x(b, last, i)
                    if h in (6, 7):
                        i = h - 6
                        sp.wait_ge(norm.tiles, b * KT + (2 * KT - 1 + i))
                        load_x(b, last, i)
                for i in range(2, KT):
                    sp.wait_ge(norm.lo_done, b * KT + (KT + i - 1))
                    load_x(b, last, i)
                for m in range(KT):
                    sp.wait_ge(turn_full, b * (TURNS * U) + TURNS * (U - (2 if m < 2 else 0)))
                    sp.dma_start(probs[:, x1_tile(m), :], x[b, m * P:(m + 1) * P, :]).then_inc(r_loaded[m], 16)
                for m in range(KT):
                    if not last:
                        sp.wait_ge(slot_full, r.full(b, ("OUT", m)))
                        load_vo(m, W_V, v_loaded)
                    if m >= 1:
                        store(m - 1)
                store(KT - 1)

            over_batches(sp, body)
            for m in range(KT):
                sp.wait_ge(y_stored[m], 16 * B)

        @block.tensor
        def _(pe):
            def project_qk(r, b, h, i):
                item = ("QK", h, i)
                cols = slice(i * QU, (i + 1) * QU)
                at = r.slot(item) if h else i % 2
                if h:
                    r.wait_free(pe, act_released, dve_released, b, item)
                elif i >= 2:
                    pe.wait_ge(act_released, i - 1)
                    pe.wait_ge(dve_released, i - 1)
                if i == 0:
                    pe.wait_ge(qk_loaded[h % 2], b * (8 * HEADS) + 16 * (h // 2 + 1))
                for kt in range(KT):
                    if h % HEADS == 0 and i == 0:
                        pe.wait_ge(norm.lo_done, (b + (h // HEADS)) * KT + (kt + 1))
                    mm = three(nc, slot[:, at, 0:QU], w_qk[:, h % 2, 0, kt], w_qk[:, h % 2, 1, kt],
                               n_hi[:, kt, cols], n_lo[:, kt, cols], kt == 0, kt == KT - 1)
                mm.then_inc(slot_full, 1)

            pe.wait_ge(zeroed, 1)
            for i in range(UNITS):
                project_qk(ring, 0, 0, i)

            def body(b, last):
                r = ring_last if last else ring

                def project_v(i):
                    r.wait_free(pe, act_released, dve_released, b, ("V", i))
                    for kt in range(KT):
                        if i == 0:
                            pe.wait_ge(v_loaded[kt], b * 16 + 16)
                        for jj in range(2):
                            js = slice((2 * i + jj) * P, (2 * i + jj + 1) * P)
                            mm = three(nc, slot[:, r.slot(("V", i)), jj * HALF:(jj + 1) * HALF],
                                       n_hi[:, kt, js], n_lo[:, kt, js],
                                       w_vo[:, kt, 0, :], w_vo[:, kt, 1, :], kt == 0, kt == KT - 1)
                    mm.then_inc(slot_full, 1)

                def scores(u, t):
                    h = u // UNITS
                    at = (u % UNITS) * QU + t * P
                    r.wait_free(pe, act_released, dve_released, b, ("S", u, t))
                    if u == 0 and t == 0:
                        pe.wait_ge(act_released, r.act_before(b))
                        pe.wait_ge(dve_released, r.dve_before(b))
                    elif u % UNITS == 0 and t == 0:
                        pe.wait_ge(act_released, r.act_done(b, ("QK", h, UNITS - 1)))
                        pe.wait_ge(dve_released, r.dve_done(b, ("QK", h, UNITS - 1)))
                    if u % UNITS == 0 and t == 0:
                        pe.wait_ge(k_hi_twice, b * U + (UNITS * h + UNITS))
                    for half in range(2):
                        cols = slice(half * HALF, (half + 1) * HALF)
                        out = slot[:, r.slot(("S", u, t)), cols]
                        nc.tensor.matmul(out, q_st[:, h % 2, at:at + P], k_hi[:, h % 2, cols], start=True, stop=False)
                        mm = nc.tensor.matmul(out, q_st[:, h % 2, at:at + P], k_lo[:, h % 2, cols],
                                              start=False, stop=True)
                    mm.then_inc(slot_full, 1)

                def turn_item(u, a):
                    if a == 0:
                        pe.wait_ge(probs_ready, b * (TILES * U) + TILES * (u + 1))
                    wait(pe, turn_lo, b * (TURNS * U) + (TURNS * u + a - 1))
                    for jj in range(2):
                        for t in range(TILES):
                            mm = nc.tensor.transpose(turn[:, a % 2, jj, t * P:(t + 1) * P],
                                                     probs[:, (TILES * u + t) % TILES_KEPT,
                                                           (2 * a + jj) * P:(2 * a + jj + 1) * P], ident)
                    mm.then_inc(turn_full, 1)

                def mix_item(k):
                    u, a = k // TURNS, k % TURNS
                    pe.wait_ge(turn_lo, b * (TURNS * U) + (k + 1))
                    if k == 0:
                        pe.wait_ge(dve_released, r.dve_done(b, ("V", JT // 2 - 1)))
                    if a == 0:
                        wait(pe, mix_read, b * U + (u - 1))
                    for n, part in enumerate((pt_hi, pt_lo)):
                        for jj in range(2):
                            mm = nc.tensor.matmul(mix[:, u % 2, 0:QU], vt[:, 2 * a + jj, u // UNITS, :], part[:, a, jj, :],
                                                  start=(n == 0 and a + jj == 0),
                                                  stop=(n == 1 and a == TURNS - 1 and jj == 1))
                    mm.then_inc(mixed, 1)

                def project_out(m, pairs):
                    if 0 in pairs:
                        r.wait_free(pe, act_released, dve_released, b, ("OUT", m))
                        pe.wait_ge(o_loaded[m], b * 16 + 16)
                    w = w_vo[:, m].rearrange("p a (k m) -> p a k m", k=KT)
                    for kt in pairs:
                        if m == 0:
                            pe.wait_ge(pair_lo, b * PAIRS + (kt + 1))
                        for half in range(2):
                            cols = slice(half * HALF, (half + 1) * HALF)
                            mm = three(nc, slot[:, r.slot(("OUT", m)), cols], w[:, 0, kt], w[:, 1, kt],
                                       o_hi[:, kt, cols], o_lo[:, kt, cols], kt == 0, kt == PAIRS - 1)
                    if PAIRS - 1 in pairs:
                        mm.then_inc(slot_full, 1)

                def group_stats(s, product):
                    r.wait_free(pe, act_released, dve_released, b, ("GN", s))
                    product(pe, b + 1, slot[:, r.slot(("GN", s)), 0:KT]).then_inc(slot_full, 1)

                for s in range(U + LAG):
                    parts = projected_at(s, last)
                    for a in range(TURNS):
                        if s >= LAG:
                            turn_item(s - LAG, a)
                            k = TURNS * (s - LAG) + a - BEHIND
                            if k >= 0:
                                mix_item(k)
                        if s == MEANS_AT and a == 2:
                            group_stats(s, norm.mean_matmul)
                        if s == VARS_AT and a == 2:
                            group_stats(s, norm.var_matmul)
                        if s < U and a % 2 == 0:
                            scores(s, a // 2)
                        if s < U and a == 1 and parts:
                            project_qk(r, b, *parts[0])
                        if s >= U and a % 2 == 1 and parts:
                            project_qk(r, b, *parts[a // 2])
                    if s < LAG:
                        project_v(2 * s)
                        project_v(2 * s + 1)
                for k in range(TURNS * U - BEHIND, TURNS * U):
                    mix_item(k)
                for m in range(2):
                    project_out(m, range(PAIRS - 1))
                for m in range(2):
                    project_out(m, [PAIRS - 1])
                for m in range(2, KT):
                    project_out(m, range(PAIRS))

            over_batches(pe, body)

        @block.scalar
        def _(act):
            def qk_hi(r, b, h, i):
                at = r.slot(("QK", h, i)) if h else i % 2
                act.wait_ge(slot_full, r.full(b, ("QK", h, i)) if h else i + 1)
                cols = slice(i * QU, (i + 1) * QU)
                nc.scalar.activation(q_st[0:HD, h % 2, cols], slot[0:HD, at, 0:QU], ACT.Copy, scale=SCALE
                                     ).then_inc(q_hi_ready, 1)
                nc.scalar.activation(k_hi[HD:P, h % 2, cols], slot[HD:P, at, 0:QU], ACT.Copy).then_inc(act_released, 1)

            def k_hi_again(r, b, h, i):
                cols = slice(i * QU, (i + 1) * QU)
                act.wait_ge(act_released, r.act_done(b, ("QK", h, i)) if h else i + 1)
                nc.scalar.activation(k_hi[0:HD, h % 2, cols], f(k_hi[HD:P, h % 2, cols]), ACT.Copy).then_inc(k_hi_twice, 1)

            for i in range(UNITS):
                qk_hi(ring, 0, 0, i)
                k_hi_again(ring, 0, 0, i)

            def body(b, last):
                r = ring_last if last else ring

                def v_hi(i):
                    act.wait_ge(slot_full, r.full(b, ("V", i)))
                    for jj in range(2):
                        src = slot[:, r.slot(("V", i)), jj * HALF:(jj + 1) * HALF].rearrange("p (g e d) -> p g e d", g=PAIRS, e=2)
                        dst = vt[:, 2 * i + jj].rearrange("p (g e) (w d) -> p g (e w) d", e=2, w=2)[:, :, 0:4:3]
                        done = nc.scalar.activation(dst, src, ACT.Copy)
                    done.then_inc(act_released, 1)

                def exponentials(u, t):
                    i = TILES * u + t
                    act.wait_ge(max_ready, b * (TILES * U) + (i + 1))
                    wait(act, turn_full, b * (TURNS * U) + TURNS * (u - 2))
                    k = i % TILES_KEPT
                    for m in range(KT):
                        if i == x1_tile(m):
                            wait(act, y_stored[m], b * 16)
                    nc.scalar.activation(probs[:, k, :], slot[:, r.slot(("S", u, t)), :], ACT.Exp,
                                         bias=neg_max[:, k:k + 1], accum_out=total[:, k:k + 1]).then_inc(act_released, 1)

                def turn_his(u, a):
                    act.wait_ge(turn_full, b * (TURNS * U) + (TURNS * u + a + 1))
                    wait(act, mixed, b * (TURNS * U) + (TURNS * (u - 1) + a + 1))
                    nc.scalar.activation(pt_hi[:, a], turn[:, a % 2], ACT.Copy).then_inc(turn_hi, 1)

                def sides(u):
                    odd = (u // UNITS) % 2
                    own, other = (slice(HD, P), slice(0, HD)) if odd else (slice(0, HD), slice(HD, P))
                    at = (u % UNITS) * QU
                    g = u // (2 * UNITS)
                    act.wait_ge(mixed, b * (TURNS * U) + TURNS * (u + 1))
                    wait(act, mix_added, b * (PAIRS * UNITS) + (UNITS * (g - 1) + u % UNITS + 1))
                    nc.scalar.activation(side[own, at:at + QU], mix[other, u % 2, 0:QU], ACT.Copy)
                    if u % (2 * UNITS) == 0:
                        wait(act, pair_lo, b * PAIRS + (g - 1))
                    nc.scalar.activation(o_mid[own, g % 2, at:at + QU], mix[own, u % 2, 0:QU], ACT.Copy
                                         ).then_inc(mix_read, 1)

                def pair_his(u):
                    g = u // (2 * UNITS)
                    act.wait_ge(mix_added, b * (PAIRS * UNITS) + UNITS * (g + 1))
                    nc.scalar.activation(o_hi[:, g, :], o_mid[:, g % 2], ACT.Copy).then_inc(pair_hi, 1)

                for s in range(U + LAG + 2):
                    turned = LAG <= s < U + LAG
                    parts = projected_at(s, last)
                    if turned:
                        turn_his(s - LAG, 0)
                    if LAG < s <= U:
                        exponentials(s - 1, 1)
                    if turned:
                        turn_his(s - LAG, 1)
                    if s < U:
                        exponentials(s, 0)
                    if parts:
                        qk_hi(r, b, *parts[0])
                    if turned:
                        turn_his(s - LAG, 2)
                    if parts:
                        k_hi_again(r, b, *parts[0])
                    if 0 <= s - LAG - 1 < U:
                        sides(s - LAG - 1)
                    if turned:
                        turn_his(s - LAG, 3)
                    if len(parts) == 2:
                        qk_hi(r, b, *parts[1])
                        k_hi_again(r, b, *parts[1])
                    if s < LAG:
                        exponentials(s, 1)
                        v_hi(2 * s)
                        v_hi(2 * s + 1)
                    if s >= LAG + 1 and (s - LAG - 1) % (2 * UNITS) == 2 * UNITS - 1:
                        pair_his(s - LAG - 1)
                    if NORM_AT <= s < NORM_AT + KT:
                        ct = s - NORM_AT
                        act.wait_ge(x_loaded[ct % 2], x_count(b, KT + ct))
                        norm.tile_hi(act, b + 1, ct, x_in[:, ct % 2], n_hi[:, ct])

            over_batches(act, body)

        @block.vector
        def _(dve):
            nc.vector.memset(f(k_lo[HD:P, :, :]), 0.0).then_inc(zeroed, 1)

            def qk_lo(r, b, h, i):
                at = r.slot(("QK", h, i)) if h else i % 2
                dve.wait_ge(q_hi_ready, b * U + (UNITS * h + i + 1))
                cols = slice(i * QU, (i + 1) * QU)
                nc.vector.scalar_tensor_tensor(q_st[HD:P, h % 2, cols], slot[0:HD, at, 0:QU], SCALE,
                                               f(q_st[0:HD, h % 2, cols]), ALU.mult, ALU.subtract)
                dve.wait_ge(act_released, r.act_done(b, ("QK", h, i)) if h else i + 1)
                nc.vector.tensor_tensor(k_lo[0:HD, h % 2, cols], slot[HD:P, at, 0:QU], f(k_hi[HD:P, h % 2, cols]),
                                        ALU.subtract).then_inc(dve_released, 1)

            for i in range(UNITS):
                qk_lo(ring, 0, 0, i)

            def body(b, last):
                r = ring_last if last else ring

                def v_lo(i):
                    dve.wait_ge(act_released, r.act_done(b, ("V", i)))
                    for jj in range(2):
                        src = slot[:, r.slot(("V", i)), jj * HALF:(jj + 1) * HALF].rearrange("p (g e d) -> p g e d", g=PAIRS, e=2)
                        heads = vt[:, 2 * i + jj].rearrange("p (g e) (w d) -> p g (e w) d", e=2, w=2)
                        done = nc.vector.tensor_tensor(heads[:, :, 1:3], src, f(heads[:, :, 0:4:3]), ALU.subtract)
                    done.then_inc(dve_released, 1)

                def maxima(u, t):
                    k = (TILES * u + t) % TILES_KEPT
                    dve.wait_ge(slot_full, r.full(b, ("S", u, t)))
                    nc.vector.tensor_reduce(neg_max[:, k:k + 1], slot[:, r.slot(("S", u, t)), :], AX_X, ALU.max,
                                            negate=True).then_inc(max_ready, 1)

                def inverses(u, t):
                    k = (TILES * u + t) % TILES_KEPT
                    dve.wait_ge(act_released, r.act_done(b, ("S", u, t)))
                    nc.vector.reciprocal(inverse[:, k:k + 1], total[:, k:k + 1]).then_inc(inverse_ready, 1)

                def turn_los(u, a):
                    dve.wait_ge(turn_hi, b * (TURNS * U) + (TURNS * u + a + 1))
                    nc.vector.tensor_tensor(pt_lo[:, a], turn[:, a % 2], f(pt_hi[:, a]), ALU.subtract).then_inc(turn_lo, 1)

                def residual(m):
                    dve.wait_ge(slot_full, r.full(b, ("OUT", m)))
                    dve.wait_ge(r_loaded[m], b * 16 + 16)
                    y = probs[:, x1_tile(m), :]
                    nc.vector.scalar_tensor_tensor(y, slot[:, r.slot(("OUT", m)), :], vecs[:, V_OB, m:m + 1], y,
                                                   ALU.add, ALU.add).then_inc(dve_released, 1)

                for s in range(U + LAG):
                    turned = LAG <= s
                    parts = projected_at(s, last)
                    if turned:
                        turn_los(s - LAG, 0)
                    if LAG < s <= U:
                        inverses(s - 1, 1)
                    if s < U:
                        maxima(s, 0)
                    if turned:
                        turn_los(s - LAG, 1)
                    if s < U:
                        inverses(s, 0)
                    if parts:
                        qk_lo(r, b, *parts[0])
                    if turned:
                        turn_los(s - LAG, 2)
                    if s == MEANS_AT:
                        dve.wait_ge(slot_full, r.full(b, ("GN", s)))
                        norm.after_means(dve, b + 1, slot[:, r.slot(("GN", s)), 0:KT], dve_released,
                                         r.dve_done(b, ("GN", s)))
                    if s == VARS_AT:
                        dve.wait_ge(slot_full, r.full(b, ("GN", s)))
                        norm.after_vars(int(last), slot[:, r.slot(("GN", s)), 0:KT], dve_released)
                    if s < U:
                        maxima(s, 1)
                    if turned:
                        turn_los(s - LAG, 3)
                    if len(parts) == 2:
                        qk_lo(r, b, *parts[1])
                    if s < LAG:
                        inverses(s, 1)
                        v_lo(2 * s)
                        v_lo(2 * s + 1)
                    if STATS_AT <= s <= STATS_AT + 4 * KT and s % 2 == 0:
                        ct, k = (s - STATS_AT) // 4, (s - STATS_AT) // 2 % 2
                        if k == 0 and ct > 0:
                            norm.join_halves(dve, b + 1, ct - 1)
                        if ct < KT:
                            dve.wait_ge(x_loaded[ct % 2], x_count(b, ct))
                            norm.half_stats(ct, k, x_in[:, ct % 2])
                    if s == COEF_AT:
                        norm.coefficients(dve, b + 1, int(last))
                    if NORM_AT <= s < NORM_AT + KT:
                        norm.tile_mid(dve, b + 1, s - NORM_AT, x_in[:, (s - NORM_AT) % 2])
                for m in range(KT):
                    residual(m)

            over_batches(dve, body)

        @block.gpsimd
        def _(pool):
            def body(b, last):
                r = ring_last if last else ring

                def normalise(u, t):
                    k = (TILES * u + t) % TILES_KEPT
                    wait_apart(pool, inverse_ready, b * (TILES * U) + (TILES * u + t + 1), scale_passed)
                    nc.gpsimd.tensor_scalar(probs[:, k, :], probs[:, k, :], inverse[:, k:k + 1], 1.0,
                                            ALU.mult, ALU.mult).then_inc(probs_ready, 1)

                def add_sides(u):
                    g = u // (2 * UNITS)
                    at = (u % UNITS) * QU
                    mid = o_mid[:, g % 2, at:at + QU]
                    pool.wait_ge(mix_read, b * U + (u + 1))
                    nc.gpsimd.tensor_tensor(mid, mid, side[:, at:at + QU], ALU.add).then_inc(mix_added, 1)

                def pair_los(u):
                    g = u // (2 * UNITS)
                    pool.wait_ge(pair_hi, b * PAIRS + (g + 1))
                    nc.gpsimd.tensor_tensor(o_lo[:, g, :], o_mid[:, g % 2], f(o_hi[:, g, :]), ALU.subtract
                                            ).then_inc(pair_lo, 1)

                for s in range(U + LAG + 2):
                    if LAG < s <= U:
                        normalise(s - 1, 1)
                    if s < U:
                        normalise(s, 0)
                    if s < LAG:
                        normalise(s, 1)
                    if 0 <= s - LAG - 1 < U and (s - LAG - 1) // UNITS % 2:
                        add_sides(s - LAG - 1)
                    if s >= LAG + 1 and (s - LAG - 1) % (2 * UNITS) == 2 * UNITS - 1:
                        pair_los(s - LAG - 1)
                    if s == VARS_AT:
                        norm.power(pool, dve_released, r.dve_done(b, ("GN", s)))
                    if NORM_AT <= s < NORM_AT + KT:
                        ct = s - NORM_AT
                        norm.tile_lo(pool, b + 1, ct, x_in[:, ct % 2], n_hi[:, ct], n_lo[:, ct])

            over_batches(pool, body)


def attend_single(nc, x1, out, w_in, w_m_dram, vecs, b2, ident, norm, n_hi, n_lo):
    with ExitStack() as ctx:
        def sb(name, shape, dt=F32):
            return ctx.enter_context(nc.sbuf_tensor(name, shape, dt))

        def sem(name):
            return ctx.enter_context(nc.semaphore(name))

        w_q = sb("w_q", [P, KT, 2, HALF], F32R)
        w_k = sb("w_k", [P, KT, 2, HALF], F32R)
        w_m = sb("w_m", [P, KT, 2, HALF], F32R)
        k_hi = sb("k1_hi", [P, KT, N], F32R)
        k_lo = sb("k1_lo", [P, KT, N], F32R)
        v_hi = sb("v1_hi", [P, JT, C], F32R)
        v_lo = sb("v1_lo", [P, JT, C], F32R)
        q_hi = sb("q1_hi", [P, KT, QU], F32R)
        q_lo = sb("q1_lo", [P, KT, QU], F32R)
        probs = sb("probs1", [P, PROBS, N])
        pt_hi = sb("pt1_hi", [P, JT, QU], F32R)
        pt_lo = sb("pt1_lo", [P, JT, QU], F32R)
        x_in = sb("x1_in", [P, 2, N])
        y = sb("y", [P, 2, KT, QU])
        neg_raw = sb("neg_raw", [P, PROBS])
        neg_max = sb("neg_max1", [P, PROBS])
        total = sb("total1", [P, PROBS])
        inverse = sb("inverse1", [P, PROBS])
        slot = ctx.enter_context(nc.psum_tensor("slot1", [P, 2, 2 * HALF], F32))
        turn = ctx.enter_context(nc.psum_tensor("turn1", [P, 2, 2, QU], F32))
        mix = ctx.enter_context(nc.psum_tensor("mix1", [P, 2, HALF], F32))

        x_loaded = [sem("x1_loaded0"), sem("x1_loaded1")]
        w_loaded = [sem(f"w1_loaded{i}") for i in range(3 * KT)]
        w_hi = sem("w1_hi")
        w_lo = sem("w1_lo")
        y_loaded = [sem("y_loaded0"), sem("y_loaded1")]
        y_stored = [sem("y1_stored0"), sem("y1_stored1")]
        slot_full = sem("slot1_full")
        act_released = sem("act1_released")
        dve_released = sem("dve1_released")
        scale_passed = sem("scale1_passed")
        raw_ready = sem("raw_ready")
        max_ready = sem("max1_ready")
        inverse_ready = sem("inverse1_ready")
        probs_ready = sem("probs1_ready")
        turn_full = sem("turn1_full")
        turn_hi = sem("turn1_hi")
        turn_lo = sem("turn1_lo")
        mix_full = sem("mix1_full")
        mix_added = sem("mix1_added")
        U = UNITS
        MEANS_AT, VARS_AT = 1, 2

        def order(last):
            items = [("Q", 0), ("V", 0), ("V", 1)]
            for s in range(U):
                items += [("S", s, 0), ("S", s, 1)]
                if s + 1 < U:
                    items.append(("Q", s + 1))
                if s == 0:
                    items += [("V", 2), ("V", 3)]
                if not last and s in (MEANS_AT, VARS_AT):
                    items.append(("GN", s))
            return items if last else items + [("K", m) for m in range(KT)]

        pre = [("K", m) for m in range(KT)]
        ring = Slots(pre, order(False), ("K", "V", "Q", "S"), ("K", "V", "Q", "GN"))
        ring_last = Slots(pre, order(True), ring.act_kinds, ring.dve_kinds, ring)

        def x_count(b, k):
            return b * (8 * 2 * KT) + 16 * (k // 2 + 1)

        chunks = [(w, kt) for w in (w_k, w_q, w_m) for kt in range(KT)]
        STAGED = PROBS * N // HALF

        def staged(i):
            i %= STAGED
            return probs[:, i // 2, (i % 2) * HALF:(i % 2 + 1) * HALF]

        block = ctx.enter_context(nc.Block())

        @block.sync
        def _(sp):
            def load_x(b, i):
                sp.dma_start(x_in[:, i % 2], x1[b, i * P:(i + 1) * P, :]).then_inc(x_loaded[i % 2], 16)

            for i, (w, kt) in enumerate(chunks):
                if i >= STAGED:
                    sp.wait_ge(w_lo, i - STAGED + 1)
                source = w_m_dram[:, kt] if w is w_m else w_in[:, (W_K1 if w is w_k else W_Q1) + kt, :]
                sp.dma_start(staged(i), source).then_inc(w_loaded[i], 16)

            def body(b, last):
                def residual(u):
                    wait(sp, y_stored[u % 2], b * 32 + 16 * (u // 2))
                    sp.dma_start(y[:, u % 2], x1[b, :, u * QU:(u + 1) * QU].rearrange("(k p) n -> p k n", p=P)
                                 ).then_inc(y_loaded[u % 2], 16)

                def store(u):
                    sp.wait_ge(mix_added, b * (KT * U) + KT * (u + 1))
                    sp.dma_start(out[b, :, u * QU:(u + 1) * QU].rearrange("(k p) n -> p k n", p=P), y[:, u % 2]
                                 ).then_inc(y_stored[u % 2], 16)

                if not last:
                    for i in range(2):
                        sp.wait_ge(norm.lo_done, b * KT + (B * KT + KT - 1 + i))
                        load_x(b + 1, i)
                residual(0)
                residual(1)
                if not last:
                    for i in range(2, 4):
                        sp.wait_ge(norm.tiles, b * KT + (B * KT + KT + i - 1))
                        load_x(b + 1, i)
                    for i in range(2):
                        sp.wait_ge(norm.tiles, b * KT + (B * KT + 2 * KT - 1 + i))
                        load_x(b + 1, i)
                store(0)
                residual(2)
                store(1)
                residual(3)
                if not last:
                    for i in range(2, 4):
                        sp.wait_ge(norm.lo_done, b * KT + (B * KT + KT + i - 1))
                        load_x(b + 1, i)
                store(2)
                store(3)

            over_batches(sp, body)
            for k in range(2):
                sp.wait_ge(y_stored[k], 32 * B)

        @block.tensor
        def _(pe):
            def project_k(r, b, m, n):
                at = m % 2 if n is b else r.slot(("K", m))
                if n is b:
                    if m >= 2:
                        pe.wait_ge(act_released, m - 1)
                        pe.wait_ge(dve_released, m - 1)
                else:
                    r.wait_free(pe, act_released, dve_released, b, ("K", m))
                ms = slice(m * P, (m + 1) * P)
                for kt in range(KT):
                    if m == 0:
                        pe.wait_ge(norm.lo_done, n * KT + (B * KT + kt + 1))
                    if m == 0 and n is b:
                        pe.wait_ge(w_lo, kt + 1)
                    for half in range(2):
                        cols = slice(half * HALF, (half + 1) * HALF)
                        mm = three(nc, slot[:, at, cols], w_k[:, kt, 0, ms], w_k[:, kt, 1, ms],
                                   n_hi[:, kt, cols], n_lo[:, kt, cols], kt == 0, kt == KT - 1)
                mm.then_inc(slot_full, 1)

            for m in range(KT):
                project_k(ring, 0, m, 0)

            def body(b, last):
                r = ring_last if last else ring

                def project_v(i):
                    r.wait_free(pe, act_released, dve_released, b, ("V", i))
                    for jj in range(2):
                        js = slice((2 * i + jj) * P, (2 * i + jj + 1) * P)
                        for kt in range(KT):
                            mm = three(nc, slot[:, r.slot(("V", i)), jj * HALF:(jj + 1) * HALF],
                                       n_hi[:, kt, js], n_lo[:, kt, js], w_m[:, kt, 0, :], w_m[:, kt, 1, :],
                                       kt == 0, kt == KT - 1)
                    mm.then_inc(slot_full, 1)

                def project_q(u):
                    r.wait_free(pe, act_released, dve_released, b, ("Q", u))
                    cols = slice(u * QU, (u + 1) * QU)
                    for m in range(KT):
                        for kt in range(KT):
                            ms = slice(m * P, (m + 1) * P)
                            mm = three(nc, slot[:, r.slot(("Q", u)), m * QU:(m + 1) * QU],
                                       w_q[:, kt, 0, ms], w_q[:, kt, 1, ms],
                                       n_hi[:, kt, cols], n_lo[:, kt, cols], kt == 0, kt == KT - 1)
                    mm.then_inc(slot_full, 1)

                def scores(u, t, half):
                    if half == 0:
                        r.wait_free(pe, act_released, dve_released, b, ("S", u, t))
                    if t == 0 and half == 0:
                        pe.wait_ge(act_released, r.act_done(b, ("Q", u)))
                        pe.wait_ge(dve_released, r.dve_done(b, ("Q", u)))
                    qs = slice(t * P, (t + 1) * P)
                    cols = slice(half * HALF, (half + 1) * HALF)
                    for kt in range(KT):
                        mm = three(nc, slot[:, r.slot(("S", u, t)), cols], q_hi[:, kt, qs], q_lo[:, kt, qs],
                                   k_hi[:, kt, cols], k_lo[:, kt, cols], kt == 0, kt == KT - 1)
                    if half == 1:
                        mm.then_inc(slot_full, 1)

                def turn_item(u, a):
                    if a == 0:
                        pe.wait_ge(probs_ready, b * (TILES * U) + TILES * (u + 1))
                    wait(pe, turn_lo, b * (TURNS * U) + (TURNS * u + a - 1))
                    for jj in range(2):
                        for t in range(TILES):
                            mm = nc.tensor.transpose(turn[:, a % 2, jj, t * P:(t + 1) * P],
                                                     probs[:, (TILES * u + t) % PROBS,
                                                           (2 * a + jj) * P:(2 * a + jj + 1) * P], ident)
                    mm.then_inc(turn_full, 1)

                def mixes(u):
                    pe.wait_ge(turn_lo, b * (TURNS * U) + TURNS * (u + 1))
                    if u == 0:
                        pe.wait_ge(dve_released, r.dve_done(b, ("V", 3)))
                    for ot in range(KT):
                        wait(pe, mix_added, b * (KT * U) + (KT * u + ot - 1))
                        os = slice(ot * P, (ot + 1) * P)
                        for j in range(JT):
                            mm = three(nc, mix[:, ot % 2, 0:QU], v_hi[:, j, os], v_lo[:, j, os], pt_hi[:, j, :], pt_lo[:, j, :],
                                       j == 0, j == JT - 1)
                        mm.then_inc(mix_full, 1)

                def group_stats(s, product):
                    r.wait_free(pe, act_released, dve_released, b, ("GN", s))
                    product(pe, b + (B + 1), slot[:, r.slot(("GN", s)), 0:KT]).then_inc(slot_full, 1)

                if isinstance(b, int) and b == 0:
                    pe.wait_ge(w_lo, 2 * KT)
                project_q(0)
                if isinstance(b, int) and b == 0:
                    pe.wait_ge(w_lo, 3 * KT)
                project_v(0)
                project_v(1)
                for s in range(U):
                    for a in range(TURNS):
                        if s >= 1:
                            turn_item(s - 1, a)
                        scores(s, a // 2, a % 2)
                    if s + 1 < U:
                        project_q(s + 1)
                    if s == 0:
                        project_v(2)
                        project_v(3)
                    if not last and s == MEANS_AT:
                        group_stats(s, norm.mean_matmul)
                    if not last and s == VARS_AT:
                        group_stats(s, norm.var_matmul)
                    if s >= 1:
                        mixes(s - 1)
                for a in range(TURNS):
                    turn_item(U - 1, a)
                    if not last:
                        project_k(r, b, a, b + 1)
                mixes(U - 1)

            over_batches(pe, body)

        @block.scalar
        def _(act):
            def split_hi(i):
                w, kt = chunks[i]
                act.wait_ge(w_loaded[i], 16)
                nc.scalar.activation(w[:, kt, 0, :], staged(i), ACT.Copy).then_inc(w_hi, 1)

            def k_his(r, b, m, n):
                at = m % 2 if n is b else r.slot(("K", m))
                act.wait_ge(slot_full, m + 1 if n is b else r.full(b, ("K", m)))
                nc.scalar.activation(k_hi[:, m], slot[:, at, :], ACT.Identity,
                                     bias=vecs[:, V_BK, m:m + 1]).then_inc(act_released, 1)

            for i in range(2 * KT):
                split_hi(i)
            for m in range(KT):
                split_hi(2 * KT + m)
                k_his(ring, 0, m, 0)

            def body(b, last):
                r = ring_last if last else ring

                def v_his(i):
                    act.wait_ge(slot_full, r.full(b, ("V", i)))
                    nc.scalar.activation(v_hi[:, 2 * i:2 * i + 2].rearrange("p j c -> p (j c)"),
                                         slot[:, r.slot(("V", i)), :], ACT.Copy).then_inc(act_released, 1)

                def q_his(u):
                    act.wait_ge(slot_full, r.full(b, ("Q", u)))
                    for m in range(KT):
                        done = nc.scalar.activation(q_hi[:, m], slot[:, r.slot(("Q", u)), m * QU:(m + 1) * QU],
                                                    ACT.Identity, bias=vecs[:, V_BQ, m:m + 1])
                    done.then_inc(act_released, 1)

                def exponentials(u, t):
                    k = (TILES * u + t) % PROBS
                    act.wait_ge(max_ready, b * (TILES * U) + (TILES * u + t + 1))
                    wait(act, turn_full, b * (TURNS * U) + TURNS * (u - 1))
                    nc.scalar.activation(probs[:, k, :], slot[:, r.slot(("S", u, t)), :], ACT.Exp, scale=SCALE,
                                         bias=neg_max[:, k:k + 1], accum_out=total[:, k:k + 1]).then_inc(act_released, 1)

                def turn_his(u, a):
                    act.wait_ge(turn_full, b * (TURNS * U) + (TURNS * u + a + 1))
                    if a == 0:
                        wait(act, mix_full, b * (KT * U) + KT * u)
                    nc.scalar.activation(pt_hi[:, 2 * a:2 * a + 2, :], turn[:, a % 2], ACT.Copy).then_inc(turn_hi, 1)

                def next_norm(ct):
                    act.wait_ge(x_loaded[ct % 2], x_count(b, KT + ct))
                    norm.tile_hi(act, b + (B + 1), ct, x_in[:, ct % 2], n_hi[:, ct])

                q_his(0)
                v_his(0)
                v_his(1)
                for s in range(U):
                    if s >= 1:
                        turn_his(s - 1, 0)
                        turn_his(s - 1, 1)
                    if s >= 1:
                        turn_his(s - 1, 2)
                    exponentials(s, 0)
                    if s >= 1:
                        turn_his(s - 1, 3)
                    if not last and s == U - 1:
                        next_norm(2)
                        next_norm(3)
                    exponentials(s, 1)
                    if s + 1 < U:
                        q_his(s + 1)
                    if s == 0:
                        v_his(2)
                        v_his(3)
                    if not last and s == U - 2:
                        next_norm(0)
                        next_norm(1)
                for a in range(TURNS):
                    turn_his(U - 1, a)
                    if not last:
                        k_his(r, b, a, b + 1)

            over_batches(act, body)

        @block.vector
        def _(dve):
            def split_lo(i):
                w, kt = chunks[i]
                dve.wait_ge(w_hi, i + 1)
                nc.vector.tensor_tensor(w[:, kt, 1, :], staged(i), f(w[:, kt, 0, :]), ALU.subtract).then_inc(w_lo, 1)

            def k_los(r, b, m, n):
                at = m % 2 if n is b else r.slot(("K", m))
                dve.wait_ge(act_released, m + 1 if n is b else r.act_done(b, ("K", m)))
                nc.vector.scalar_tensor_tensor(k_lo[:, m], slot[:, at, :], vecs[:, V_BK, m:m + 1],
                                               f(k_hi[:, m]), ALU.add, ALU.subtract).then_inc(dve_released, 1)

            for i in range(2 * KT):
                split_lo(i)
            for m in range(KT):
                split_lo(2 * KT + m)
                k_los(ring, 0, m, 0)

            def body(b, last):
                r = ring_last if last else ring

                def v_los(i):
                    dve.wait_ge(act_released, r.act_done(b, ("V", i)))
                    nc.vector.tensor_tensor(v_lo[:, 2 * i:2 * i + 2].rearrange("p j c -> p (j c)"),
                                            slot[:, r.slot(("V", i)), :],
                                            f(v_hi[:, 2 * i:2 * i + 2].rearrange("p j c -> p (j c)")),
                                            ALU.subtract).then_inc(dve_released, 1)

                def q_los(u):
                    dve.wait_ge(act_released, r.act_done(b, ("Q", u)))
                    for m in range(KT):
                        done = nc.vector.scalar_tensor_tensor(
                            q_lo[:, m], slot[:, r.slot(("Q", u)), m * QU:(m + 1) * QU], vecs[:, V_BQ, m:m + 1],
                            f(q_hi[:, m]), ALU.add, ALU.subtract)
                    done.then_inc(dve_released, 1)

                def maxima(u, t):
                    k = (TILES * u + t) % PROBS
                    n = b * (TILES * U) + (TILES * u + t + 1)
                    dve.wait_ge(slot_full, r.full(b, ("S", u, t)))
                    nc.vector.tensor_reduce(neg_raw[:, k:k + 1], slot[:, r.slot(("S", u, t)), :], AX_X, ALU.max,
                                            negate=True).then_inc(raw_ready, 1)
                    dve.wait_ge(raw_ready, n)
                    nc.vector.tensor_scalar(neg_max[:, k:k + 1], neg_raw[:, k:k + 1], SCALE, None, ALU.mult
                                            ).then_inc(max_ready, 1)

                def inverses(u, t):
                    k = (TILES * u + t) % PROBS
                    dve.wait_ge(act_released, r.act_done(b, ("S", u, t)))
                    nc.vector.reciprocal(inverse[:, k:k + 1], total[:, k:k + 1]).then_inc(inverse_ready, 1)

                def turn_los(u, a):
                    dve.wait_ge(turn_hi, b * (TURNS * U) + (TURNS * u + a + 1))
                    nc.vector.tensor_tensor(pt_lo[:, 2 * a:2 * a + 2, :], turn[:, a % 2],
                                            f(pt_hi[:, 2 * a:2 * a + 2, :]), ALU.subtract).then_inc(turn_lo, 1)

                def finish(u):
                    dve.wait_ge(y_loaded[u % 2], b * 32 + 16 * (u // 2 + 1))
                    for ot in range(KT):
                        dve.wait_ge(mix_full, b * (KT * U) + (KT * u + ot + 1))
                        part = y[:, u % 2, ot]
                        nc.vector.scalar_tensor_tensor(part, mix[:, ot % 2, 0:QU], b2[:, ot:ot + 1], part, ALU.add, ALU.add
                                                       ).then_inc(mix_added, 1)

                def next_stats(i):
                    dve.wait_ge(x_loaded[i % 2], x_count(b, i))
                    norm.tile_stats(dve, b + (B + 1), i, x_in[:, i % 2])

                q_los(0)
                v_los(0)
                v_los(1)
                if not last:
                    next_stats(0)
                    next_stats(1)
                for s in range(U):
                    if s >= 1:
                        turn_los(s - 1, 0)
                        turn_los(s - 1, 1)
                    maxima(s, 0)
                    if s >= 1:
                        turn_los(s - 1, 2)
                    inverses(s, 0)
                    if s >= 1:
                        turn_los(s - 1, 3)
                    if not last and s == U - 1:
                        for ct in (2, 3):
                            norm.tile_mid(dve, b + (B + 1), ct, x_in[:, ct % 2])
                    maxima(s, 1)
                    inverses(s, 1)
                    if s + 1 < U:
                        q_los(s + 1)
                    if s == 0:
                        v_los(2)
                        v_los(3)
                        if not last:
                            next_stats(2)
                            next_stats(3)
                    if not last and s == MEANS_AT:
                        dve.wait_ge(slot_full, r.full(b, ("GN", s)))
                        norm.after_means(dve, b + (B + 1), slot[:, r.slot(("GN", s)), 0:KT], dve_released,
                                         r.dve_done(b, ("GN", s)))
                    if not last and s == VARS_AT:
                        dve.wait_ge(slot_full, r.full(b, ("GN", s)))
                        norm.after_vars(1, slot[:, r.slot(("GN", s)), 0:KT], dve_released)
                        norm.coefficients(dve, b + (B + 1), 1)
                    if s >= 1:
                        finish(s - 1)
                    if not last and s == U - 2:
                        for ct in (0, 1):
                            norm.tile_mid(dve, b + (B + 1), ct, x_in[:, ct % 2])
                for a in range(TURNS):
                    turn_los(U - 1, a)
                    if not last:
                        k_los(r, b, a, b + 1)
                finish(U - 1)

            over_batches(dve, body)

        @block.gpsimd
        def _(pool):
            def body(b, last):
                r = ring_last if last else ring
                def normalise(s, t):
                    k = (TILES * s + t) % PROBS
                    wait_apart(pool, inverse_ready, b * (TILES * U) + (TILES * s + t + 1), scale_passed)
                    nc.gpsimd.tensor_scalar(probs[:, k, :], probs[:, k, :], inverse[:, k:k + 1], 1.0,
                                            ALU.mult, ALU.mult).then_inc(probs_ready, 1)

                def next_norm(ct):
                    norm.tile_lo(pool, b + (B + 1), ct, x_in[:, ct % 2], n_hi[:, ct], n_lo[:, ct])

                for s in range(U):
                    normalise(s, 0)
                    if not last and s == U - 1:
                        next_norm(2)
                        next_norm(3)
                    normalise(s, 1)
                    if not last and s == VARS_AT:
                        norm.power(pool, dve_released, r.dve_done(b, ("GN", s)))
                    if not last and s == U - 2:
                        next_norm(0)
                        next_norm(1)

            over_batches(pool, body)


def two_attentions(nc, x, w_in, v_in, t_in, out):
    x1 = nc.dram_tensor("x1", (B, C, N), F32, kind="Internal").ap()
    scratch = nc.dram_tensor("w_split_dram", (P, CHUNKS, 2, HALF), F32, kind="Internal").ap()
    w_m_dram = nc.dram_tensor("w_m_dram", (P, KT, C), F32, kind="Internal").ap()
    with ExitStack() as ctx:
        def sb(name, shape, dt=F32):
            return ctx.enter_context(nc.sbuf_tensor(name, shape, dt))

        def sem(name):
            return ctx.enter_context(nc.semaphore(name))

        vecs = sb("vecs", [P, 9, KT])
        tables = sb("tables", [P, 2 * P + KT])
        b2 = sb("b2", [P, KT])
        n_hi = sb("n_hi", [P, KT, N], F32R)
        n_lo = sb("n_lo", [P, KT, N], F32R)
        ident = tables[:, 0:P]
        norm = Norm(nc, sb, sem, ((vecs[:, V_GNW, :], vecs[:, V_GNB, :], EPS0), (vecs[:, V_GS, :], vecs[:, V_GB, :], EPS1)),
                    tables[:, P:2 * P], tables[:, 2 * P:2 * P + KT])
        split_weights(nc, x, w_in, v_in, t_in, scratch, w_m_dram, vecs, tables, b2, norm, n_hi, n_lo)
        attend_heads(nc, x, x1, scratch, vecs, ident, norm, n_hi, n_lo)
        attend_single(nc, x1, out, w_in, w_m_dram, vecs, b2, ident, norm, n_hi, n_lo)


def kernel(**inputs):
    import numpy as np
    import concourse.bacc as bacc
    from concourse.bass_utils import run_bass_kernel_spmd as run

    def host(name):
        return np.asarray(inputs[name])

    def contraction_first(wt):
        return wt.reshape(KT, P, -1).transpose(1, 0, 2)

    qkv = host("L0_conv_qkv_w").reshape(HEADS, 3, HD, C)
    w_qk = qkv[:, 0:2].reshape(HEADS, P, KT, P).transpose(3, 0, 2, 1).reshape(P, HEADS, HALF)
    w_v = contraction_first(qkv[:, 2].reshape(C, C).T)
    w_o = host("L0_conv_out_w").reshape(KT, P, KT, P).transpose(3, 0, 2, 1).reshape(P, KT, HALF)
    w_in = np.ascontiguousarray(np.concatenate([
        w_qk, w_v, w_o, contraction_first(host("L1_conv_wq").T), contraction_first(host("L1_conv_wk").T),
        contraction_first(host("L1_conv_wp").T), contraction_first(host("L1_conv_wv"))], axis=1))
    v_in = np.ascontiguousarray(np.stack([host(n).reshape(KT, P).T for n in (
        "L0_conv_gn_w", "L0_conv_gn_b", "L0_conv_out_b", "L1_conv_gn_scale", "L1_conv_gn_bias",
        "L1_conv_bq", "L1_conv_bk", "L1_conv_bv", "L1_conv_bp")], axis=1))
    size = C // GROUPS
    averager = np.kron(np.eye(P // size), np.full((size, size), 1.0 / size))
    t_in = np.concatenate([np.eye(P), averager, np.full((P, KT), -0.5)], axis=1).astype(np.float32)
    x = host("x").reshape(B, C, N)

    nc = bacc.Bacc("TRN2", target_bir_lowering=False, num_devices=1)
    arrays, args = {}, []
    for name, a in (("x", x), ("w_in", w_in), ("v_in", v_in), ("t_in", t_in)):
        arrays[name] = np.ascontiguousarray(a)
        args.append(nc.dram_tensor(name, a.shape, mybir.dt.from_np(a.dtype), kind="ExternalInput").ap())
    out = nc.dram_tensor("out", (B, C, N), F32, kind="ExternalOutput").ap()
    two_attentions(nc, *args, out)
    r = run(nc, [arrays], core_ids=[0])
    return r.results[0]["out"].reshape(B, C, 32, 32)
```
